# Optimizing a Trainium2 kernel written in Bass

```python
import numpy as np
import jax
import jax.numpy as jnp

def _softmax(x, axis=-1):
    return jax.nn.softmax(x, axis=axis)

def _gelu(x):
    return jax.nn.gelu(x, approximate=True)

def _silu(x):
    return jax.nn.silu(x)

def _sigmoid(x):
    return jax.nn.sigmoid(x)

def _layernorm(x, axis=-1, eps=1e-05):
    m = jnp.mean(x, axis=axis, keepdims=True)
    v = jnp.var(x, axis=axis, keepdims=True)
    return (x - m) / jnp.sqrt(v + eps)

def _scatter_add(tgt, idx, src, axis=0):
    return tgt.at[idx].add(src)

def _segment_sum(src, seg, n):
    return jax.ops.segment_sum(src, seg, n)
kernel_name = 'mk_audio_tower_d2_tok_aud1d512_r4_7bc3e2'

def setup_inputs(seed: int=0):
    np.random.seed(seed)
    _w = jnp.asarray

    def _rec_inputs():
        import jax
        import jax.numpy as jnp
        _rk = jax.random.key(seed)
        x = -0.00238186 + 1.00146 * jax.random.normal(jax.random.fold_in(_rk, 1), (64, 5000), jnp.float32)
        return x
    x = _rec_inputs()

    def _L0_tok_setup():
        import jax, jax.numpy as jnp
        import numpy as np
        B, E, G, P = (8, 16, 5000, 128)
        MASK_DENSITY = 0.1
        key = jax.random.key(seed)
        k_x, k_w, k_m = jax.random.split(key, 3)
        x = jax.random.normal(k_x, (B, G), dtype=jnp.float32)
        weight = jax.random.normal(k_w, (E, G, P), dtype=jnp.float32) * 0.01
        bias = jnp.zeros((E, P), dtype=jnp.float32)
        mask = (jax.random.uniform(k_m, (G, P)) < MASK_DENSITY).astype(jnp.float32)
        return {'x': x, 'weight': weight, 'bias': bias, 'mask': mask}
    _L0_tok_all = _L0_tok_setup()
    _L0_tok_in = {k: v for k, v in _L0_tok_all.items() if k in ('weight', 'bias', 'mask')}
    del _L0_tok_all

    def _L0_attn_setup():
        import jax, jax.numpy as jnp
        import numpy as np
        S, B, D = (256, 8, 128)
        N_HEAD, D_HEAD = (8, 64)
        LN_EPS = 1e-05

        def _sqdist(q, k):
            q2 = jnp.sum(q * q, axis=-1)[..., :, None]
            k2 = jnp.sum(k * k, axis=-1)[..., None, :]
            qk = jnp.einsum('nbid,nbjd->nbij', q, k)
            return jnp.maximum(q2 + k2 - 2.0 * qk, 0.0)
        key = jax.random.key(seed)
        ks = jax.random.split(key, 7)
        h = jax.random.normal(ks[0], (S, B, D), dtype=jnp.float32)
        std = D ** (-0.5)
        Wq = jax.random.normal(ks[1], (D, N_HEAD * D_HEAD), dtype=jnp.float32) * std
        Wkv = jax.random.normal(ks[2], (D, 2 * N_HEAD * D_HEAD), dtype=jnp.float32) * std
        Wo = jax.random.normal(ks[3], (N_HEAD * D_HEAD, D), dtype=jnp.float32) * std
        mu = jax.random.normal(ks[4], (2, N_HEAD, D_HEAD), dtype=jnp.float32) * 0.5
        mu = mu * jnp.array([0.0, 1.0], dtype=jnp.float32)[:, None, None]
        gamma = jnp.ones((D,), dtype=jnp.float32)
        beta = jnp.zeros((D,), dtype=jnp.float32)
        return {'h': h, 'Wq': Wq, 'Wkv': Wkv, 'Wo': Wo, 'mu': mu, 'gamma': gamma, 'beta': beta}
    _L0_attn_all = _L0_attn_setup()
    _L0_attn_in = {k: v for k, v in _L0_attn_all.items() if k in ('Wq', 'Wkv', 'Wo', 'mu', 'gamma', 'beta')}
    del _L0_attn_all

    def _L0_ffn_setup():
        import jax, jax.numpy as jnp
        import numpy as np
        B, S, H = (4, 1024, 128)
        E, K = (64, 8)
        IE, IS = (128, 352)
        key = jax.random.key(seed)
        ks = jax.random.split(key, 8)
        scale = 0.02
        return {'x': jax.random.normal(ks[0], (B, S, H), jnp.float32), 'gate_w': jax.random.normal(ks[1], (E, H), jnp.float32) * scale, 'w1': jax.random.normal(ks[2], (E, H, IE), jnp.float32) * scale, 'w3': jax.random.normal(ks[3], (E, H, IE), jnp.float32) * scale, 'w2': jax.random.normal(ks[4], (E, IE, H), jnp.float32) * scale, 'sw1': jax.random.normal(ks[5], (H, IS), jnp.float32) * scale, 'sw3': jax.random.normal(ks[6], (H, IS), jnp.float32) * scale, 'sw2': jax.random.normal(ks[7], (IS, H), jnp.float32) * scale}
    _L0_ffn_all = _L0_ffn_setup()
    _L0_ffn_in = {k: v for k, v in _L0_ffn_all.items() if k in ('gate_w', 'w1', 'w3', 'w2', 'sw1', 'sw3', 'sw2')}
    del _L0_ffn_all

    def _L1_attn_setup():
        import jax, jax.numpy as jnp
        import numpy as np
        B, T, D_MODEL, N_HEADS, D_FF = (2, 512, 128, 8, 512)
        D_HEAD = D_MODEL // N_HEADS
        EPS_LN = 1e-05
        DEN_MIN = 1e-06

        def layer_norm(x, g, b):
            mu = jnp.mean(x, axis=-1, keepdims=True)
            var = jnp.var(x, axis=-1, keepdims=True)
            return (x - mu) * jax.lax.rsqrt(var + EPS_LN) * g + b

        def causal_linear_attention(Q, K, V):
            KV = jnp.cumsum(K[..., :, None] * V[..., None, :], axis=2)
            z = jnp.cumsum(K, axis=2)
            num = jnp.einsum('bhtd,bhtdm->bhtm', Q, KV)
            den = jnp.maximum(jnp.einsum('bhtd,bhtd->bht', Q, z), DEN_MIN)[..., None]
            return num / den
        key = jax.random.key(seed)
        ks = jax.random.split(key, 12)

        def lin_w(k, din, dout):
            return jax.random.normal(k, (din, dout), jnp.float32) / np.sqrt(din).astype(np.float32)
        return {'x': jax.random.normal(ks[0], (B, T, D_MODEL), jnp.float32), 'ln1_g': jnp.ones((D_MODEL,), jnp.float32), 'ln1_b': jnp.zeros((D_MODEL,), jnp.float32), 'Wq': lin_w(ks[1], D_MODEL, D_MODEL), 'bq': jnp.zeros((D_MODEL,), jnp.float32), 'Wk': lin_w(ks[2], D_MODEL, D_MODEL), 'bk': jnp.zeros((D_MODEL,), jnp.float32), 'Wv': lin_w(ks[3], D_MODEL, D_MODEL), 'bv': jnp.zeros((D_MODEL,), jnp.float32), 'Wo': lin_w(ks[4], D_MODEL, D_MODEL), 'bo': jnp.zeros((D_MODEL,), jnp.float32), 'ln2_g': jnp.ones((D_MODEL,), jnp.float32), 'ln2_b': jnp.zeros((D_MODEL,), jnp.float32), 'W1': lin_w(ks[5], D_MODEL, D_FF), 'b1': jnp.zeros((D_FF,), jnp.float32), 'W2': lin_w(ks[6], D_FF, D_MODEL), 'b2': jnp.zeros((D_MODEL,), jnp.float32)}
    _L1_attn_all = _L1_attn_setup()
    _L1_attn_in = {k: v for k, v in _L1_attn_all.items() if k in ('ln1_g', 'ln1_b', 'Wq', 'bq', 'Wk', 'bk', 'Wv', 'bv', 'Wo', 'bo', 'ln2_g', 'ln2_b', 'W1', 'b1', 'W2', 'b2')}
    del _L1_attn_all

    def _L1_ffn_setup():
        import jax, jax.numpy as jnp
        import numpy as np
        E = 8
        K = 1
        D = 128
        I = 512
        B, T = (2, 512)
        key = jax.random.key(seed)
        ks = jax.random.split(key, 7)
        s = 0.02
        x = jax.random.normal(ks[0], (B, T, D), jnp.float32)
        gate_w = jax.random.normal(ks[1], (E, D), jnp.float32) * s
        w1 = jax.random.normal(ks[2], (E, I, D), jnp.float32) * s
        w2 = jax.random.normal(ks[3], (E, D, I), jnp.float32) * s
        w3 = jax.random.normal(ks[4], (E, I, D), jnp.float32) * s
        sw1 = jax.random.normal(ks[5], (I, D), jnp.float32) * s
        sw2 = jax.random.normal(ks[6], (D, I), jnp.float32) * s
        return {'x': x, 'gate_w': gate_w, 'w1': w1, 'w2': w2, 'w3': w3, 'sw1': sw1, 'sw2': sw2}
    _L1_ffn_all = _L1_ffn_setup()
    _L1_ffn_in = {k: v for k, v in _L1_ffn_all.items() if k in ('gate_w', 'w1', 'w2', 'w3', 'sw1', 'sw2')}
    del _L1_ffn_all
    return {'x': x, 'L0_tok_weight': _L0_tok_in['weight'], 'L0_tok_bias': _L0_tok_in['bias'], 'L0_tok_mask': _L0_tok_in['mask'], 'L0_attn_Wq': _L0_attn_in['Wq'], 'L0_attn_Wkv': _L0_attn_in['Wkv'], 'L0_attn_Wo': _L0_attn_in['Wo'], 'L0_attn_mu': _L0_attn_in['mu'], 'L0_attn_gamma': _L0_attn_in['gamma'], 'L0_attn_beta': _L0_attn_in['beta'], 'L0_ffn_gate_w': _L0_ffn_in['gate_w'], 'L0_ffn_w1': _L0_ffn_in['w1'], 'L0_ffn_w3': _L0_ffn_in['w3'], 'L0_ffn_w2': _L0_ffn_in['w2'], 'L0_ffn_sw1': _L0_ffn_in['sw1'], 'L0_ffn_sw3': _L0_ffn_in['sw3'], 'L0_ffn_sw2': _L0_ffn_in['sw2'], 'L1_attn_ln1_g': _L1_attn_in['ln1_g'], 'L1_attn_ln1_b': _L1_attn_in['ln1_b'], 'L1_attn_Wq': _L1_attn_in['Wq'], 'L1_attn_bq': _L1_attn_in['bq'], 'L1_attn_Wk': _L1_attn_in['Wk'], 'L1_attn_bk': _L1_attn_in['bk'], 'L1_attn_Wv': _L1_attn_in['Wv'], 'L1_attn_bv': _L1_attn_in['bv'], 'L1_attn_Wo': _L1_attn_in['Wo'], 'L1_attn_bo': _L1_attn_in['bo'], 'L1_attn_ln2_g': _L1_attn_in['ln2_g'], 'L1_attn_ln2_b': _L1_attn_in['ln2_b'], 'L1_attn_W1': _L1_attn_in['W1'], 'L1_attn_b1': _L1_attn_in['b1'], 'L1_attn_W2': _L1_attn_in['W2'], 'L1_attn_b2': _L1_attn_in['b2'], 'L1_ffn_gate_w': _L1_ffn_in['gate_w'], 'L1_ffn_w1': _L1_ffn_in['w1'], 'L1_ffn_w2': _L1_ffn_in['w2'], 'L1_ffn_w3': _L1_ffn_in['w3'], 'L1_ffn_sw1': _L1_ffn_in['sw1'], 'L1_ffn_sw2': _L1_ffn_in['sw2']}

def reference(x, L0_tok_weight, L0_tok_bias, L0_tok_mask, L0_attn_Wq, L0_attn_Wkv, L0_attn_Wo, L0_attn_mu, L0_attn_gamma, L0_attn_beta, L0_ffn_gate_w, L0_ffn_w1, L0_ffn_w3, L0_ffn_w2, L0_ffn_sw1, L0_ffn_sw3, L0_ffn_sw2, L1_attn_ln1_g, L1_attn_ln1_b, L1_attn_Wq, L1_attn_bq, L1_attn_Wk, L1_attn_bk, L1_attn_Wv, L1_attn_bv, L1_attn_Wo, L1_attn_bo, L1_attn_ln2_g, L1_attn_ln2_b, L1_attn_W1, L1_attn_b1, L1_attn_W2, L1_attn_b2, L1_ffn_gate_w, L1_ffn_w1, L1_ffn_w2, L1_ffn_w3, L1_ffn_sw1, L1_ffn_sw2):
    import jax
    import jax.numpy as jnp

    def _L0_tok_ref(x, weight, bias, mask):
        import jax, jax.numpy as jnp
        import numpy as np
        B, E, G, P = (8, 16, 5000, 128)
        MASK_DENSITY = 0.1
        W = weight * mask[None, :, :]
        out = jnp.einsum('bg,egp->bep', x, W)
        return out + bias[None, :, :]

    def _L0_attn_ref(h, Wq, Wkv, Wo, mu, gamma, beta):
        import jax, jax.numpy as jnp
        import numpy as np
        S, B, D = (256, 8, 128)
        N_HEAD, D_HEAD = (8, 64)
        LN_EPS = 1e-05

        def _sqdist(q, k):
            q2 = jnp.sum(q * q, axis=-1)[..., :, None]
            k2 = jnp.sum(k * k, axis=-1)[..., None, :]
            qk = jnp.einsum('nbid,nbjd->nbij', q, k)
            return jnp.maximum(q2 + k2 - 2.0 * qk, 0.0)
        s, b, d = h.shape
        n, dh = (mu.shape[1], mu.shape[2])
        scale = dh ** (-0.5)
        q = (h @ Wq).reshape(s, b, n, dh)
        k, v = jnp.split(h @ Wkv, 2, axis=-1)
        k = k.reshape(s, b, n, dh)
        v = v.reshape(s, b, n, dh)
        qt = q.transpose(2, 1, 0, 3)
        k0 = (k - mu[0]).transpose(2, 1, 0, 3)
        k1 = (k - mu[1]).transpose(2, 1, 0, 3)
        d0 = -scale / 2.0 * _sqdist(qt, k0)
        d1 = -1.5 * scale * _sqdist(qt, k1)
        score = jnp.maximum(d0, d1)
        score = score.transpose(2, 3, 1, 0)
        prob = jax.nn.softmax(score, axis=1)
        vec = jnp.einsum('ijbn,jbnd->ibnd', prob, v).reshape(s, b, n * dh)
        attn_out = vec @ Wo
        x = h + attn_out
        mean = jnp.mean(x, axis=-1, keepdims=True)
        var = jnp.mean(jnp.square(x - mean), axis=-1, keepdims=True)
        return (x - mean) / jnp.sqrt(var + LN_EPS) * gamma + beta

    def _L0_ffn_ref(x, gate_w, w1, w3, w2, sw1, sw3, sw2):
        import jax, jax.numpy as jnp
        import numpy as np
        B, S, H = (4, 1024, 128)
        E, K = (64, 8)
        IE, IS = (128, 352)
        b, s, h = x.shape
        xf = x.reshape(-1, h)
        T = xf.shape[0]
        logits = xf @ gate_w.T
        topk_w, topk_idx = jax.lax.top_k(logits, K)
        topk_w = jax.nn.softmax(topk_w, axis=-1)
        expert_flat = topk_idx.reshape(-1)
        order = jnp.argsort(expert_flat)
        group_sizes = jnp.bincount(expert_flat, length=E).astype(jnp.int32)
        tok_ids = (jnp.arange(T * K) // K)[order]
        xg = xf[tok_ids]
        hid = jax.nn.silu(jax.lax.ragged_dot(xg, w1, group_sizes)) * jax.lax.ragged_dot(xg, w3, group_sizes)
        y = jax.lax.ragged_dot(hid, w2, group_sizes)
        y = y * topk_w.reshape(-1)[order][:, None]
        routed = jnp.zeros_like(xf).at[tok_ids].add(y)
        shared = jax.nn.silu(xf @ sw1) * (xf @ sw3) @ sw2
        return (routed + shared).reshape(b, s, h)

    def _L1_attn_ref(x, ln1_g, ln1_b, Wq, bq, Wk, bk, Wv, bv, Wo, bo, ln2_g, ln2_b, W1, b1, W2, b2):
        import jax, jax.numpy as jnp
        import numpy as np
        B, T, D_MODEL, N_HEADS, D_FF = (2, 512, 128, 8, 512)
        D_HEAD = D_MODEL // N_HEADS
        EPS_LN = 1e-05
        DEN_MIN = 1e-06

        def layer_norm(x, g, b):
            mu = jnp.mean(x, axis=-1, keepdims=True)
            var = jnp.var(x, axis=-1, keepdims=True)
            return (x - mu) * jax.lax.rsqrt(var + EPS_LN) * g + b

        def causal_linear_attention(Q, K, V):
            KV = jnp.cumsum(K[..., :, None] * V[..., None, :], axis=2)
            z = jnp.cumsum(K, axis=2)
            num = jnp.einsum('bhtd,bhtdm->bhtm', Q, KV)
            den = jnp.maximum(jnp.einsum('bhtd,bhtd->bht', Q, z), DEN_MIN)[..., None]
            return num / den
        Bx, Tx, _ = x.shape
        h = layer_norm(x, ln1_g, ln1_b)

        def heads(y):
            return y.reshape(Bx, Tx, N_HEADS, D_HEAD).transpose(0, 2, 1, 3)
        Q = jax.nn.elu(heads(h @ Wq + bq)) + 1.0
        K = jax.nn.elu(heads(h @ Wk + bk)) + 1.0
        V = heads(h @ Wv + bv)
        attn = causal_linear_attention(Q, K, V)
        attn = attn.transpose(0, 2, 1, 3).reshape(Bx, Tx, D_MODEL)
        x = x + (attn @ Wo + bo)
        h2 = layer_norm(x, ln2_g, ln2_b)
        ffn = jax.nn.relu(h2 @ W1 + b1) @ W2 + b2
        return x + ffn

    def _L1_ffn_ref(x, gate_w, w1, w2, w3, sw1, sw2):
        import jax, jax.numpy as jnp
        import numpy as np
        E = 8
        K = 1
        D = 128
        I = 512
        B, T = (2, 512)
        xf = x.reshape(-1, D)
        logits = xf @ gate_w.T
        wts, idx = jax.lax.top_k(logits, K)
        wts = jax.nn.softmax(wts, axis=-1)
        comb = jnp.einsum('nke,nk->ne', jax.nn.one_hot(idx, E, dtype=xf.dtype), wts)
        h = jax.nn.silu(jnp.einsum('nd,eid->nei', xf, w1)) * jnp.einsum('nd,eid->nei', xf, w3)
        y = jnp.einsum('nei,edi->nd', h * comb[:, :, None], w2)
        y = y + jax.nn.gelu(xf @ sw1.T, approximate=False) @ sw2.T
        return y.reshape(x.shape)
    h = _L0_tok_ref(x, L0_tok_weight, L0_tok_bias, L0_tok_mask)
    h = h + _L0_attn_ref(_layernorm(h, axis=-1), L0_attn_Wq, L0_attn_Wkv, L0_attn_Wo, L0_attn_mu, L0_attn_gamma, L0_attn_beta)
    h = h + _L0_ffn_ref(_layernorm(h, axis=-1), L0_ffn_gate_w, L0_ffn_w1, L0_ffn_w3, L0_ffn_w2, L0_ffn_sw1, L0_ffn_sw3, L0_ffn_sw2)
    h = h + _L1_attn_ref(_layernorm(h, axis=-1), L1_attn_ln1_g, L1_attn_ln1_b, L1_attn_Wq, L1_attn_bq, L1_attn_Wk, L1_attn_bk, L1_attn_Wv, L1_attn_bv, L1_attn_Wo, L1_attn_bo, L1_attn_ln2_g, L1_attn_ln2_b, L1_attn_W1, L1_attn_b1, L1_attn_W2, L1_attn_b2)
    h = h + _L1_ffn_ref(_layernorm(h, axis=-1), L1_ffn_gate_w, L1_ffn_w1, L1_ffn_w2, L1_ffn_w3, L1_ffn_sw1, L1_ffn_sw2)
    return h

_drawn_inputs = setup_inputs


def setup_inputs(seed=0):
    import zlib

    import numpy as np

    out = dict(_drawn_inputs(seed))
    spreads = {'L0_tok_bias': (0.0, 0.1),
     'L0_attn_gamma': (1.0, 0.2),
     'L0_attn_beta': (0.0, 0.1),
     'L1_attn_ln1_g': (1.0, 0.2),
     'L1_attn_ln1_b': (0.0, 0.1),
     'L1_attn_bq': (0.0, 0.8),
     'L1_attn_bk': (0.0, 0.8),
     'L1_attn_bv': (0.0, 0.1),
     'L1_attn_bo': (0.0, 0.1),
     'L1_attn_ln2_g': (1.0, 0.2),
     'L1_attn_ln2_b': (0.0, 0.1),
     'L1_attn_b1': (0.0, 0.1),
     'L1_attn_b2': (0.0, 0.1)}
    factors = {'L0_ffn_gate_w': 8.0,
     'L0_ffn_w1': 8.0,
     'L0_ffn_w3': 8.0,
     'L0_ffn_w2': 8.0,
     'L0_ffn_sw1': 7.256,
     'L0_ffn_sw3': 7.244,
     'L0_ffn_sw2': 7.229,
     'L1_attn_Wq': 2.672,
     'L1_ffn_gate_w': 8.0,
     'L1_ffn_w1': 8.0,
     'L1_ffn_w2': 8.0,
     'L1_ffn_w3': 8.0,
     'L1_ffn_sw1': 8.0,
     'L1_ffn_sw2': 8.0}
    for name, (base, spread) in spreads.items():
        noise = np.random.default_rng([zlib.crc32(name.encode()), seed]).standard_normal(out[name].shape)
        drawn = base * np.exp(spread * noise) if base else spread * noise
        out[name] = jnp.asarray(drawn.astype(out[name].dtype))
    for name, factor in factors.items():
        out[name] = (out[name] * factor).astype(out[name].dtype)
    return out
```

```python
from contextlib import ExitStack

import concourse.bass as bass
from concourse import mybir

F32 = mybir.dt.float32
F32R = mybir.dt.float32r
U32 = mybir.dt.uint32
ALU = mybir.AluOpType
ACT = mybir.ActivationFunctionType
AX = mybir.AxisListType

P = 128
S, B, D = 64, 16, 128
NT = S * B // P
ROWS = S * B
G = 5000
GT = G // P
GR = G - GT * P
NHEAD, DH = 8, 64
NC = NHEAD * DH // P
SCALE = DH ** -0.5
E0, K0 = 64, 8
IS_CHUNKS = 3
H1, DH1 = 8, 16
FF = 512
E1, I1 = 8, 512
C1 = I1 // P
EPS = 1e-5
DEN_MIN = 1e-6
TOKW = B * D + S + D
RING = 6
FEW = P * 3


def audio_tower(nc, a, out):
    ctx = ExitStack()
    with ctx:
        def sb(name, shape, dt=F32):
            return ctx.enter_context(nc.sbuf_tensor(name, shape, dt))

        def sem(name):
            return ctx.enter_context(nc.semaphore(name))

        bank = [ctx.enter_context(nc.psum_tensor(f"bank{i}", [P, 512], F32)) for i in range(8)]
        comb_rows0 = nc.dram_tensor("comb_rows0", [E0, ROWS], F32).ap()
        comb_rows1 = nc.dram_tensor("comb_rows1", [E1 * C1, ROWS], F32).ap()

        ident = sb("ident", [P, P])
        headones = sb("headones", [P, P])
        causal = sb("causal", [P, P])
        headmask = sb("headmask", [P, H1])
        iota8 = sb("iota8", [P, E1])
        onesrow = sb("onesrow", [1, 512])
        wq = sb("wq", [P, NHEAD * DH])
        wkv = sb("wkv", [P, 2 * NHEAD * DH])
        wo = sb("wo", [P, NC, D])
        mu = sb("mu", [P, 2, NC])
        gate0 = sb("gate0", [P, E0])
        gate1 = sb("gate1", [P, E1])
        rowvec = sb("rowvec", [P, 6, D])
        w1q = sb("w1q", [P, D])
        w1k = sb("w1k", [P, D])
        w1v = sb("w1v", [P, D])
        w1o = sb("w1o", [P, D])
        b1q = sb("b1q", [P, 1])
        b1k = sb("b1k", [P, 1])
        bvob2 = sb("bvob2", [1, 3, D])
        wf1 = sb("wf1", [P, FF])
        bf1 = sb("bf1", [P, FF // P])
        wf2 = sb("wf2", [P, FF // P, D])
        ring = sb("ring", [P, RING, TOKW])
        tail = ring[0:GR, GT % RING, :]
        H = sb("H", [P, NT, D])
        Y = sb("Y", [P, NT, D])
        XN = sb("XN", [P, NT, D])
        stats = sb("stats", [P, NT, 6])
        mv = sb("mv", [P, NT, 2])
        var_eps = sb("var_eps", [P, NT])
        neg_half = sb("neg_half", [P, NT])
        rstd = sb("rstd", [P, NT])
        over = ring[:].rearrange("p j n -> p (j n)")
        FT = over[:, 0:4 * ROWS].rearrange("p (f r) -> p f r", r=ROWS)
        eq = over[:, 4 * ROWS:6 * ROWS].rearrange("p (j r) -> p j r", r=ROWS)
        rq = over[:, 6 * ROWS:8 * ROWS].rearrange("p (j r) -> p j r", r=ROWS)
        QT = over[:, 8 * ROWS:9 * ROWS]
        KT = over[:, 9 * ROWS:10 * ROWS]
        HT = over[:, 10 * ROWS:11 * ROWS]
        HN = over[:, 11 * ROWS:12 * ROWS].rearrange("p (t d) -> p t d", d=D)
        X1 = over[:, 12 * ROWS:13 * ROWS].rearrange("p (t d) -> p t d", d=D)
        xs = [sb(f"xs{u}", [P, D]) for u in range(2)]
        hT = [sb(f"hT{u}", [P, P]) for u in range(2)]
        qc = [sb(f"qc{u}", [P, 2, NC, P]) for u in range(2)]
        qsq = [sb(f"qsq{u}", [P, 2, NC, P]) for u in range(2)]
        km2 = [sb(f"km2{u}", [P, NC, P]) for u in range(2)]
        ksq = [sb(f"ksq{u}", [P, NC, P]) for u in range(2)]
        vt = [sb(f"vt{u}", [P, NHEAD * DH]) for u in range(2)]
        z1 = [sb(f"z1{u}", [P, NHEAD, S]) for u in range(2)]
        sc = [sb(f"sc{u}", [P, NHEAD, S]) for u in range(2)]
        pT = [sb(f"pT{u}", [P, NC, P]) for u in range(2)]
        vecT = [sb(f"vecT{u}", [P, NC, 2, S]) for u in range(2)]
        rmin = [sb(f"rmin{u}", [P, NHEAD]) for u in range(2)]
        rsum = [sb(f"rsum{u}", [P, NHEAD]) for u in range(2)]
        XT = sb("XT", [P, ROWS])
        XTh = sb("XTh", [P, ROWS], F32R)
        XTl = sb("XTl", [P, ROWS], F32R)
        few = [sb(f"few{u}", [P, FEW]) for u in range(2)]
        fewh13 = [sb(f"fewh13{u}", [P, 2 * P], F32R) for u in range(2)]
        fewl13 = [sb(f"fewl13{u}", [P, 2 * P], F32R) for u in range(2)]
        fewh2 = [sb(f"fewh2{u}", [P, P], F32R) for u in range(2)]
        fewl2 = [sb(f"fewl2{u}", [P, P], F32R) for u in range(2)]
        comb_b = [sb(f"comb_b{u}", [P, ROWS]) for u in range(2)]
        act_s = [sb(f"act_s{u}", [P, 512]) for u in range(2)]
        act_g = [sb(f"act_g{u}", [P, 512]) for u in range(2)]
        hid = [sb(f"hid{u}", [P, 512]) for u in range(2)]
        hidh = [sb(f"hidh{u}", [P, 512], F32R) for u in range(4)]
        hidl = [sb(f"hidl{u}", [P, 512], F32R) for u in range(4)]
        lg = sb("lg", [P, NT, E0])
        lgr = sb("lgr", [P, NT, E0])
        comb = sb("comb", [P, NT, E0])
        combT = sb("combT", [E0, ROWS])
        mx = sb("mx", [P, NT, 8])
        mxi = sb("mxi", [P, NT, 8], U32)
        rs8 = sb("rs8", [P, NT])
        HN2 = HN
        VA = sb("VA", [P, NT, H1, DH1 + 1])
        qbd = [qc[u][:].rearrange("p a c r -> p (a c) r") for u in range(2)]
        am = [qsq[u][:].rearrange("p a c r -> p (a c) r") for u in range(2)]
        den = sb("den", [P, NT, H1])
        rden = sb("rden", [P, NT, H1])
        AO = XN
        onescol = sb("onescol", [P, S])


        consts = [
            (ident[:], a["ident"]), (headones[:], a["headones"]), (causal[:], a["causal"]),
            (headmask[:], a["headmask"]), (iota8[:], a["iota8"]), (onesrow[:], a["onesrow"]),
            (wq[:], a["L0_attn_Wq"]), (wkv[:], a["L0_attn_Wkv"]),
            (wo[:], a["L0_attn_Wo"].rearrange("(c p) d -> p c d", p=P)),
            (mu[:].rearrange("p c k -> p (c k)"), a["mu_cols"]),
            (qc[0][0:1, :, :, :].rearrange("p a c r -> p (a c r)"), a["tok_bias_row"][:, 0:1024]),
            (qc[1][0:1, :, :, :].rearrange("p a c r -> p (a c r)"), a["tok_bias_row"][:, 1024:2048]),
            (gate0[:], a["gate0T"]), (gate1[:], a["gate1T"]),
            (w1q[:], a["L1_attn_Wq"]), (w1k[:], a["L1_attn_Wk"]), (w1v[:], a["L1_attn_Wv"]),
            (w1o[:], a["L1_attn_Wo"]), (b1q[:], a["L1_attn_bq"]), (b1k[:], a["L1_attn_bk"]),
            (bvob2[:, 0, :], a["L1_attn_bv"]), (bvob2[:, 1, :], a["L1_attn_bo"]),
            (bvob2[:, 2, :], a["L1_attn_b2"]),
            (wf1[:], a["L1_attn_W1"]), (bf1[:], a["b1_cols"]),
            (wf2[:], a["L1_attn_W2"].rearrange("(c p) d -> p c d", p=P)),
        ] + [(rowvec[:, n, :], a[name].partition_broadcast(P)) for n, name in enumerate(
            ["L0_attn_gamma", "L0_attn_beta", "L1_attn_ln1_g", "L1_attn_ln1_b", "L1_attn_ln2_g", "L1_attn_ln2_b"])]
        N_CONSTS = 16 * len(consts)

        names = """const_loaded tail_loaded tok_masked tok_used tok_done h0_ready fill_done
            var_ready rstd_ready dve_step
            xs_ready xT_done hT_ready q_done q_read k_done k_read v_done v_read qsq_ready x_done
            z1_read m_done e_ready p_exp p_ready pT_done pT_ready pv_done vec0_ready vec1_ready wo_done y_ready
            norm_ready tr_done tr_copied xth_ready xtl_ready logits_done logits_copied
            lmax_sub lexp comb_ready combT_done combT_copied comb_stored ht_done ht_copied
            few_loaded0 few_loaded1 row_loaded0 row_loaded1 w13h_ready w13l_ready w2h_ready w2l_ready
            h1_done h_done act_ready gated_ready hid_ready hidh_ready hidl_ready y_done g_ready
            qk1_done erq_ready qk_ready v1_done va_ready qbd_ready at_done am_ready
            num_done ao_ready wo1_done x2_ready ff1_done ft_ready ff2_done
            out_ready out_stored""".split()
        s = {n: sem(n) for n in names}
        tok_loaded = [sem(f"tok_loaded{j}") for j in range(RING)]

        W1 = IS_CHUNKS + E0
        WS = W1 + E1 * C1
        WEND = WS + C1

        def wait(eng, name, value):
            if not isinstance(value, int) or value > 0:
                eng.wait_ge(s[name], value)

        def pairs(eng, body, n):
            body(0)
            with eng.Fori(1, n) as i:
                body(i)

        def chunks(eng, body, layer):
            first, end = ((0, W1), (W1, WEND))[layer]
            loop0 = (first + 4) // 2
            loop1 = (W1 if layer == 0 else WS) // 2
            for w in range(first, 2 * loop0):
                body(w, w // 2, w % 2, min(w - first, 2))
            with eng.Fori(loop0, loop1) as i:
                for u in range(2):
                    body(2 * i + u, i, u, 2)
            for w in range(2 * loop1, end):
                body(w, w // 2, w % 2, 2)

        def is_last(w):
            return isinstance(w, int) and w + 1 in (W1, WEND)

        def is_gelu(w):
            return isinstance(w, int) and w >= WS

        block = ctx.enter_context(nc.Block())

        @block.sync
        def _(sp):
            def load_tile(k, j):
                sp.dma_start(ring[:, j, :], a["tok_main"][bass.ds(k, 1), :, :].rearrange("t p n -> (t p) n")
                             ).then_inc(tok_loaded[j], 16)

            for j in range(RING):
                load_tile(j, j)
            with sp.Fori(1, GT // RING) as r:
                for j in range(RING):
                    sp.wait_ge(s["tok_used"], RING * (r - 1) + j + 1)
                    load_tile(r * RING + j, j)
            for j in range(GT % RING):
                k = GT // RING * RING + j
                sp.wait_ge(s["tok_used"], k - RING + 1)
                load_tile(k, j)
            sp.wait_ge(s["tok_used"], GT // RING * RING - RING + GT % RING + 1)
            sp.dma_start(tail, a["tok_tail"]).then_inc(s["tail_loaded"], 16)

            def load_chunk(w, i, u, age):
                layer = w_layer[0]
                few_dram, rows = (a["few0"], comb_rows0) if layer == 0 else (a["few1"], comb_rows1)
                base = 0 if layer == 0 else W1
                wait(sp, "w2l_ready", w - 1)
                sp.dma_start(few[u][:], few_dram[bass.ds(w - base, 1), :, :].rearrange("e p n -> (e p) n")
                             ).then_inc(s[f"few_loaded{u}"], 16)
                wait(sp, "gated_ready", 2 * (w - 1))
                if isinstance(w, int) and (w < IS_CHUNKS or w >= WS):
                    row = a["ones_row"].partition_broadcast(P)
                else:
                    first = IS_CHUNKS if layer == 0 else W1
                    if isinstance(w, int) and w == first:
                        sp.wait_ge(s["combT_copied"], 2 * layer + 2)
                        sp.dma_start(rows, combT[0:rows.shape[0], :]).then_inc(s["comb_stored"], 16)
                        sp.wait_ge(s["comb_stored"], 16 * (layer + 1))
                    row = rows[bass.ds(w - first, 1), :].rearrange("a n -> (a n)").partition_broadcast(P)
                sp.dma_start(comb_b[u][:], row).then_inc(s[f"row_loaded{u}"], 16)

            w_layer = [0]
            chunks(sp, load_chunk, 0)
            w_layer[0] = 1
            chunks(sp, load_chunk, 1)

            o = out.rearrange("(t s) b d -> (s b) t d", s=P // B)
            for h in range(2):
                sp.wait_ge(s["out_ready"], h + 1)
                sp.dma_start(o[:, 4 * h:4 * h + 4, :], H[:, 4 * h:4 * h + 4, :]).then_inc(s["out_stored"], 16)
            sp.wait_ge(s["out_stored"], 32)

        @block.scalar
        def _(act):
            for dst, src in consts:
                act.dma_start(dst, src).then_inc(s["const_loaded"], 16)

            act.wait_ge(s["tok_done"], 1)
            for h in range(2):
                nc.scalar.copy(H[:, 4 * h:4 * h + 4, :], bank[h][:].rearrange("p (t d) -> p t d", d=D)
                               ).then_inc(s["h0_ready"], 1)

            def in_front(i, u):
                t = 2 * i + u
                act.wait_ge(s["xT_done"], t + 1)
                wait(act, "v_done", t - 1)
                nc.scalar.copy(hT[u][:], bank[0][:, 0:P]).then_inc(s["hT_ready"], 1)
                act.wait_ge(s["k_done"], t + 1)
                wait(act, "x_done", 2 * (t - 1))
                kp = bank[2][:].rearrange("p (c r) -> p c r", c=NC)
                nc.scalar.mul(km2[u][:], kp, -2.0).then_inc(s["k_read"], 1)
                nc.scalar.activation(ksq[u][:], kp, ACT.Square).then_inc(s["k_read"], 1)
                act.wait_ge(s["v_done"], t + 1)
                wait(act, "pv_done", t - 1)
                nc.scalar.copy(vt[u][:], bank[3][:]).then_inc(s["v_read"], 1)

            def distance1(i, u):
                t = 2 * i + u
                act.wait_ge(s["x_done"], 2 * t + 2)
                wait(act, "m_done", t - 1)
                nc.scalar.mul(z1[u][:], bank[5][:].rearrange("p (n j) -> p n j", j=S), 1.5 * SCALE
                              ).then_inc(s["z1_read"], 1)

            def prob(i, u):
                t = 2 * i + u
                act.wait_ge(s["e_ready"], t + 1)
                nc.scalar.activation(sc[u][:], sc[u][:], ACT.Exp, scale=-1.0).then_inc(s["p_exp"], 1)

            def mix(i, u):
                t = 2 * i + u
                act.wait_ge(s["pT_done"], t + 1)
                wait(act, "pv_done", t - 1)
                nc.scalar.copy(pT[u][:], bank[6][:].rearrange("p (c r) -> p c r", c=NC)).then_inc(s["pT_ready"], 1)
                act.wait_ge(s["pv_done"], t + 1)
                wait(act, "wo_done", t - 1)
                nc.scalar.copy(vecT[u][:, :, 0, :], bank[6][:, 0:NC * S].rearrange("p (c i) -> p c i", c=NC)
                               ).then_inc(s["vec0_ready"], 1)

            def attention(i):
                in_front(i, 0)
                distance1(i, 0)
                in_front(i, 1)
                prob(i, 0)
                distance1(i, 1)
                prob(i, 1)
                mix(i, 0)
                mix(i, 1)
            pairs(act, attention, NT // 2)

            def copy_transposed(n, dst):
                for h in range(2):
                    act.wait_ge(s["tr_done"], 2 * n + h + 1)
                    nc.scalar.copy(dst(h), bank[h][:] if len(dst(h).shape) == 2 else
                                   bank[h][:].rearrange("p (t d) -> p t d", d=D)).then_inc(s["tr_copied"], 1)

            def XT_half(h):
                return XT[:, 512 * h:512 * h + 512]

            def x_high(layer, n):
                act.wait_ge(s["tr_copied"], 2 * n + 2)
                nc.scalar.copy(XTh[:], XT[:]).then_inc(s["xth_ready"], 1)

            def comb_transposed(layer, n):
                for h in range(2):
                    act.wait_ge(s["combT_done"], 2 * layer + h + 1)
                    nc.scalar.copy(combT[0:n, 512 * h:512 * h + 512], bank[h][0:n, :]).then_inc(s["combT_copied"], 1)

            def w13_high(w, i, u):
                act.wait_ge(s[f"few_loaded{u}"], 16 * (i + 1))
                wait(act, "h_done", 2 * (w - 1))
                wait(act, "w13l_ready", w - 1)
                nc.scalar.copy(fewh13[u][:], few[u][:, 0:2 * P]).then_inc(s["w13h_ready"], 1)

            def w2_high(w, u):
                wait(act, "y_done", 2 * (w - 1))
                wait(act, "w2l_ready", w - 1)
                nc.scalar.copy(fewh2[u][:], few[u][:, 2 * P:]).then_inc(s["w2h_ready"], 1)

            def activate(n, m, gelu):
                act.wait_ge(s["h_done" if gelu else "h1_done"], n + 1)
                wait(act, "gated_ready", n - 1)
                nc.scalar.activation(act_s[m % 2][:], bank[m % 2][:], ACT.Gelu if gelu else ACT.Silu
                                     ).then_inc(s["act_ready"], 1)

            def hidden_high(n, m):
                act.wait_ge(s["hid_ready"], n + 1)
                wait(act, "y_done", n - 3)
                nc.scalar.copy(hidh[m % 4][:], hid[m % 2][:]).then_inc(s["hidh_ready"], 1)

            def chunk(w, i, u, age):
                n = 2 * w
                activate(n, 2 * u, is_gelu(w))
                if age:
                    hidden_high(n - 1, 2 * u - 1)
                if not is_last(w):
                    w13_high(w + 1, i + u, 1 - u)
                activate(n + 1, 2 * u + 1, is_gelu(w))
                hidden_high(n, 2 * u)
                w2_high(w, u)
                if is_last(w):
                    hidden_high(n + 1, 2 * u + 1)

            copy_transposed(0, XT_half)
            x_high(0, 0)
            act.wait_ge(s["logits_done"], 1)
            nc.scalar.copy(lg[:], bank[2][:].rearrange("p (t e) -> p t e", e=E0)).then_inc(s["logits_copied"], 1)
            for h in range(2):
                act.wait_ge(s["ht_done"], h + 1)
                nc.scalar.copy(HT[:, 512 * h:512 * h + 512], bank[6 + h][:]).then_inc(s["ht_copied"], 1)
            act.wait_ge(s["lmax_sub"], 1)
            nc.scalar.activation(comb[:], comb[:], ACT.Exp).then_inc(s["lexp"], 1)
            comb_transposed(0, E0)
            w13_high(0, 0, 0)
            chunks(act, chunk, 0)

            copy_transposed(1, lambda h: H[:, 4 * h:4 * h + 4, :])
            copy_transposed(2, XT_half)
            for n in range(4):
                j, h = n // 2, n % 2
                act.wait_ge(s["qk1_done"], n + 1)
                bias = (b1q, b1k)[j][:, 0:1]
                cols = slice(512 * h, 512 * h + 512)
                nc.scalar.activation(eq[:, j, cols], bank[2 + n][:], ACT.Exp, bias=bias).then_inc(s["erq_ready"], 1)
                nc.scalar.activation(rq[:, j, cols], bank[2 + n][:], ACT.Relu, bias=bias).then_inc(s["erq_ready"], 1)
            for h in range(2):
                act.wait_ge(s["v1_done"], h + 1)
                act.wait_ge(s["fill_done"], 1)
                nc.scalar.copy(VA[:, 4 * h:4 * h + 4, :, 0:DH1].rearrange("p t h d -> p (t h) d"),
                               bank[6 + h][:].rearrange("p (t d) -> p t d", d=DH1)).then_inc(s["va_ready"], 1)
            copy_transposed(3, XT_half)
            copy_transposed(4, XT_half)
            for n in range(2 * (FF // P)):
                f, h = n // 2, n % 2
                act.wait_ge(s["ff1_done"], n + 1)
                nc.scalar.activation(FT[:, f, 512 * h:512 * h + 512], bank[2 + n % 4][:], ACT.Relu,
                                     bias=bf1[:, f:f + 1]).then_inc(s["ft_ready"], 1)

            copy_transposed(5, XT_half)
            x_high(1, 5)
            act.wait_ge(s["logits_done"], 2)
            nc.scalar.copy(lg[:, :, 0:E1], bank[2][:, 0:NT * E1].rearrange("p (t e) -> p t e", e=E1)
                           ).then_inc(s["logits_copied"], 1)
            comb_transposed(1, E1 * C1)
            w13_high(W1, W1 // 2, W1 % 2)
            chunks(act, chunk, 1)

        @block.gpsimd
        def _(pool):
            pool.memset(neg_half[:], -0.5).then_inc(s["fill_done"], 1)

            def root(k):
                pool.wait_ge(s["var_ready"], k)
                pool.wait_ge(s["fill_done"], 1)
                pool.tensor_tensor(rstd[:], var_eps[:], neg_half[:], ALU.pow).then_inc(s["rstd_ready"], 1)

            def q_squares(i, u):
                t = 2 * i + u
                pool.wait_ge(s["q_read"], t + 1)
                wait(pool, "x_done", 2 * (t - 1))
                pool.tensor_tensor(qsq[u][:], qc[u][:], qc[u][:], ALU.mult).then_inc(s["qsq_ready"], 1)

            def attention(i):
                q_squares(i, 0)
                q_squares(i, 1)

            def chunk(w, i, u, age):
                pool.wait_ge(s[f"row_loaded{u}"], 16 * (i + 1))
                for h in range(2):
                    n = 2 * w + h
                    pool.wait_ge(s["act_ready"], n + 1)
                    wait(pool, "hid_ready", n - 1)
                    pool.tensor_tensor(act_g[h][:], act_s[h][:], comb_b[u][:, 512 * h:512 * h + 512], ALU.mult
                                       ).then_inc(s["gated_ready"], 1)

            root(1)
            pairs(pool, attention, NT // 2)
            root(2)
            root(3)
            chunks(pool, chunk, 0)
            root(4)
            root(5)
            for T in range(NT):
                pool.wait_ge(s["qk_ready"], 4)
                wait(pool, "at_done", 2 * (T - 1))
                pool.tensor_tensor(qbd[T % 2], QT[:, P * T:P * T + P].unsqueeze(1).broadcast_to([P, H1, P]),
                                   headmask[:].unsqueeze(2).broadcast_to([P, H1, P]), ALU.mult
                                   ).then_inc(s["qbd_ready"], 1)
            root(6)
            root(7)
            chunks(pool, chunk, 1)

        @block.vector
        def _(dve):
            class Chain:
                base, n = 0, 0

                def __call__(self, ins):
                    self.n += 1
                    ins.then_inc(s["dve_step"], 1)

                def sync(self):
                    dve.wait_ge(s["dve_step"], self.base + self.n)

                def link(self, ins):
                    self(ins)
                    self.sync()
            chain = Chain()

            def stats_of(src, k):
                for T in range(NT):
                    chain(dve.bn_stats(stats[:, T, :], src[:, T, :]))
                chain.sync()
                for T in range(NT):
                    chain(dve.bn_aggr(mv[:, T, :], stats[:, T, :]))
                chain.sync()
                dve.tensor_scalar(var_eps[:], mv[:, :, 1], EPS, None, ALU.add).then_inc(s["var_ready"], 1)
                dve.wait_ge(s["rstd_ready"], k)

            def normalised(dst, src, signal=None):
                for T in range(NT):
                    ins = dve.tensor_scalar(dst[:, T, :], src[:, T, :], mv[:, T, 0:1], rstd[:, T:T + 1],
                                            ALU.subtract, ALU.mult)
                    if signal and T == NT - 1:
                        ins.then_inc(s[signal], 1)
                    else:
                        chain(ins)
                if not signal:
                    chain.sync()

            def vec(n):
                return rowvec[:, n, :].unsqueeze(1).broadcast_to([P, NT, D])

            def mask(rows, slot_ap):
                w = slot_ap[:, 0:B * D].rearrange("p (b d) -> p b d", d=D)
                m = slot_ap[:, B * D + S:].unsqueeze(1).broadcast_to([rows, B, D])
                dve.tensor_tensor(w, w, m, ALU.mult).then_inc(s["tok_masked"], 1)

            dve.memset(onescol[:], 1.0).then_inc(s["dve_step"], 1)
            dve.memset(VA[:].rearrange("p t h d -> p (t h d)"), 1.0).then_inc(s["dve_step"], 1)
            chain.n = 2
            with dve.Fori(0, GT // RING) as r:
                for j in range(RING):
                    dve.wait_ge(tok_loaded[j], 16 * (r + 1))
                    mask(P, ring[:, j, :])
            for j in range(GT % RING):
                dve.wait_ge(tok_loaded[j], 16 * (GT // RING + 1))
                mask(P, ring[:, j, :])
            dve.wait_ge(s["tail_loaded"], 16)
            mask(GR, tail)

            dve.wait_ge(s["h0_ready"], 2)
            stats_of(H, 1)
            dve.wait_ge(s["const_loaded"], N_CONSTS)

            def normed(i, u):
                t = 2 * i + u
                wait(dve, "y_ready", t - 1)
                wait(dve, "xT_done", t - 1)
                dve.tensor_scalar(xs[u][:], H[:, bass.ds(t, 1), :].rearrange("p a d -> p (a d)"),
                                  mv[:, bass.ds(t, 1), 0:1].rearrange("p a d -> p (a d)"), rstd[:, bass.ds(t, 1)],
                                  ALU.subtract, ALU.mult).then_inc(s["xs_ready"], 1)

            def queries(i, u):
                t = 2 * i + u
                dve.wait_ge(s["q_done"], t + 1)
                wait(dve, "x_done", 2 * (t - 1))
                wait(dve, "qsq_ready", t - 1)
                for c in range(2):
                    ins = dve.tensor_tensor(qc[u][:, c, :, :], bank[1][:].rearrange("p (c r) -> p c r", c=NC),
                                            mu[:, c, :].unsqueeze(2).broadcast_to([P, NC, P]), ALU.add)
                ins.then_inc(s["q_read"], 1)

            def nearer(i, u):
                t = 2 * i + u
                dve.wait_ge(s["z1_read"], t + 1)
                wait(dve, "pT_done", t - 1)
                dve.scalar_tensor_tensor(out=sc[u][:], in0=bank[4][:].rearrange("p (n j) -> p n j", j=S),
                                         scalar=0.5 * SCALE, in1=z1[u][:], op0=ALU.mult, op1=ALU.min
                                         ).then_inc(s["m_done"], 1)

            def shifted(i, u):
                t = 2 * i + u
                dve.wait_ge(s["m_done"], t + 1)
                chain.link(dve.tensor_reduce(rmin[u][:], sc[u][:], AX.X, ALU.min))
                chain.link(dve.tensor_scalar(rmin[u][:], rmin[u][:], 0.0, None, ALU.max))
                dve.scalar_tensor_tensor(out=sc[u][:], in0=sc[u][:], scalar=0.0,
                                         in1=rmin[u][:].unsqueeze(2).broadcast_to([P, 2 * NC, S]),
                                         op0=ALU.max, op1=ALU.subtract).then_inc(s["e_ready"], 1)

            def probs(i, u):
                t = 2 * i + u
                dve.wait_ge(s["p_exp"], t + 1)
                chain.link(dve.tensor_reduce(rsum[u][:], sc[u][:], AX.X, ALU.add))
                chain.link(dve.reciprocal(rsum[u][:], rsum[u][:]))
                dve.tensor_tensor(sc[u][:], sc[u][:], rsum[u][:].unsqueeze(2).broadcast_to([P, 2 * NC, S]),
                                  ALU.mult).then_inc(s["p_ready"], 1)

            def mixed(i, u):
                t = 2 * i + u
                dve.wait_ge(s["pv_done"], t + 1)
                wait(dve, "wo_done", t - 1)
                dve.tensor_copy(vecT[u][:, :, 1, :], bank[7][:, 0:NC * S].rearrange("p (c i) -> p c i", c=NC)
                                ).then_inc(s["vec1_ready"], 1)
                dve.wait_ge(s["wo_done"], t + 1)
                dve.tensor_tensor(Y[:, bass.ds(t, 1), :].rearrange("p a d -> p (a d)"), bank[0][:, P:2 * P],
                                  xs[u][:], ALU.add).then_inc(s["y_ready"], 1)

            STEPS = 8
            before = chain.n

            def attention(i):
                chain.base, chain.n = before + STEPS * i, 0
                normed(i, 0)
                queries(i, 0)
                normed(i, 1)
                nearer(i, 0)
                queries(i, 1)
                shifted(i, 0)
                nearer(i, 1)
                probs(i, 0)
                shifted(i, 1)
                probs(i, 1)
                mixed(i, 0)
                mixed(i, 1)
                assert chain.n == STEPS
            pairs(dve, attention, NT // 2)
            chain.base, chain.n = 0, before + STEPS * NT // 2

            dve.wait_ge(s["y_ready"], NT)
            stats_of(Y, 2)
            normalised(XN, Y)
            chain.link(dve.tensor_tensor(XN[:], XN[:], vec(0), ALU.mult))
            chain.link(dve.tensor_tensor(XN[:], XN[:], vec(1), ALU.add))
            chain.link(dve.tensor_tensor(H[:], H[:], XN[:], ALU.add))

            stats_of(H, 3)
            normalised(XN, H, "norm_ready")

            def x_low(layer):
                dve.wait_ge(s["xth_ready"], layer + 1)
                dve.tensor_tensor(XTl[:], XT[:], XTh[:].bitcast(F32), ALU.subtract).then_inc(s["xtl_ready"], 1)

            x_low(0)
            dve.wait_ge(s["logits_copied"], 1)
            for T in range(NT):
                chain(dve.max(mx[:, T, :], lg[:, T, :]))
            chain.sync()
            dve.tensor_tensor(comb[:], lg[:], mx[:, :, 0:1].broadcast_to([P, NT, E0]), ALU.subtract
                              ).then_inc(s["lmax_sub"], 1)
            TAKEN = -3.0e38
            for T in range(NT):
                chain(dve.match_replace(lgr[:, T, :], mx[:, T, :], lg[:, T, :], TAKEN))
            chain.sync()
            chain.link(dve.tensor_scalar(lgr[:], lgr[:], TAKEN, None, ALU.is_equal))
            dve.wait_ge(s["lexp"], 1)
            chain.link(dve.tensor_tensor(comb[:], comb[:], lgr[:], ALU.mult))
            chain.link(dve.tensor_reduce(rs8[:], comb[:], AX.X, ALU.add))
            chain.link(dve.reciprocal(rs8[:], rs8[:]))
            dve.tensor_tensor(comb[:], comb[:], rs8[:].unsqueeze(2).broadcast_to([P, NT, E0]), ALU.mult
                              ).then_inc(s["comb_ready"], 1)

            def w13_low(w, u):
                dve.wait_ge(s["w13h_ready"], w + 1)
                dve.tensor_tensor(fewl13[u][:], few[u][:, 0:2 * P], fewh13[u][:].bitcast(F32), ALU.subtract
                                  ).then_inc(s["w13l_ready"], 1)

            def w2_low(w, u):
                dve.wait_ge(s["w2h_ready"], w + 1)
                dve.tensor_tensor(fewl2[u][:], few[u][:, 2 * P:], fewh2[u][:].bitcast(F32), ALU.subtract
                                  ).then_inc(s["w2l_ready"], 1)

            def hidden(n, m, gelu):
                dve.wait_ge(s["gated_ready"], n + 1)
                dve.wait_ge(s["h_done"], n + 1)
                wait(dve, "hidh_ready", n - 1)
                wait(dve, "hidl_ready", n - 1)
                if gelu:
                    dve.tensor_copy(hid[m % 2][:], act_g[m % 2][:]).then_inc(s["hid_ready"], 1)
                else:
                    dve.tensor_tensor(hid[m % 2][:], bank[2 + m % 2][:], act_g[m % 2][:], ALU.mult
                                      ).then_inc(s["hid_ready"], 1)

            def hidden_low(n, m):
                dve.wait_ge(s["hidh_ready"], n + 1)
                dve.tensor_tensor(hidl[m % 4][:], hid[m % 2][:], hidh[m % 4][:].bitcast(F32), ALU.subtract
                                  ).then_inc(s["hidl_ready"], 1)

            def chunk(w, i, u, age):
                n = 2 * w
                hidden(n, 2 * u, is_gelu(w))
                if age:
                    hidden_low(n - 1, 2 * u - 1)
                if not is_last(w):
                    w13_low(w + 1, 1 - u)
                hidden(n + 1, 2 * u + 1, is_gelu(w))
                hidden_low(n, 2 * u)
                w2_low(w, u)
                if is_last(w):
                    hidden_low(n + 1, 2 * u + 1)

            w13_low(0, 0)
            chunks(dve, chunk, 0)

            dve.wait_ge(s["ht_copied"], 2)
            dve.wait_ge(s["y_done"], 2 * W1)
            for h in range(2):
                dve.tensor_tensor(XT[:].rearrange("p (s b) -> p b s", b=B)[:, 8 * h:8 * h + 8, :],
                                  HT[:, 512 * h:512 * h + 512].rearrange("p (b s) -> p b s", s=S),
                                  bank[4 + h][:].rearrange("p (b s) -> p b s", s=S), ALU.add
                                  ).then_inc(s["g_ready"], 1)
            dve.wait_ge(s["tr_copied"], 4)
            stats_of(H, 4)
            normalised(X1, H)
            stats_of(X1, 5)
            normalised(HN, X1)
            chain.link(dve.tensor_tensor(HN, HN, vec(2), ALU.mult))
            dve.tensor_tensor(HN, HN, vec(3), ALU.add).then_inc(s["norm_ready"], 1)
            for n in range(4):
                j, h = n // 2, n % 2
                cols = slice(512 * h, 512 * h + 512)
                dve.wait_ge(s["erq_ready"], 2 * n + 2)
                dve.scalar_tensor_tensor(out=(QT, KT)[j][:, cols], in0=eq[:, j, cols], scalar=1.0,
                                         in1=rq[:, j, cols], op0=ALU.min, op1=ALU.add).then_inc(s["qk_ready"], 1)

            def causal_scores(T):
                wait(dve, "num_done", T - 1)
                for q in range(2):
                    dve.wait_ge(s["at_done"], 2 * T + q + 1)
                    dve.tensor_tensor(am[T % 2][:, 4 * q:4 * q + 4, :],
                                      bank[2 * (T % 2) + q][:].rearrange("p (h r) -> p h r", h=4),
                                      causal[:].unsqueeze(1).broadcast_to([P, 4, P]), ALU.mult
                                      ).then_inc(s["am_ready"], 1)

            def divided(T):
                dve.wait_ge(s["num_done"], T + 1)
                o = bank[4 + T % 2][:, 0:H1 * (DH1 + 1)].rearrange("p (h d) -> p h d", h=H1)
                chain.link(dve.tensor_scalar(den[:, T, :], o[:, :, DH1], DEN_MIN, None, ALU.max))
                chain.link(dve.reciprocal(rden[:, T, :], den[:, T, :]))
                dve.tensor_tensor(AO[:, T, :].rearrange("p (h d) -> p h d", h=H1), o[:, :, 0:DH1],
                                  rden[:, T, :].unsqueeze(2).broadcast_to([P, H1, DH1]), ALU.mult
                                  ).then_inc(s["ao_ready"], 1)

            causal_scores(0)
            for T in range(NT):
                if T + 1 < NT:
                    causal_scores(T + 1)
                divided(T)
            for h in range(2):
                dve.wait_ge(s["wo1_done"], h + 1)
                chain(dve.tensor_tensor(Y[:, 4 * h:4 * h + 4, :], X1[:, 4 * h:4 * h + 4, :],
                                        bank[h][:].rearrange("p (t d) -> p t d", d=D), ALU.add))
            chain.sync()
            stats_of(Y, 6)
            normalised(HN2, Y)
            chain.link(dve.tensor_tensor(HN2, HN2, vec(4), ALU.mult))
            dve.tensor_tensor(HN2, HN2, vec(5), ALU.add).then_inc(s["norm_ready"], 1)
            chain.link(dve.tensor_tensor(H[:], H[:], Y[:], ALU.add))
            for h in range(2):
                dve.wait_ge(s["ff2_done"], h + 1)
                chain(dve.tensor_tensor(H[:, 4 * h:4 * h + 4, :], H[:, 4 * h:4 * h + 4, :],
                                        bank[6 + h][:].rearrange("p (t d) -> p t d", d=D), ALU.add))
            chain.sync()

            stats_of(H, 7)
            normalised(XN, H, "norm_ready")
            x_low(1)
            dve.wait_ge(s["logits_copied"], 2)
            for T in range(NT):
                chain(dve.max(mx[:, T, :], lg[:, T, 0:E1]))
            chain.sync()
            for T in range(NT):
                chain(dve.max_index(mxi[:, T, :], mx[:, T, :], lg[:, T, 0:E1]))
            chain.sync()
            chain.link(dve.tensor_copy(rs8[:], mxi[:, :, 0]))
            chain.link(dve.tensor_tensor(lgr[:, :, 0:E1], iota8[:].unsqueeze(1).broadcast_to([P, NT, E1]),
                                         rs8[:].unsqueeze(2).broadcast_to([P, NT, E1]), ALU.is_equal))
            for c in range(C1):
                ins = dve.tensor_copy(comb[:, :, 0:E1 * C1].rearrange("p t (e c) -> p t e c", c=C1)[:, :, :, c],
                                      lgr[:, :, 0:E1])
            ins.then_inc(s["comb_ready"], 1)
            w13_low(W1, W1 % 2)
            chunks(dve, chunk, 1)
            dve.wait_ge(s["y_done"], 2 * WEND)
            for h in range(2):
                dve.tensor_copy(HT[:, 512 * h:512 * h + 512], bank[4 + h][:]).then_inc(s["g_ready"], 1)
            for h in range(2):
                dve.wait_ge(s["tr_done"], 2 * 6 + h + 1)
                dve.tensor_tensor(H[:, 4 * h:4 * h + 4, :], H[:, 4 * h:4 * h + 4, :],
                                  bank[h][:].rearrange("p (t d) -> p t d", d=D), ALU.add).then_inc(s["out_ready"], 1)

        @block.tensor
        def _(pe):
            def tok_product(src, h, b2, **flags):
                return pe.matmul(bank[h][S * b2:S * b2 + S, :], src[:, B * D:B * D + S],
                                 src[:, 1024 * b2 + 512 * h:1024 * b2 + 512 * h + 512], **flags)

            def tile_products(src, signal, stop=False):
                for h in range(2):
                    for b2 in range(2):
                        mm = tok_product(src, h, b2, start=False, stop=stop)
                mm.then_inc(s[signal], 1)

            pe.wait_ge(s["const_loaded"], N_CONSTS)
            for h in range(2):
                for b2 in range(2):
                    pe.matmul(bank[h][S * b2:S * b2 + S, :], onesrow[:, 0:S],
                              qc[b2][0:1, h, :, :].rearrange("p c r -> p (c r)"), start=True, stop=False)
            with pe.Fori(0, GT // RING) as r:
                for j in range(RING):
                    pe.wait_ge(s["tok_masked"], RING * r + j + 1)
                    tile_products(ring[:, j, :], "tok_used")
            for j in range(GT % RING):
                pe.wait_ge(s["tok_masked"], GT // RING * RING + j + 1)
                tile_products(ring[:, j, :], "tok_used")
            pe.wait_ge(s["tok_masked"], GT + 1)
            tile_products(tail, "tok_done", stop=True)

            def project(i, u):
                t = 2 * i + u
                pe.wait_ge(s["xs_ready"], t + 1)
                wait(pe, "hT_ready", t)
                pe.transpose(bank[0][:, 0:P], xs[u][:], ident[:]).then_inc(s["xT_done"], 1)
                pe.wait_ge(s["hT_ready"], t + 1)
                wait(pe, "q_read", t)
                for c in range(NC):
                    mm = pe.matmul(bank[1][:, P * c:P * c + P], wq[:, P * c:P * c + P], hT[u][:], start=True, stop=True)
                mm.then_inc(s["q_done"], 1)
                wait(pe, "k_read", 2 * t)
                for c in range(NC):
                    mm = pe.matmul(bank[2][:, P * c:P * c + P], wkv[:, P * c:P * c + P], hT[u][:], start=True, stop=True)
                mm.then_inc(s["k_done"], 1)
                wait(pe, "v_read", t)
                pe.matmul(bank[3][:], hT[u][:], wkv[:, NHEAD * DH:], start=True, stop=True).then_inc(s["v_done"], 1)

            def wait_apart():
                pe.wait_ge(s["const_loaded"], N_CONSTS)

            def distances(i, u):
                t = 2 * i + u
                pe.wait_ge(s["k_read"], 2 * t + 2)
                wait(pe, "m_done", t)
                wait(pe, "z1_read", t)
                for m in range(2):
                    pe.matmul(bank[4 + m][:], headones[:], ksq[u][:].rearrange("p c r -> p (c r)"),
                              start=True, stop=True)
                wait_apart()
                pe.wait_ge(s["q_read"], t + 1)

                def blocks(m, left, right):
                    for c in range(NC):
                        for b2 in range(2):
                            for n2 in range(2):
                                rows = slice(S * n2, S * n2 + S)
                                mm = pe.matmul(bank[4 + m][rows, S * (2 * c + b2):S * (2 * c + b2) + S],
                                               left(rows, c, b2), right(rows, c, b2), start=False,
                                               stop=True,
                                               skip_group_check=True)
                    return mm
                for m in range(2):
                    blocks(m, lambda r, c, b2: qc[u][r, m, c, S * b2:S * b2 + S],
                           lambda r, c, b2: km2[u][r, c, S * b2:S * b2 + S])
                wait_apart()
                pe.wait_ge(s["qsq_ready"], t + 1)
                for m in range(2):
                    blocks(m, lambda r, c, b2: qsq[u][r, m, c, S * b2:S * b2 + S],
                           lambda r, c, b2: onescol[r, :]).then_inc(s["x_done"], 1)

            def mix(i, u):
                t = 2 * i + u
                pe.wait_ge(s["p_ready"], t + 1)
                wait(pe, "vec0_ready", t)
                for c in range(NC):
                    mm = pe.transpose(bank[6][:, P * c:P * c + P], sc[u][:, 2 * c:2 * c + 2, :].rearrange(
                        "p n j -> p (n j)"), ident[:])
                mm.then_inc(s["pT_done"], 1)
                wait_apart()
                pe.wait_ge(s["pT_ready"], t + 1)
                pe.wait_ge(s["v_read"], t + 1)
                wait(pe, "vec1_ready", t)
                for c in range(NC):
                    for n2 in range(2):
                        for b2 in range(2):
                            rows = slice(S * b2, S * b2 + S)
                            mm = pe.matmul(bank[6 + b2][S * n2:S * n2 + S, S * c:S * c + S],
                                           vt[u][rows, DH * (2 * c + n2):DH * (2 * c + n2) + DH],
                                           pT[u][rows, c, S * n2:S * n2 + S], start=True, stop=True)
                mm.then_inc(s["pv_done"], 1)
                pe.wait_ge(s["vec0_ready"], t + 1)
                pe.wait_ge(s["vec1_ready"], t + 1)
                wait(pe, "y_ready", t)
                for c in range(NC):
                    mm = pe.matmul(bank[0][:, P:2 * P], vecT[u][:, c, :, :].rearrange("p b i -> p (b i)"), wo[:, c, :],
                                   start=(c == 0), stop=(c == NC - 1))
                mm.then_inc(s["wo_done"], 1)

            def attention(i):
                project(i, 0)
                distances(i, 0)
                project(i, 1)
                distances(i, 1)
                mix(i, 0)
                mix(i, 1)
            pe.wait_ge(s["dve_step"], 2)
            pairs(pe, attention, NT // 2)

            def transposed(src_tile, first_bank, signal):
                for T in range(NT):
                    tr = pe.transpose(bank[first_bank + T // 4][:, P * (T % 4):P * (T % 4) + P], src_tile(T), ident[:])
                    if T % 4 == 3:
                        tr.then_inc(s[signal], 1)

            pe.wait_ge(s["norm_ready"], 1)
            transposed(lambda T: XN[:, T, :], 0, "tr_done")
            transposed(lambda T: H[:, T, :], 6, "ht_done")

            def logits(gate, e):
                for T in range(NT):
                    mm = pe.matmul(bank[2][:, e * T:e * T + e], XT[:, P * T:P * T + P], gate[:], start=True, stop=True)
                mm.then_inc(s["logits_done"], 1)

            def comb_transposed(e, layer):
                pe.wait_ge(s["comb_ready"], layer + 1)
                for T in range(NT):
                    mm = pe.matmul(bank[T // 4][0:e, P * (T % 4):P * (T % 4) + P], comb[:, T, 0:e], ident[:],
                                   start=True, stop=True)
                    if T % 4 == 3:
                        mm.then_inc(s["combT_done"], 1)

            def three(dst, high, low, x_high, x_low, start, stop):
                pe.matmul(dst, high, x_high, start=start, stop=False)
                pe.matmul(dst, high, x_low, start=False, stop=False)
                return pe.matmul(dst, low, x_high, start=False, stop=stop)

            def units_in(w, n, m, u, h):
                cols = slice(512 * h, 512 * h + 512)
                wait(pe, "act_ready", n - 1)
                for j in range(1 if is_gelu(w) else 2):
                    if j == 1:
                        wait(pe, "hid_ready", n - 1)
                    c = slice(P * j, P * j + P)
                    mm = three(bank[2 * j + m % 2][:], fewh13[u][:, c], fewl13[u][:, c], XTh[:, cols], XTl[:, cols],
                               True, True)
                    if is_gelu(w) or j == 1:
                        mm.then_inc(s["h_done"], 1)
                    else:
                        mm.then_inc(s["h1_done"], 1)

            def unit_out(w, n, m, first, last):
                pe.wait_ge(s["hidl_ready"], n + 1)
                pe.wait_ge(s["w2l_ready"], w + 1)
                u = m // 2 % 2
                three(bank[4 + m % 2][:], fewh2[u][:], fewl2[u][:], hidh[m % 4][:], hidl[m % 4][:], first, last
                      ).then_inc(s["y_done"], 1)

            def chunk(w, i, u, age):
                n, m = 2 * w, 2 * u
                pe.wait_ge(s["w13l_ready"], w + 1)
                units_in(w, n, m, u, 0)
                if age == 2:
                    unit_out(w - 2, n - 3, m - 3, isinstance(w, int) and w in (2, W1 + 2), False)
                units_in(w, n + 1, m + 1, u, 1)
                if age:
                    unit_out(w - 1, n - 2, m - 2, age == 1, False)
                if is_last(w):
                    unit_out(w - 1, n - 1, m - 1, False, False)
                    unit_out(w, n, m, False, True)
                    unit_out(w, n + 1, m + 1, False, True)

            pe.wait_ge(s["tr_copied"], 2)
            logits(gate0, E0)
            comb_transposed(E0, 0)
            pe.wait_ge(s["xtl_ready"], 1)
            pe.wait_ge(s["combT_copied"], 2)
            pe.wait_ge(s["ht_copied"], 2)
            chunks(pe, chunk, 0)

            pe.wait_ge(s["g_ready"], 2)
            transposed(lambda T: XT[:, P * T:P * T + P], 0, "tr_done")
            pe.wait_ge(s["norm_ready"], 2)
            transposed(lambda T: HN[:, T, :], 0, "tr_done")
            pe.wait_ge(s["tr_copied"], 6)
            for n in range(4):
                j, h = n // 2, n % 2
                pe.matmul(bank[2 + n][:], (w1q, w1k)[j][:], XT[:, 512 * h:512 * h + 512], start=True, stop=True
                          ).then_inc(s["qk1_done"], 1)

            def rows_product(first_bank, bias, terms, signal):
                for h in range(2):
                    bk = bank[first_bank + h]
                    pe.matmul(bk[:], onesrow[:, 0:P], bvob2[:, bias, :].unsqueeze(1).broadcast_to([1, 4, D]),
                              start=True, stop=True)
                    for T in range(4 * h, 4 * h + 4):
                        for left, right in terms(T):
                            mm = pe.matmul(bk[:, D * (T % 4):D * (T % 4) + D], left, right, start=False,
                                           stop=True, skip_group_check=True)
                    mm.then_inc(s[signal], 1)

            def XT_tile(T):
                return XT[:, P * T:P * T + P]

            rows_product(6, 0, lambda T: [(XT_tile(T), w1v[:])], "v1_done")

            def scores1(T):
                pe.wait_ge(s["qbd_ready"], T + 1)
                wait(pe, "am_ready", 2 * (T - 1))
                for q in range(2):
                    pe.matmul(bank[2 * (T % 2) + q][:], KT[:, P * T:P * T + P],
                              qbd[T % 2][:, 4 * q:4 * q + 4, :].rearrange("p h r -> p (h r)"), start=True, stop=True
                              ).then_inc(s["at_done"], 1)

            def sums1(T):
                pe.wait_ge(s["am_ready"], 2 * T + 2)
                wait(pe, "ao_ready", T - 1)
                for h in range(H1):
                    mm = pe.matmul(bank[4 + T % 2][:, (DH1 + 1) * h:(DH1 + 1) * (h + 1)], am[T % 2][:, h, :],
                                   VA[:, T, h, :], start=True, stop=True)
                mm.then_inc(s["num_done"], 1)

            pe.wait_ge(s["qk_ready"], 4)
            pe.wait_ge(s["va_ready"], 2)
            scores1(0)
            for T in range(NT):
                if T + 1 < NT:
                    scores1(T + 1)
                sums1(T)
            pe.wait_ge(s["ao_ready"], NT)
            transposed(lambda T: AO[:, T, :], 0, "tr_done")
            pe.wait_ge(s["tr_copied"], 8)
            rows_product(0, 1, lambda T: [(XT_tile(T), w1o[:])], "wo1_done")
            pe.wait_ge(s["norm_ready"], 3)
            transposed(lambda T: HN2[:, T, :], 0, "tr_done")
            pe.wait_ge(s["tr_copied"], 10)
            for n in range(2 * (FF // P)):
                f, h = n // 2, n % 2
                wait(pe, "ft_ready", n - 3)
                pe.matmul(bank[2 + n % 4][:], wf1[:, P * f:P * f + P], XT[:, 512 * h:512 * h + 512],
                          start=True, stop=True).then_inc(s["ff1_done"], 1)
            pe.wait_ge(s["ft_ready"], 2 * (FF // P))
            rows_product(6, 2, lambda T: [(FT[:, f, P * T:P * T + P], wf2[:, f, :]) for f in range(FF // P)],
                         "ff2_done")

            pe.wait_ge(s["norm_ready"], 4)
            transposed(lambda T: XN[:, T, :], 0, "tr_done")
            pe.wait_ge(s["tr_copied"], 12)
            logits(gate1, E1)
            comb_transposed(E1 * C1, 1)
            pe.wait_ge(s["xtl_ready"], 2)
            pe.wait_ge(s["combT_copied"], 4)
            chunks(pe, chunk, 1)
            pe.wait_ge(s["g_ready"], 4)
            transposed(lambda T: HT[:, P * T:P * T + P], 0, "tr_done")


def kernel(**inputs):
    import numpy as np
    import concourse.bacc as bacc
    from concourse.bass_utils import run_bass_kernel_spmd as run

    x = {n: np.asarray(v) for n, v in inputs.items()}

    w = x["L0_tok_weight"].reshape(NT, 2, G, D).transpose(2, 1, 0, 3).reshape(G, B * D)
    tok = np.concatenate([w, x["x"].T, x["L0_tok_mask"]], axis=1)
    arrays = {"tok_main": tok[:GT * P].reshape(GT, P, TOKW), "tok_tail": tok[GT * P:]}
    arrays["tok_bias_row"] = x["L0_tok_bias"].reshape(NT, 2, D).transpose(1, 0, 2).reshape(1, B * D)

    p = np.arange(P)
    arrays["ident"] = np.eye(P, dtype=np.float32)
    arrays["headones"] = (p[:, None] // S == p[None, :] // S).astype(np.float32)
    arrays["causal"] = ((p[:, None] // B == p[None, :] // B) & (p[:, None] <= p[None, :])).astype(np.float32)
    arrays["headmask"] = (p[:, None] // DH1 == np.arange(H1)[None, :]).astype(np.float32)
    arrays["iota8"] = np.tile(np.arange(E1, dtype=np.float32), (P, 1))
    arrays["onesrow"] = np.ones((1, 512), np.float32)
    arrays["ones_row"] = np.ones(ROWS, np.float32)

    for n in ("L0_attn_Wq", "L0_attn_Wkv", "L0_attn_Wo", "L0_attn_gamma", "L0_attn_beta", "L1_attn_ln1_g",
              "L1_attn_ln1_b", "L1_attn_ln2_g", "L1_attn_ln2_b", "L1_attn_Wq", "L1_attn_Wk", "L1_attn_Wv",
              "L1_attn_Wo", "L1_attn_W1", "L1_attn_W2"):
        arrays[n] = x[n]
    for n in ("L1_attn_bq", "L1_attn_bk"):
        arrays[n] = x[n].reshape(D, 1)
    for n in ("L1_attn_bv", "L1_attn_bo", "L1_attn_b2"):
        arrays[n] = x[n].reshape(1, D)
    arrays["b1_cols"] = x["L1_attn_b1"].reshape(FF // P, P).T
    arrays["mu_cols"] = x["L0_attn_mu"].reshape(2, NC, P).transpose(2, 0, 1).reshape(P, 2 * NC)
    arrays["gate0T"] = x["L0_ffn_gate_w"].T
    arrays["gate1T"] = x["L1_ffn_gate_w"].T

    IS = x["L0_ffn_sw1"].shape[1]
    few0 = np.zeros((IS_CHUNKS + E0, P, 3, P), np.float32)
    for c in range(IS_CHUNKS):
        cols = slice(P * c, min(P * c + P, IS))
        k = cols.stop - cols.start
        few0[c, :, 0, :k] = x["L0_ffn_sw1"][:, cols]
        few0[c, :, 1, :k] = x["L0_ffn_sw3"][:, cols]
        few0[c, :k, 2, :] = x["L0_ffn_sw2"][cols]
    few0[IS_CHUNKS:, :, 0] = x["L0_ffn_w1"]
    few0[IS_CHUNKS:, :, 1] = x["L0_ffn_w3"]
    few0[IS_CHUNKS:, :, 2] = x["L0_ffn_w2"]
    arrays["few0"] = few0.reshape(-1, P, FEW)
    few1 = np.zeros((E1 * C1 + C1, P, 3, P), np.float32)
    few1[:E1 * C1, :, 0] = x["L1_ffn_w1"].reshape(E1 * C1, P, D).transpose(0, 2, 1)
    few1[:E1 * C1, :, 1] = x["L1_ffn_w3"].reshape(E1 * C1, P, D).transpose(0, 2, 1)
    few1[:E1 * C1, :, 2] = x["L1_ffn_w2"].reshape(E1, D, C1, P).transpose(0, 2, 3, 1).reshape(E1 * C1, P, D)
    few1[E1 * C1:, :, 0] = x["L1_ffn_sw1"].reshape(C1, P, D).transpose(0, 2, 1)
    few1[E1 * C1:, :, 2] = x["L1_ffn_sw2"].reshape(D, C1, P).transpose(1, 2, 0)
    arrays["few1"] = few1.reshape(-1, P, FEW)
    arrays = {n: np.ascontiguousarray(v) for n, v in arrays.items()}

    nc = bacc.Bacc("TRN2", target_bir_lowering=False, num_devices=1)
    a = {n: nc.dram_tensor(f"in_{n}", v.shape, F32, kind="ExternalInput").ap() for n, v in arrays.items()}
    out = nc.dram_tensor("out_0", (S, B, D), F32, kind="ExternalOutput").ap()
    audio_tower(nc, a, out)
    r = run(nc, [{f"in_{n}": v for n, v in arrays.items()}], core_ids=[0])
    return r.results[0]["out_0"]
```

```python
from contextlib import ExitStack

import concourse.bass as bass
from concourse import mybir

F32 = mybir.dt.float32
F32R = mybir.dt.float32r
U32 = mybir.dt.uint32
ALU = mybir.AluOpType
ACT = mybir.ActivationFunctionType
AX = mybir.AxisListType

P = 128
S, B, D = 64, 16, 128
NT = S * B // P
ROWS = S * B
G = 5000
GT = G // P
GR = G - GT * P
NHEAD, DH = 8, 64
NC = NHEAD * DH // P
SCALE = DH ** -0.5
E0, K0 = 64, 8
SLOTS = 4
IS_CHUNKS = 3
H1, DH1 = 8, 16
FF = 512
E1, I1 = 8, 512
C1 = I1 // P
EPS = 1e-5
DEN_MIN = 1e-6
TOKW = B * D + S + D
RING = 6
FEW = P * 3


def audio_tower(nc, a, out):
    ctx = ExitStack()
    with ctx:
        def sb(name, shape, dt=F32):
            return ctx.enter_context(nc.sbuf_tensor(name, shape, dt))

        def sem(name):
            return ctx.enter_context(nc.semaphore(name))

        bank = [ctx.enter_context(nc.psum_tensor(f"bank{i}", [P, 512], F32)) for i in range(8)]
        comb_rows0 = nc.dram_tensor("comb_rows0", [E0, ROWS], F32).ap()
        comb_rows1 = nc.dram_tensor("comb_rows1", [E1 * C1, ROWS], F32).ap()

        ident = sb("ident", [P, P])
        headones = sb("headones", [P, P])
        causal = sb("causal", [P, P])
        headmask = sb("headmask", [P, H1])
        iota8 = sb("iota8", [P, E1])
        onesrow = sb("onesrow", [1, 512])
        wq = sb("wq", [P, NHEAD * DH])
        wkv = sb("wkv", [P, 2 * NHEAD * DH])
        wo = sb("wo", [P, NC, D])
        mu = sb("mu", [P, 2, NC])
        gate0 = sb("gate0", [P, E0])
        gate1 = sb("gate1", [P, E1])
        rowvec = sb("rowvec", [P, 6, D])
        w1q = sb("w1q", [P, D])
        w1k = sb("w1k", [P, D])
        w1v = sb("w1v", [P, D])
        w1o = sb("w1o", [P, D])
        b1q = sb("b1q", [P, 1])
        b1k = sb("b1k", [P, 1])
        bvob2 = sb("bvob2", [1, 3, D])
        wf1 = sb("wf1", [P, FF])
        bf1 = sb("bf1", [P, FF // P])
        wf2 = sb("wf2", [P, FF // P, D])
        ring = sb("ring", [P, RING, TOKW])
        tail = ring[0:GR, GT % RING, :]
        H = sb("H", [P, NT, D])
        Y = sb("Y", [P, NT, D])
        XN = sb("XN", [P, NT, D])
        stats = sb("stats", [P, NT, 6])
        mv = sb("mv", [P, NT, 2])
        var_eps = sb("var_eps", [P, NT])
        neg_half = sb("neg_half", [P, NT])
        rstd = sb("rstd", [P, NT])
        over = ring[:].rearrange("p j n -> p (j n)")
        FT = over[:, 0:4 * ROWS].rearrange("p (f r) -> p f r", r=ROWS)
        eq = over[:, 4 * ROWS:6 * ROWS].rearrange("p (j r) -> p j r", r=ROWS)
        rq = over[:, 6 * ROWS:8 * ROWS].rearrange("p (j r) -> p j r", r=ROWS)
        QT = over[:, 8 * ROWS:9 * ROWS]
        KT = over[:, 9 * ROWS:10 * ROWS]
        HT = over[:, 10 * ROWS:11 * ROWS]
        HN = over[:, 11 * ROWS:12 * ROWS].rearrange("p (t d) -> p t d", d=D)
        X1 = over[:, 12 * ROWS:13 * ROWS].rearrange("p (t d) -> p t d", d=D)
        xs = [sb(f"xs{u}", [P, D]) for u in range(2)]
        hT = [sb(f"hT{u}", [P, P]) for u in range(2)]
        LQ = [[sb(f"LQ{u}{n2}", [P, 2, NC, P]) for n2 in range(2)] for u in range(2)]
        RK = [[sb(f"RK{u}{n2}", [P, NC, P]) for n2 in range(2)] for u in range(2)]
        ksq = [sb(f"ksq{u}", [P, NC, P]) for u in range(2)]
        vt = [sb(f"vt{u}", [P, NHEAD * DH]) for u in range(2)]
        z1 = [sb(f"z1{u}", [P, NHEAD, S]) for u in range(2)]
        sc = [sb(f"sc{u}", [P, NHEAD, S]) for u in range(2)]
        pT = [sb(f"pT{u}", [P, NC, P]) for u in range(2)]
        vecT = [sb(f"vecT{u}", [P, NC, 2, S]) for u in range(2)]
        rmin = [sb(f"rmin{u}", [P, NHEAD]) for u in range(2)]
        rsum = [sb(f"rsum{u}", [P, NHEAD]) for u in range(2)]
        XT = sb("XT", [P, ROWS])
        XTh = sb("XTh", [P, ROWS], F32R)
        XTl = sb("XTl", [P, ROWS], F32R)
        few = [sb(f"few{u}", [P, FEW]) for u in range(SLOTS)]
        fewh13 = [sb(f"fewh13{u}", [P, 2 * P], F32R) for u in range(2)]
        fewl13 = [sb(f"fewl13{u}", [P, 2 * P], F32R) for u in range(2)]
        fewh2 = [sb(f"fewh2{u}", [P, P], F32R) for u in range(2)]
        fewl2 = [sb(f"fewl2{u}", [P, P], F32R) for u in range(2)]
        comb_b = [over[:, u * ROWS:(u + 1) * ROWS] for u in range(SLOTS)]
        act_s = [sb(f"act_s{u}", [P, 512]) for u in range(2)]
        act_g = [sb(f"act_g{u}", [P, 512]) for u in range(2)]
        hid = [sb(f"hid{u}", [P, 512]) for u in range(2)]
        hidh = [sb(f"hidh{u}", [P, 512], F32R) for u in range(4)]
        hidl = [sb(f"hidl{u}", [P, 512], F32R) for u in range(4)]
        lg = sb("lg", [P, NT, E0])
        lgr = sb("lgr", [P, NT, E0])
        comb = sb("comb", [P, NT, E0])
        combT = sb("combT", [E0, ROWS])
        mx = sb("mx", [P, NT, 8])
        mxi = sb("mxi", [P, NT, 8], U32)
        rs8 = sb("rs8", [P, NT])
        HN2 = HN
        VA = sb("VA", [P, NT, H1, DH1 + 1])
        qbd = [LQ[u][0][:].rearrange("p a c r -> p (a c) r") for u in range(2)]
        am = [LQ[u][1][:].rearrange("p a c r -> p (a c) r") for u in range(2)]
        den = sb("den", [P, NT, H1])
        rden = sb("rden", [P, NT, H1])
        AO = XN
        bias0, bias1 = (LQ[u][0][0:1, :, :, :].rearrange("p a c r -> p (a c r)") for u in range(2))

        consts = [
            (onesrow[:], a["onesrow"]),
            (bias0, a["tok_bias_row"][:, 0:B * D // 2]), (bias1, a["tok_bias_row"][:, B * D // 2:]),
            (ident[:], a["ident"]), (headones[:], a["headones"]),
            (wq[:], a["L0_attn_Wq"]), (wkv[:], a["L0_attn_Wkv"]),
            (wo[:], a["L0_attn_Wo"].rearrange("(c p) d -> p c d", p=P)),
            (mu[:].rearrange("p c k -> p (c k)"), a["mu_cols"]),
            (gate0[:], a["gate0T"]), (gate1[:], a["gate1T"]),
            (causal[:], a["causal"]), (headmask[:], a["headmask"]), (iota8[:], a["iota8"]),
            (w1q[:], a["L1_attn_Wq"]), (w1k[:], a["L1_attn_Wk"]), (w1v[:], a["L1_attn_Wv"]),
            (w1o[:], a["L1_attn_Wo"]), (b1q[:], a["L1_attn_bq"]), (b1k[:], a["L1_attn_bk"]),
            (bvob2[:, 0, :], a["L1_attn_bv"]), (bvob2[:, 1, :], a["L1_attn_bo"]),
            (bvob2[:, 2, :], a["L1_attn_b2"]),
            (wf1[:], a["L1_attn_W1"]), (bf1[:], a["b1_cols"]),
            (wf2[:], a["L1_attn_W2"].rearrange("(c p) d -> p c d", p=P)),
        ] + [(rowvec[:, n, :], a[name].partition_broadcast(P)) for n, name in enumerate(
            ["L0_attn_gamma", "L0_attn_beta", "L1_attn_ln1_g", "L1_attn_ln1_b", "L1_attn_ln2_g", "L1_attn_ln2_b"])]
        N_FIRST = 3
        N_CONSTS = 16 * (len(consts) - N_FIRST)

        names = """first_loaded const_loaded tail_loaded tok_masked tok_used tok_done h0_ready fill_done ones_filled xn_ready
            var_ready rstd_ready dve_step
            xs_ready xT_done hT_ready q_done q_read k_done k_read v_done v_read qsq_ready x_done
            z1_read m_done e_ready p_exp p_ready pT_done pT_ready pv_done vec0_ready vec1_ready wo_done y_ready
            norm_ready tr_done tr_copied xth_ready xtl_ready logits_done logits_copied
            lmax_sub lexp comb_ready combT_done combT_copied comb_stored ht_done ht_copied
            few_loaded0 few_loaded1 few_loaded2 few_loaded3 row_loaded0 row_loaded1 row_loaded2 row_loaded3 w13h_ready w13l_ready w2h_ready w2l_ready
            h1_done h_done act_ready gated_ready hid_ready hidh_ready hidl_ready y_done g_ready
            qk1_done erq_ready qk_ready v1_done va_ready qbd_ready at_done am_ready
            num_done ao_ready wo1_done x2_ready ff1_done ft_ready ff2_done
            out_ready out_stored""".split()
        s = {n: sem(n) for n in names}
        tok_loaded = [sem(f"tok_loaded{j}") for j in range(RING)]

        W1 = IS_CHUNKS + E0
        WS = W1 + E1 * C1
        WEND = WS + C1

        def wait(eng, name, value):
            if not isinstance(value, int) or value > 0:
                eng.wait_ge(s[name], value)

        def steps(eng, step):
            def peeled(t):
                step(t, t % 2, lambda d: 0 <= t + d < NT)
            for t in range(-2, 2):
                peeled(t)
            with eng.Fori(1, NT // 2 - 1) as i:
                for u in range(2):
                    step(2 * i + u, u, lambda d: True)
            for t in range(NT - 2, NT + 1):
                peeled(t)

        def chunks(eng, body, layer):
            first, end = ((0, W1), (W1, WEND))[layer]
            loop0 = -(-(first + IS_CHUNKS + 1) // SLOTS)
            loop1 = (W1 if layer == 0 else WS) // SLOTS
            for w in range(first, SLOTS * loop0):
                body(w, w // SLOTS, w % SLOTS, min(w - first, 2))
            with eng.Fori(loop0, loop1) as i:
                for u in range(SLOTS):
                    body(SLOTS * i + u, i, u, 2)
            for w in range(SLOTS * loop1, end):
                body(w, w // SLOTS, w % SLOTS, 2)

        def is_last(w):
            return isinstance(w, int) and w + 1 in (W1, WEND)

        def is_gelu(w):
            return isinstance(w, int) and w >= WS

        block = ctx.enter_context(nc.Block())

        @block.sync
        def _(sp):
            def load_tile(k, j):
                sp.dma_start(ring[:, j, :], a["tok_main"][bass.ds(k, 1), :, :].rearrange("t p n -> (t p) n")
                             ).then_inc(tok_loaded[j], 16)

            for j in range(RING):
                load_tile(j, j)
            with sp.Fori(1, GT // RING) as r:
                for j in range(RING):
                    sp.wait_ge(s["tok_used"], RING * (r - 1) + j + 1)
                    load_tile(r * RING + j, j)
            for j in range(GT % RING):
                k = GT // RING * RING + j
                sp.wait_ge(s["tok_used"], k - RING + 1)
                load_tile(k, j)
            sp.wait_ge(s["tok_used"], GT // RING * RING - RING + GT % RING + 1)
            sp.dma_start(tail, a["tok_tail"]).then_inc(s["tail_loaded"], 16)

            def load_chunk(w, i, u, age):
                layer = w_layer[0]
                few_dram, rows = (a["few0"], comb_rows0) if layer == 0 else (a["few1"], comb_rows1)
                base = 0 if layer == 0 else W1
                wait(sp, "w2l_ready", w - 3)
                sp.dma_start(few[u][:], few_dram[bass.ds(w - base, 1), :, :].rearrange("e p n -> (e p) n")
                             ).then_inc(s[f"few_loaded{u}"], 16)
                wait(sp, "gated_ready", 2 * (w - 3))
                if isinstance(w, int) and w == 0:
                    sp.wait_ge(s["tok_done"], 1)
                if isinstance(w, int) and (w < IS_CHUNKS or w >= WS):
                    row = a["ones_row"].partition_broadcast(P)
                else:
                    first = IS_CHUNKS if layer == 0 else W1
                    if isinstance(w, int) and w == first:
                        sp.wait_ge(s["combT_copied"], 2 * layer + 2)
                        sp.dma_start(rows, combT[0:rows.shape[0], :]).then_inc(s["comb_stored"], 16)
                        sp.wait_ge(s["comb_stored"], 16 * (layer + 1))
                    row = rows[bass.ds(w - first, 1), :].rearrange("a n -> (a n)").partition_broadcast(P)
                sp.dma_start(comb_b[u], row).then_inc(s[f"row_loaded{u}"], 16)

            w_layer = [0]
            chunks(sp, load_chunk, 0)
            w_layer[0] = 1
            chunks(sp, load_chunk, 1)

            o = out.rearrange("(t s) b d -> (s b) t d", s=P // B)
            for h in range(2):
                sp.wait_ge(s["out_ready"], h + 1)
                sp.dma_start(o[:, 4 * h:4 * h + 4, :], H[:, 4 * h:4 * h + 4, :]).then_inc(s["out_stored"], 16)
            sp.wait_ge(s["out_stored"], 32)

        @block.scalar
        def _(act):
            for n, (dst, src) in enumerate(consts):
                act.dma_start(dst, src).then_inc(s["first_loaded" if n < N_FIRST else "const_loaded"], 16)

            act.wait_ge(s["tok_done"], 1)
            for h in range(2):
                nc.scalar.copy(H[:, 4 * h:4 * h + 4, :], bank[h][:].rearrange("p (t d) -> p t d", d=D)
                               ).then_inc(s["h0_ready"], 1)

            def attention(t, u, has):
                v = 1 - u
                if has(1):
                    act.wait_ge(s["k_done"], t + 2)
                    wait(act, "x_done", 2 * t)
                    for n2 in range(2):
                        rows = slice(S * n2, S * n2 + S)
                        nc.scalar.mul(RK[v][n2][rows, :, :], bank[2][rows, :].rearrange("p (c r) -> p c r", c=NC), -2.0
                                      ).then_inc(s["k_read"], 1)
                    nc.scalar.activation(ksq[v][:], bank[2][:].rearrange("p (c r) -> p c r", c=NC), ACT.Square
                                         ).then_inc(s["k_read"], 1)
                if has(-1):
                    act.wait_ge(s["pT_done"], t)
                    wait(act, "pv_done", t - 2)
                    nc.scalar.copy(pT[v][:], bank[6][:].rearrange("p (c r) -> p c r", c=NC)).then_inc(s["pT_ready"], 1)
                if has(1):
                    act.wait_ge(s["q_read"], 4 * t + 8)
                    for n2 in range(2):
                        rows, other = slice(S * n2, S * n2 + S), slice(S * (1 - n2), S * (1 - n2) + S)
                        nc.scalar.activation(LQ[v][n2][other, :, :, :], LQ[v][n2][rows, :, :, :], ACT.Square
                                             ).then_inc(s["qsq_ready"], 1)
                if has(0):
                    act.wait_ge(s["x_done"], 2 * t + 2)
                    wait(act, "m_done", t - 1)
                    nc.scalar.mul(z1[u][:], bank[5][:].rearrange("p (n j) -> p n j", j=S), 1.5 * SCALE
                                  ).then_inc(s["z1_read"], 1)
                if has(-1):
                    act.wait_ge(s["pv_done"], t)
                    wait(act, "wo_done", t - 2)
                    nc.scalar.copy(vecT[v][:, :, 0, :], bank[6][:, 0:NC * S].rearrange("p (c i) -> p c i", c=NC)
                                   ).then_inc(s["vec0_ready"], 1)
                if has(1):
                    act.wait_ge(s["v_done"], t + 2)
                    wait(act, "pv_done", t)
                    nc.scalar.copy(vt[v][:], bank[3][:]).then_inc(s["v_read"], 1)
                if has(2):
                    act.wait_ge(s["xT_done"], t + 3)
                    wait(act, "v_done", t + 1)
                    nc.scalar.copy(hT[u][:], bank[0][:, 0:P]).then_inc(s["hT_ready"], 1)
                if has(0):
                    act.wait_ge(s["e_ready"], t + 1)
                    nc.scalar.activation(sc[u][:], sc[u][:], ACT.Exp, scale=-1.0).then_inc(s["p_exp"], 1)
            steps(act, attention)

            def copy_transposed(n, dst):
                for h in range(2):
                    act.wait_ge(s["tr_done"], 2 * n + h + 1)
                    nc.scalar.copy(dst(h), bank[h][:] if len(dst(h).shape) == 2 else
                                   bank[h][:].rearrange("p (t d) -> p t d", d=D)).then_inc(s["tr_copied"], 1)

            def XT_half(h):
                return XT[:, 512 * h:512 * h + 512]

            def x_high(layer, n):
                act.wait_ge(s["tr_copied"], 2 * n + 2)
                nc.scalar.copy(XTh[:], XT[:]).then_inc(s["xth_ready"], 1)

            def comb_transposed(layer, n):
                for h in range(2):
                    act.wait_ge(s["combT_done"], 2 * layer + h + 1)
                    nc.scalar.copy(combT[0:n, 512 * h:512 * h + 512], bank[h][0:n, :]).then_inc(s["combT_copied"], 1)

            def w13_high(w, i, u):
                act.wait_ge(s[f"few_loaded{u}"], 16 * (i + 1))
                wait(act, "h_done", 2 * (w - 1))
                wait(act, "w13l_ready", w - 1)
                nc.scalar.copy(fewh13[u % 2][:], few[u][:, 0:2 * P]).then_inc(s["w13h_ready"], 1)

            def w2_high(w, u):
                wait(act, "y_done", 2 * (w - 1))
                wait(act, "w2l_ready", w - 1)
                nc.scalar.copy(fewh2[u % 2][:], few[u][:, 2 * P:]).then_inc(s["w2h_ready"], 1)

            def activate(n, m, gelu):
                act.wait_ge(s["h_done" if gelu else "h1_done"], n + 1)
                wait(act, "gated_ready", n - 1)
                nc.scalar.activation(act_s[m % 2][:], bank[m % 2][:], ACT.Gelu if gelu else ACT.Silu
                                     ).then_inc(s["act_ready"], 1)

            def hidden_high(n, m):
                act.wait_ge(s["hid_ready"], n + 1)
                wait(act, "y_done", n - 3)
                nc.scalar.copy(hidh[m % 4][:], hid[m % 2][:]).then_inc(s["hidh_ready"], 1)

            def chunk(w, i, u, age):
                n = 2 * w
                if not is_last(w):
                    w13_high(w + 1, i + (u + 1) // SLOTS, (u + 1) % SLOTS)
                activate(n, 2 * u, is_gelu(w))
                if age:
                    hidden_high(n - 1, 2 * u - 1)
                activate(n + 1, 2 * u + 1, is_gelu(w))
                hidden_high(n, 2 * u)
                w2_high(w, u)
                if is_last(w):
                    hidden_high(n + 1, 2 * u + 1)

            copy_transposed(0, XT_half)
            x_high(0, 0)
            act.wait_ge(s["logits_done"], 1)
            nc.scalar.copy(lg[:], bank[2][:].rearrange("p (t e) -> p t e", e=E0)).then_inc(s["logits_copied"], 1)
            for h in range(2):
                act.wait_ge(s["ht_done"], h + 1)
                nc.scalar.copy(HT[:, 512 * h:512 * h + 512], bank[6 + h][:]).then_inc(s["ht_copied"], 1)
            act.wait_ge(s["lmax_sub"], 1)
            nc.scalar.activation(comb[:], comb[:], ACT.Exp).then_inc(s["lexp"], 1)
            comb_transposed(0, E0)
            w13_high(0, 0, 0)
            chunks(act, chunk, 0)

            copy_transposed(1, lambda h: H[:, 4 * h:4 * h + 4, :])
            copy_transposed(2, XT_half)
            for n in range(4):
                j, h = n // 2, n % 2
                act.wait_ge(s["qk1_done"], n + 1)
                bias = (b1q, b1k)[j][:, 0:1]
                cols = slice(512 * h, 512 * h + 512)
                nc.scalar.activation(eq[:, j, cols], bank[2 + n][:], ACT.Exp, bias=bias).then_inc(s["erq_ready"], 1)
                nc.scalar.activation(rq[:, j, cols], bank[2 + n][:], ACT.Relu, bias=bias).then_inc(s["erq_ready"], 1)
            for h in range(2):
                act.wait_ge(s["v1_done"], h + 1)
                act.wait_ge(s["fill_done"], 1)
                nc.scalar.copy(VA[:, 4 * h:4 * h + 4, :, 0:DH1].rearrange("p t h d -> p (t h) d"),
                               bank[6 + h][:].rearrange("p (t d) -> p t d", d=DH1)).then_inc(s["va_ready"], 1)
            copy_transposed(3, XT_half)
            copy_transposed(4, XT_half)
            for n in range(2 * (FF // P)):
                f, h = n // 2, n % 2
                act.wait_ge(s["ff1_done"], n + 1)
                nc.scalar.activation(FT[:, f, 512 * h:512 * h + 512], bank[2 + n % 4][:], ACT.Relu,
                                     bias=bf1[:, f:f + 1]).then_inc(s["ft_ready"], 1)

            copy_transposed(5, XT_half)
            x_high(1, 5)
            act.wait_ge(s["logits_done"], 2)
            nc.scalar.copy(lg[:, :, 0:E1], bank[2][:, 0:NT * E1].rearrange("p (t e) -> p t e", e=E1)
                           ).then_inc(s["logits_copied"], 1)
            comb_transposed(1, E1 * C1)
            w13_high(W1, W1 // SLOTS, W1 % SLOTS)
            chunks(act, chunk, 1)

        @block.gpsimd
        def _(pool):
            pool.memset(neg_half[:], -0.5).then_inc(s["fill_done"], 1)

            def root(k):
                pool.wait_ge(s["var_ready"], k)
                pool.wait_ge(s["fill_done"], 1)
                pool.tensor_tensor(rstd[:], var_eps[:], neg_half[:], ALU.pow).then_inc(s["rstd_ready"], 1)

            def attention(t, u, has):
                if has(2):
                    wait(pool, "xT_done", t + 1)
                    pool.tensor_copy(xs[u][:], XN[:, bass.ds(t + 2, 1), :].rearrange("p a d -> p (a d)")
                                     ).then_inc(s["xs_ready"], 1)

            def chunk(w, i, u, age):
                pool.wait_ge(s[f"row_loaded{u}"], 16 * (i + 1))
                for h in range(2):
                    n = 2 * w + h
                    pool.wait_ge(s["act_ready"], n + 1)
                    wait(pool, "hid_ready", n - 1)
                    pool.tensor_tensor(act_g[h][:], act_s[h][:], comb_b[u][:, 512 * h:512 * h + 512], ALU.mult
                                       ).then_inc(s["gated_ready"], 1)

            root(1)
            pool.wait_ge(s["xn_ready"], 1)
            steps(pool, attention)
            root(2)
            root(3)
            chunks(pool, chunk, 0)
            root(4)
            root(5)
            for T in range(NT):
                pool.wait_ge(s["qk_ready"], 4)
                wait(pool, "at_done", 2 * (T - 1))
                pool.tensor_tensor(qbd[T % 2], QT[:, P * T:P * T + P].unsqueeze(1).broadcast_to([P, H1, P]),
                                   headmask[:].unsqueeze(2).broadcast_to([P, H1, P]), ALU.mult
                                   ).then_inc(s["qbd_ready"], 1)
            root(6)
            root(7)
            chunks(pool, chunk, 1)

        @block.vector
        def _(dve):
            class Chain:
                base, n = 0, 0

                def __call__(self, ins):
                    self.n += 1
                    ins.then_inc(s["dve_step"], 1)

                def sync(self):
                    dve.wait_ge(s["dve_step"], self.base + self.n)

                def link(self, ins):
                    self(ins)
                    self.sync()
            chain = Chain()

            def stats_of(src, k):
                for T in range(NT):
                    chain(dve.bn_stats(stats[:, T, :], src[:, T, :]))
                chain.sync()
                for T in range(NT):
                    chain(dve.bn_aggr(mv[:, T, :], stats[:, T, :]))
                chain.sync()
                dve.tensor_scalar(var_eps[:], mv[:, :, 1], EPS, None, ALU.add).then_inc(s["var_ready"], 1)
                dve.wait_ge(s["rstd_ready"], k)

            def normalised(dst, src, signal=None):
                for T in range(NT):
                    ins = dve.tensor_scalar(dst[:, T, :], src[:, T, :], mv[:, T, 0:1], rstd[:, T:T + 1],
                                            ALU.subtract, ALU.mult)
                    if signal and T == NT - 1:
                        ins.then_inc(s[signal], 1)
                    else:
                        chain(ins)
                if not signal:
                    chain.sync()

            def vec(n):
                return rowvec[:, n, :].unsqueeze(1).broadcast_to([P, NT, D])

            def mask(rows, slot_ap):
                w = slot_ap[:, 0:B * D].rearrange("p (b d) -> p b d", d=D)
                m = slot_ap[:, B * D + S:].unsqueeze(1).broadcast_to([rows, B, D])
                dve.tensor_tensor(w, w, m, ALU.mult).then_inc(s["tok_masked"], 1)

            dve.memset(VA[:].rearrange("p t h d -> p (t h d)"), 1.0).then_inc(s["dve_step"], 1)
            chain.n = 1
            for u in range(2):
                for n2 in range(2):
                    other = slice(S * (1 - n2), S * (1 - n2) + S)
                    dve.memset(RK[u][n2][other, :, :], 1.0).then_inc(s["ones_filled"], 1)
            with dve.Fori(0, GT // RING) as r:
                for j in range(RING):
                    dve.wait_ge(tok_loaded[j], 16 * (r + 1))
                    mask(P, ring[:, j, :])
            for j in range(GT % RING):
                dve.wait_ge(tok_loaded[j], 16 * (GT // RING + 1))
                mask(P, ring[:, j, :])
            dve.wait_ge(s["tail_loaded"], 16)
            mask(GR, tail)

            dve.wait_ge(s["h0_ready"], 2)
            stats_of(H, 1)
            normalised(XN, H, "xn_ready")
            dve.wait_ge(s["const_loaded"], N_CONSTS)
            dve.wait_ge(s["xn_ready"], 1)

            before = chain.n

            def attention(t, u, has):
                v = 1 - u
                chain.base, chain.n = before + 4 * t, 0
                if has(1):
                    dve.wait_ge(s["q_done"], t + 2)
                    wait(dve, "x_done", 2 * t)
                    for n2 in range(2):
                        rows = slice(S * n2, S * n2 + S)
                        for c in range(2):
                            dve.tensor_tensor(LQ[v][n2][rows, c, :, :],
                                              bank[1][rows, :].rearrange("p (c r) -> p c r", c=NC),
                                              mu[rows, c, :].unsqueeze(2).broadcast_to([S, NC, P]), ALU.add
                                              ).then_inc(s["q_read"], 1)
                if has(-1):
                    dve.wait_ge(s["pv_done"], t)
                    wait(dve, "wo_done", t - 2)
                    dve.tensor_copy(vecT[v][:, :, 1, :], bank[7][:, 0:NC * S].rearrange("p (c i) -> p c i", c=NC)
                                    ).then_inc(s["vec1_ready"], 1)
                if has(0):
                    dve.wait_ge(s["z1_read"], t + 1)
                    wait(dve, "pT_done", t - 1)
                    dve.scalar_tensor_tensor(out=sc[u][:], in0=bank[4][:].rearrange("p (n j) -> p n j", j=S),
                                             scalar=0.5 * SCALE, in1=z1[u][:], op0=ALU.mult, op1=ALU.min
                                             ).then_inc(s["m_done"], 1)
                    dve.wait_ge(s["m_done"], t + 1)
                    chain.link(dve.tensor_reduce(rmin[u][:], sc[u][:], AX.X, ALU.min))
                    chain.link(dve.tensor_scalar(rmin[u][:], rmin[u][:], 0.0, None, ALU.max))
                    dve.scalar_tensor_tensor(out=sc[u][:], in0=sc[u][:], scalar=0.0,
                                             in1=rmin[u][:].unsqueeze(2).broadcast_to([P, 2 * NC, S]),
                                             op0=ALU.max, op1=ALU.subtract).then_inc(s["e_ready"], 1)
                if has(-1):
                    dve.wait_ge(s["wo_done"], t)
                    dve.tensor_tensor(Y[:, bass.ds(t - 1, 1), :].rearrange("p a d -> p (a d)"), bank[7][:, 2 * P:3 * P],
                                      XN[:, bass.ds(t - 1, 1), :].rearrange("p a d -> p (a d)"), ALU.add
                                      ).then_inc(s["y_ready"], 1)
                if has(0):
                    dve.wait_ge(s["p_exp"], t + 1)
                    chain.link(dve.tensor_reduce(rsum[u][:], sc[u][:], AX.X, ALU.add))
                    chain.link(dve.reciprocal(rsum[u][:], rsum[u][:]))
                    dve.tensor_tensor(sc[u][:], sc[u][:], rsum[u][:].unsqueeze(2).broadcast_to([P, 2 * NC, S]),
                                      ALU.mult).then_inc(s["p_ready"], 1)
                    assert chain.n == 4
            steps(dve, attention)
            chain.base, chain.n = 0, before + 4 * NT

            dve.wait_ge(s["y_ready"], NT)
            stats_of(Y, 2)
            normalised(XN, Y)
            chain.link(dve.tensor_tensor(XN[:], XN[:], vec(0), ALU.mult))
            chain.link(dve.tensor_tensor(XN[:], XN[:], vec(1), ALU.add))
            chain.link(dve.tensor_tensor(H[:], H[:], XN[:], ALU.add))

            stats_of(H, 3)
            normalised(XN, H, "norm_ready")

            def x_low(layer):
                dve.wait_ge(s["xth_ready"], layer + 1)
                dve.tensor_tensor(XTl[:], XT[:], XTh[:].bitcast(F32), ALU.subtract).then_inc(s["xtl_ready"], 1)

            x_low(0)
            dve.wait_ge(s["logits_copied"], 1)
            for T in range(NT):
                chain(dve.max(mx[:, T, :], lg[:, T, :]))
            chain.sync()
            dve.tensor_tensor(comb[:], lg[:], mx[:, :, 0:1].broadcast_to([P, NT, E0]), ALU.subtract
                              ).then_inc(s["lmax_sub"], 1)
            TAKEN = -3.0e38
            for T in range(NT):
                chain(dve.match_replace(lgr[:, T, :], mx[:, T, :], lg[:, T, :], TAKEN))
            chain.sync()
            chain.link(dve.tensor_scalar(lgr[:], lgr[:], TAKEN, None, ALU.is_equal))
            dve.wait_ge(s["lexp"], 1)
            chain.link(dve.tensor_tensor(comb[:], comb[:], lgr[:], ALU.mult))
            chain.link(dve.tensor_reduce(rs8[:], comb[:], AX.X, ALU.add))
            chain.link(dve.reciprocal(rs8[:], rs8[:]))
            dve.tensor_tensor(comb[:], comb[:], rs8[:].unsqueeze(2).broadcast_to([P, NT, E0]), ALU.mult
                              ).then_inc(s["comb_ready"], 1)

            def w13_low(w, u):
                dve.wait_ge(s["w13h_ready"], w + 1)
                dve.tensor_tensor(fewl13[u % 2][:], few[u][:, 0:2 * P], fewh13[u % 2][:].bitcast(F32), ALU.subtract
                                  ).then_inc(s["w13l_ready"], 1)

            def w2_low(w, u):
                dve.wait_ge(s["w2h_ready"], w + 1)
                dve.tensor_tensor(fewl2[u % 2][:], few[u][:, 2 * P:], fewh2[u % 2][:].bitcast(F32), ALU.subtract
                                  ).then_inc(s["w2l_ready"], 1)

            def hidden(n, m, gelu):
                dve.wait_ge(s["gated_ready"], n + 1)
                dve.wait_ge(s["h_done"], n + 1)
                wait(dve, "hidh_ready", n - 1)
                wait(dve, "hidl_ready", n - 1)
                if gelu:
                    dve.tensor_copy(hid[m % 2][:], act_g[m % 2][:]).then_inc(s["hid_ready"], 1)
                else:
                    dve.tensor_tensor(hid[m % 2][:], bank[2 + m % 2][:], act_g[m % 2][:], ALU.mult
                                      ).then_inc(s["hid_ready"], 1)

            def hidden_low(n, m):
                dve.wait_ge(s["hidh_ready"], n + 1)
                dve.tensor_tensor(hidl[m % 4][:], hid[m % 2][:], hidh[m % 4][:].bitcast(F32), ALU.subtract
                                  ).then_inc(s["hidl_ready"], 1)

            def chunk(w, i, u, age):
                n = 2 * w
                if not is_last(w):
                    w13_low(w + 1, (u + 1) % SLOTS)
                hidden(n, 2 * u, is_gelu(w))
                if age:
                    hidden_low(n - 1, 2 * u - 1)
                hidden(n + 1, 2 * u + 1, is_gelu(w))
                hidden_low(n, 2 * u)
                w2_low(w, u)
                if is_last(w):
                    hidden_low(n + 1, 2 * u + 1)

            w13_low(0, 0)
            chunks(dve, chunk, 0)

            dve.wait_ge(s["ht_copied"], 2)
            dve.wait_ge(s["y_done"], 2 * W1)
            for h in range(2):
                dve.tensor_tensor(XT[:].rearrange("p (s b) -> p b s", b=B)[:, 8 * h:8 * h + 8, :],
                                  HT[:, 512 * h:512 * h + 512].rearrange("p (b s) -> p b s", s=S),
                                  bank[4 + h][:].rearrange("p (b s) -> p b s", s=S), ALU.add
                                  ).then_inc(s["g_ready"], 1)
            dve.wait_ge(s["tr_copied"], 4)
            stats_of(H, 4)
            normalised(X1, H)
            stats_of(X1, 5)
            normalised(HN, X1)
            chain.link(dve.tensor_tensor(HN, HN, vec(2), ALU.mult))
            dve.tensor_tensor(HN, HN, vec(3), ALU.add).then_inc(s["norm_ready"], 1)
            for n in range(4):
                j, h = n // 2, n % 2
                cols = slice(512 * h, 512 * h + 512)
                dve.wait_ge(s["erq_ready"], 2 * n + 2)
                dve.scalar_tensor_tensor(out=(QT, KT)[j][:, cols], in0=eq[:, j, cols], scalar=1.0,
                                         in1=rq[:, j, cols], op0=ALU.min, op1=ALU.add).then_inc(s["qk_ready"], 1)

            def causal_scores(T):
                wait(dve, "num_done", T - 1)
                for q in range(2):
                    dve.wait_ge(s["at_done"], 2 * T + q + 1)
                    dve.tensor_tensor(am[T % 2][:, 4 * q:4 * q + 4, :],
                                      bank[2 * (T % 2) + q][:].rearrange("p (h r) -> p h r", h=4),
                                      causal[:].unsqueeze(1).broadcast_to([P, 4, P]), ALU.mult
                                      ).then_inc(s["am_ready"], 1)

            def divided(T):
                dve.wait_ge(s["num_done"], T + 1)
                o = bank[4 + T % 2][:, 0:H1 * (DH1 + 1)].rearrange("p (h d) -> p h d", h=H1)
                chain.link(dve.tensor_scalar(den[:, T, :], o[:, :, DH1], DEN_MIN, None, ALU.max))
                chain.link(dve.reciprocal(rden[:, T, :], den[:, T, :]))
                dve.tensor_tensor(AO[:, T, :].rearrange("p (h d) -> p h d", h=H1), o[:, :, 0:DH1],
                                  rden[:, T, :].unsqueeze(2).broadcast_to([P, H1, DH1]), ALU.mult
                                  ).then_inc(s["ao_ready"], 1)

            causal_scores(0)
            for T in range(NT):
                if T + 1 < NT:
                    causal_scores(T + 1)
                divided(T)
            for h in range(2):
                dve.wait_ge(s["wo1_done"], h + 1)
                chain(dve.tensor_tensor(Y[:, 4 * h:4 * h + 4, :], X1[:, 4 * h:4 * h + 4, :],
                                        bank[h][:].rearrange("p (t d) -> p t d", d=D), ALU.add))
            chain.sync()
            stats_of(Y, 6)
            normalised(HN2, Y)
            chain.link(dve.tensor_tensor(HN2, HN2, vec(4), ALU.mult))
            dve.tensor_tensor(HN2, HN2, vec(5), ALU.add).then_inc(s["norm_ready"], 1)
            chain.link(dve.tensor_tensor(H[:], H[:], Y[:], ALU.add))
            for h in range(2):
                dve.wait_ge(s["ff2_done"], h + 1)
                chain(dve.tensor_tensor(H[:, 4 * h:4 * h + 4, :], H[:, 4 * h:4 * h + 4, :],
                                        bank[6 + h][:].rearrange("p (t d) -> p t d", d=D), ALU.add))
            chain.sync()

            stats_of(H, 7)
            normalised(XN, H, "norm_ready")
            x_low(1)
            dve.wait_ge(s["logits_copied"], 2)
            for T in range(NT):
                chain(dve.max(mx[:, T, :], lg[:, T, 0:E1]))
            chain.sync()
            for T in range(NT):
                chain(dve.max_index(mxi[:, T, :], mx[:, T, :], lg[:, T, 0:E1]))
            chain.sync()
            chain.link(dve.tensor_copy(rs8[:], mxi[:, :, 0]))
            chain.link(dve.tensor_tensor(lgr[:, :, 0:E1], iota8[:].unsqueeze(1).broadcast_to([P, NT, E1]),
                                         rs8[:].unsqueeze(2).broadcast_to([P, NT, E1]), ALU.is_equal))
            for c in range(C1):
                ins = dve.tensor_copy(comb[:, :, 0:E1 * C1].rearrange("p t (e c) -> p t e c", c=C1)[:, :, :, c],
                                      lgr[:, :, 0:E1])
            ins.then_inc(s["comb_ready"], 1)
            w13_low(W1, W1 % SLOTS)
            chunks(dve, chunk, 1)
            dve.wait_ge(s["y_done"], 2 * WEND)
            for h in range(2):
                dve.tensor_copy(HT[:, 512 * h:512 * h + 512], bank[4 + h][:]).then_inc(s["g_ready"], 1)
            for h in range(2):
                dve.wait_ge(s["tr_done"], 2 * 6 + h + 1)
                dve.tensor_tensor(H[:, 4 * h:4 * h + 4, :], H[:, 4 * h:4 * h + 4, :],
                                  bank[h][:].rearrange("p (t d) -> p t d", d=D), ALU.add).then_inc(s["out_ready"], 1)

        @block.tensor
        def _(pe):
            def tok_product(src, h, b2, **flags):
                return pe.matmul(bank[h][S * b2:S * b2 + S, :], src[:, B * D:B * D + S],
                                 src[:, 1024 * b2 + 512 * h:1024 * b2 + 512 * h + 512], **flags)

            def tile_products(src, signal, stop=False):
                for h in range(2):
                    for b2 in range(2):
                        mm = tok_product(src, h, b2, start=False, stop=stop)
                mm.then_inc(s[signal], 1)

            pe.wait_ge(s["first_loaded"], 16 * N_FIRST)
            for h in range(2):
                for b2 in range(2):
                    pe.matmul(bank[h][S * b2:S * b2 + S, :], onesrow[:, 0:S],
                              (bias0, bias1)[b2][:, 512 * h:512 * h + 512], start=True, stop=False)
            with pe.Fori(0, GT // RING) as r:
                for j in range(RING):
                    pe.wait_ge(s["tok_masked"], RING * r + j + 1)
                    tile_products(ring[:, j, :], "tok_used")
            for j in range(GT % RING):
                pe.wait_ge(s["tok_masked"], GT // RING * RING + j + 1)
                tile_products(ring[:, j, :], "tok_used")
            pe.wait_ge(s["tok_masked"], GT + 1)
            tile_products(tail, "tok_done", stop=True)

            def wait_apart():
                pe.wait_ge(s["const_loaded"], N_CONSTS)

            def distances(u, m):
                for c in range(NC):
                    for b2 in range(2):
                        for n2 in range(2):
                            mm = pe.matmul(bank[4 + m][S * n2:S * n2 + S, S * (2 * c + b2):S * (2 * c + b2) + S],
                                           LQ[u][n2][:, m, c, S * b2:S * b2 + S], RK[u][n2][:, c, S * b2:S * b2 + S],
                                           start=False, stop=True, skip_group_check=True)
                mm.then_inc(s["x_done"], 1)

            def attention(t, u, has):
                v = 1 - u
                if has(0):
                    pe.wait_ge(s["k_read"], 3 * t + 3)
                    wait(pe, "m_done", t)
                    wait(pe, "z1_read", t)
                    for m in range(2):
                        pe.matmul(bank[4 + m][:], headones[:], ksq[u][:].rearrange("p c r -> p (c r)"),
                                  start=True, stop=True)
                if has(1):
                    pe.wait_ge(s["hT_ready"], t + 2)
                    wait(pe, "q_read", 4 * t + 4)
                    for c in range(NC):
                        mm = pe.matmul(bank[1][:, P * c:P * c + P], wq[:, P * c:P * c + P], hT[v][:],
                                       start=True, stop=True)
                    mm.then_inc(s["q_done"], 1)
                    wait(pe, "k_read", 3 * t + 3)
                    for c in range(NC):
                        mm = pe.matmul(bank[2][:, P * c:P * c + P], wkv[:, P * c:P * c + P], hT[v][:],
                                       start=True, stop=True)
                    mm.then_inc(s["k_done"], 1)
                if has(0):
                    pe.wait_ge(s["qsq_ready"], 2 * t + 2)
                    distances(u, 0)
                if has(-1):
                    pe.wait_ge(s["p_ready"], t)
                    wait(pe, "vec0_ready", t - 1)
                    for c in range(NC):
                        mm = pe.transpose(bank[6][:, P * c:P * c + P], sc[v][:, 2 * c:2 * c + 2, :].rearrange(
                            "p n j -> p (n j)"), ident[:])
                    mm.then_inc(s["pT_done"], 1)
                if has(0):
                    distances(u, 1)
                if has(-1):
                    wait_apart()
                    pe.wait_ge(s["pT_ready"], t)
                    pe.wait_ge(s["v_read"], t)
                    wait(pe, "y_ready", t - 1)
                    for c in range(NC):
                        for n2 in range(2):
                            for b2 in range(2):
                                rows = slice(S * b2, S * b2 + S)
                                mm = pe.matmul(bank[6 + b2][S * n2:S * n2 + S, S * c:S * c + S],
                                               vt[v][rows, DH * (2 * c + n2):DH * (2 * c + n2) + DH],
                                               pT[v][rows, c, S * n2:S * n2 + S], start=True, stop=True)
                    mm.then_inc(s["pv_done"], 1)
                if has(1):
                    wait(pe, "v_read", t + 1)
                    pe.matmul(bank[3][:], hT[v][:], wkv[:, NHEAD * DH:], start=True, stop=True
                              ).then_inc(s["v_done"], 1)
                if has(2):
                    pe.wait_ge(s["xs_ready"], t + 3)
                    wait(pe, "hT_ready", t + 2)
                    pe.transpose(bank[0][:, 0:P], xs[u][:], ident[:]).then_inc(s["xT_done"], 1)
                if has(-1):
                    pe.wait_ge(s["vec0_ready"], t)
                    pe.wait_ge(s["vec1_ready"], t)
                    for c in range(NC):
                        mm = pe.matmul(bank[7][:, 2 * P:3 * P], vecT[v][:, c, :, :].rearrange("p b i -> p (b i)"),
                                       wo[:, c, :], start=(c == 0), stop=(c == NC - 1))
                    mm.then_inc(s["wo_done"], 1)
            pe.wait_ge(s["const_loaded"], N_CONSTS)
            pe.wait_ge(s["ones_filled"], 4)
            steps(pe, attention)

            def transposed(src_tile, first_bank, signal):
                for T in range(NT):
                    tr = pe.transpose(bank[first_bank + T // 4][:, P * (T % 4):P * (T % 4) + P], src_tile(T), ident[:])
                    if T % 4 == 3:
                        tr.then_inc(s[signal], 1)

            pe.wait_ge(s["norm_ready"], 1)
            transposed(lambda T: XN[:, T, :], 0, "tr_done")
            transposed(lambda T: H[:, T, :], 6, "ht_done")

            def logits(gate, e):
                for T in range(NT):
                    mm = pe.matmul(bank[2][:, e * T:e * T + e], XT[:, P * T:P * T + P], gate[:], start=True, stop=True)
                mm.then_inc(s["logits_done"], 1)

            def comb_transposed(e, layer):
                pe.wait_ge(s["comb_ready"], layer + 1)
                for T in range(NT):
                    mm = pe.matmul(bank[T // 4][0:e, P * (T % 4):P * (T % 4) + P], comb[:, T, 0:e], ident[:],
                                   start=True, stop=True)
                    if T % 4 == 3:
                        mm.then_inc(s["combT_done"], 1)

            def three(dst, high, low, x_high, x_low, start, stop):
                pe.matmul(dst, high, x_high, start=start, stop=False)
                pe.matmul(dst, high, x_low, start=False, stop=False)
                return pe.matmul(dst, low, x_high, start=False, stop=stop)

            def units_in(w, n, m, u, h):
                cols = slice(512 * h, 512 * h + 512)
                wait(pe, "act_ready", n - 1)
                for j in range(1 if is_gelu(w) else 2):
                    if j == 1:
                        wait(pe, "hid_ready", n - 1)
                    c = slice(P * j, P * j + P)
                    mm = three(bank[2 * j + m % 2][:], fewh13[u % 2][:, c], fewl13[u % 2][:, c], XTh[:, cols], XTl[:, cols],
                               True, True)
                    if is_gelu(w) or j == 1:
                        mm.then_inc(s["h_done"], 1)
                    else:
                        mm.then_inc(s["h1_done"], 1)

            def unit_out(w, n, m, first, last):
                pe.wait_ge(s["hidl_ready"], n + 1)
                pe.wait_ge(s["w2l_ready"], w + 1)
                u = m // 2
                three(bank[4 + m % 2][:], fewh2[u % 2][:], fewl2[u % 2][:], hidh[m % 4][:], hidl[m % 4][:], first, last
                      ).then_inc(s["y_done"], 1)

            def chunk(w, i, u, age):
                n, m = 2 * w, 2 * u
                pe.wait_ge(s["w13l_ready"], w + 1)
                units_in(w, n, m, u, 0)
                if age == 2:
                    unit_out(w - 2, n - 3, m - 3, isinstance(w, int) and w in (2, W1 + 2), False)
                units_in(w, n + 1, m + 1, u, 1)
                if age:
                    unit_out(w - 1, n - 2, m - 2, age == 1, False)
                if is_last(w):
                    unit_out(w - 1, n - 1, m - 1, False, False)
                    unit_out(w, n, m, False, True)
                    unit_out(w, n + 1, m + 1, False, True)

            pe.wait_ge(s["tr_copied"], 2)
            logits(gate0, E0)
            comb_transposed(E0, 0)
            pe.wait_ge(s["xtl_ready"], 1)
            pe.wait_ge(s["combT_copied"], 2)
            pe.wait_ge(s["ht_copied"], 2)
            chunks(pe, chunk, 0)

            pe.wait_ge(s["g_ready"], 2)
            transposed(lambda T: XT[:, P * T:P * T + P], 0, "tr_done")
            pe.wait_ge(s["norm_ready"], 2)
            transposed(lambda T: HN[:, T, :], 0, "tr_done")
            pe.wait_ge(s["tr_copied"], 6)
            for n in range(4):
                j, h = n // 2, n % 2
                pe.matmul(bank[2 + n][:], (w1q, w1k)[j][:], XT[:, 512 * h:512 * h + 512], start=True, stop=True
                          ).then_inc(s["qk1_done"], 1)

            def rows_product(first_bank, bias, terms, signal):
                for h in range(2):
                    bk = bank[first_bank + h]
                    pe.matmul(bk[:], onesrow[:, 0:P], bvob2[:, bias, :].unsqueeze(1).broadcast_to([1, 4, D]),
                              start=True, stop=True)
                    for T in range(4 * h, 4 * h + 4):
                        for left, right in terms(T):
                            mm = pe.matmul(bk[:, D * (T % 4):D * (T % 4) + D], left, right, start=False,
                                           stop=True, skip_group_check=True)
                    mm.then_inc(s[signal], 1)

            def XT_tile(T):
                return XT[:, P * T:P * T + P]

            rows_product(6, 0, lambda T: [(XT_tile(T), w1v[:])], "v1_done")

            def scores1(T):
                pe.wait_ge(s["qbd_ready"], T + 1)
                wait(pe, "am_ready", 2 * (T - 1))
                for q in range(2):
                    pe.matmul(bank[2 * (T % 2) + q][:], KT[:, P * T:P * T + P],
                              qbd[T % 2][:, 4 * q:4 * q + 4, :].rearrange("p h r -> p (h r)"), start=True, stop=True
                              ).then_inc(s["at_done"], 1)

            def sums1(T):
                pe.wait_ge(s["am_ready"], 2 * T + 2)
                wait(pe, "ao_ready", T - 1)
                for h in range(H1):
                    mm = pe.matmul(bank[4 + T % 2][:, (DH1 + 1) * h:(DH1 + 1) * (h + 1)], am[T % 2][:, h, :],
                                   VA[:, T, h, :], start=True, stop=True)
                mm.then_inc(s["num_done"], 1)

            pe.wait_ge(s["qk_ready"], 4)
            pe.wait_ge(s["va_ready"], 2)
            scores1(0)
            for T in range(NT):
                if T + 1 < NT:
                    scores1(T + 1)
                sums1(T)
            pe.wait_ge(s["ao_ready"], NT)
            transposed(lambda T: AO[:, T, :], 0, "tr_done")
            pe.wait_ge(s["tr_copied"], 8)
            rows_product(0, 1, lambda T: [(XT_tile(T), w1o[:])], "wo1_done")
            pe.wait_ge(s["norm_ready"], 3)
            transposed(lambda T: HN2[:, T, :], 0, "tr_done")
            pe.wait_ge(s["tr_copied"], 10)
            for n in range(2 * (FF // P)):
                f, h = n // 2, n % 2
                wait(pe, "ft_ready", n - 3)
                pe.matmul(bank[2 + n % 4][:], wf1[:, P * f:P * f + P], XT[:, 512 * h:512 * h + 512],
                          start=True, stop=True).then_inc(s["ff1_done"], 1)
            pe.wait_ge(s["ft_ready"], 2 * (FF // P))
            rows_product(6, 2, lambda T: [(FT[:, f, P * T:P * T + P], wf2[:, f, :]) for f in range(FF // P)],
                         "ff2_done")

            pe.wait_ge(s["norm_ready"], 4)
            transposed(lambda T: XN[:, T, :], 0, "tr_done")
            pe.wait_ge(s["tr_copied"], 12)
            logits(gate1, E1)
            comb_transposed(E1 * C1, 1)
            pe.wait_ge(s["xtl_ready"], 2)
            pe.wait_ge(s["combT_copied"], 4)
            chunks(pe, chunk, 1)
            pe.wait_ge(s["g_ready"], 4)
            transposed(lambda T: HT[:, P * T:P * T + P], 0, "tr_done")


def kernel(**inputs):
    import numpy as np
    import concourse.bacc as bacc
    from concourse.bass_utils import run_bass_kernel_spmd as run

    x = {n: np.asarray(v) for n, v in inputs.items()}

    w = x["L0_tok_weight"].reshape(NT, 2, G, D).transpose(2, 1, 0, 3).reshape(G, B * D)
    tok = np.concatenate([w, x["x"].T, x["L0_tok_mask"]], axis=1)
    arrays = {"tok_main": tok[:GT * P].reshape(GT, P, TOKW), "tok_tail": tok[GT * P:]}
    arrays["tok_bias_row"] = x["L0_tok_bias"].reshape(NT, 2, D).transpose(1, 0, 2).reshape(1, B * D)

    p = np.arange(P)
    arrays["ident"] = np.eye(P, dtype=np.float32)
    arrays["headones"] = (p[:, None] // S == p[None, :] // S).astype(np.float32)
    arrays["causal"] = ((p[:, None] // B == p[None, :] // B) & (p[:, None] <= p[None, :])).astype(np.float32)
    arrays["headmask"] = (p[:, None] // DH1 == np.arange(H1)[None, :]).astype(np.float32)
    arrays["iota8"] = np.tile(np.arange(E1, dtype=np.float32), (P, 1))
    arrays["onesrow"] = np.ones((1, 512), np.float32)
    arrays["ones_row"] = np.ones(ROWS, np.float32)

    for n in ("L0_attn_Wq", "L0_attn_Wkv", "L0_attn_Wo", "L0_attn_gamma", "L0_attn_beta", "L1_attn_ln1_g",
              "L1_attn_ln1_b", "L1_attn_ln2_g", "L1_attn_ln2_b", "L1_attn_Wq", "L1_attn_Wk", "L1_attn_Wv",
              "L1_attn_Wo", "L1_attn_W1", "L1_attn_W2"):
        arrays[n] = x[n]
    for n in ("L1_attn_bq", "L1_attn_bk"):
        arrays[n] = x[n].reshape(D, 1)
    for n in ("L1_attn_bv", "L1_attn_bo", "L1_attn_b2"):
        arrays[n] = x[n].reshape(1, D)
    arrays["b1_cols"] = x["L1_attn_b1"].reshape(FF // P, P).T
    arrays["mu_cols"] = x["L0_attn_mu"].reshape(2, NC, P).transpose(2, 0, 1).reshape(P, 2 * NC)
    arrays["gate0T"] = x["L0_ffn_gate_w"].T
    arrays["gate1T"] = x["L1_ffn_gate_w"].T

    IS = x["L0_ffn_sw1"].shape[1]
    few0 = np.zeros((IS_CHUNKS + E0, P, 3, P), np.float32)
    for c in range(IS_CHUNKS):
        cols = slice(P * c, min(P * c + P, IS))
        k = cols.stop - cols.start
        few0[c, :, 0, :k] = x["L0_ffn_sw1"][:, cols]
        few0[c, :, 1, :k] = x["L0_ffn_sw3"][:, cols]
        few0[c, :k, 2, :] = x["L0_ffn_sw2"][cols]
    few0[IS_CHUNKS:, :, 0] = x["L0_ffn_w1"]
    few0[IS_CHUNKS:, :, 1] = x["L0_ffn_w3"]
    few0[IS_CHUNKS:, :, 2] = x["L0_ffn_w2"]
    arrays["few0"] = few0.reshape(-1, P, FEW)
    few1 = np.zeros((E1 * C1 + C1, P, 3, P), np.float32)
    few1[:E1 * C1, :, 0] = x["L1_ffn_w1"].reshape(E1 * C1, P, D).transpose(0, 2, 1)
    few1[:E1 * C1, :, 1] = x["L1_ffn_w3"].reshape(E1 * C1, P, D).transpose(0, 2, 1)
    few1[:E1 * C1, :, 2] = x["L1_ffn_w2"].reshape(E1, D, C1, P).transpose(0, 2, 3, 1).reshape(E1 * C1, P, D)
    few1[E1 * C1:, :, 0] = x["L1_ffn_sw1"].reshape(C1, P, D).transpose(0, 2, 1)
    few1[E1 * C1:, :, 2] = x["L1_ffn_sw2"].reshape(D, C1, P).transpose(1, 2, 0)
    arrays["few1"] = few1.reshape(-1, P, FEW)
    arrays = {n: np.ascontiguousarray(v) for n, v in arrays.items()}

    nc = bacc.Bacc("TRN2", target_bir_lowering=False, num_devices=1)
    a = {n: nc.dram_tensor(f"in_{n}", v.shape, F32, kind="ExternalInput").ap() for n, v in arrays.items()}
    out = nc.dram_tensor("out_0", (S, B, D), F32, kind="ExternalOutput").ap()
    audio_tower(nc, a, out)
    r = run(nc, [{f"in_{n}": v for n, v in arrays.items()}], core_ids=[0])
    return r.results[0]["out_0"]
```

```python
from contextlib import ExitStack

import concourse.bass as bass
from concourse import mybir

F32 = mybir.dt.float32
F32R = mybir.dt.float32r
U32 = mybir.dt.uint32
ALU = mybir.AluOpType
ACT = mybir.ActivationFunctionType
AX = mybir.AxisListType

P = 128
S, B, D = 64, 16, 128
NT = S * B // P
ROWS = S * B
G = 5000
GT = G // P
GR = G - GT * P
NHEAD, DH = 8, 64
NC = NHEAD * DH // P
SCALE = DH ** -0.5
E0, K0 = 64, 8
SLOTS = 4
IS_CHUNKS = 3
H1, DH1 = 8, 16
FF = 512
E1, I1 = 8, 512
C1 = I1 // P
MT = (ROWS - E1) // P + E1
EPS = 1e-5
DEN_MIN = 1e-6
TOKW = B * D + S + D
RING = 6
FEW = P * 3


def audio_tower(nc, a, out):
    ctx = ExitStack()
    with ctx:
        def sb(name, shape, dt=F32):
            return ctx.enter_context(nc.sbuf_tensor(name, shape, dt))

        def sem(name):
            return ctx.enter_context(nc.semaphore(name))

        bank = [ctx.enter_context(nc.psum_tensor(f"bank{i}", [P, 512], F32)) for i in range(8)]
        comb_rows0 = nc.dram_tensor("comb_rows0", [E0, ROWS], F32).ap()
        x_grouped = nc.dram_tensor("x_grouped", [MT * P, D + 1], F32).ap()
        y_rows = nc.dram_tensor("y_rows", [ROWS, D], F32).ap()

        ident = sb("ident", [P, P])
        headones = sb("headones", [P, P])
        causal = sb("causal", [P, P])
        headmask = sb("headmask", [P, H1])
        iota8 = sb("iota8", [P, E1])
        onesrow = sb("onesrow", [1, 512])
        before_p = sb("before_p", [P, P])
        allones = sb("allones", [P, P])
        before_e = sb("before_e", [P, E1, E1])
        steps128 = sb("steps128", [P, MT])
        row_id = sb("row_id", [P, NT])
        warmed = sb("warmed", [P, 3])
        wq = sb("wq", [P, NHEAD * DH])
        wkv = sb("wkv", [P, 2 * NHEAD * DH])
        wo = sb("wo", [P, NC, D])
        mu = sb("mu", [P, 2, NC])
        gate0 = sb("gate0", [P, E0])
        gate1 = sb("gate1", [P, E1])
        rowvec = sb("rowvec", [P, 2, D])
        lncols = sb("lncols", [P, 4])
        w1q = sb("w1q", [P, D])
        w1k = sb("w1k", [P, D])
        w1v = sb("w1v", [P, D])
        w1o = sb("w1o", [P, D])
        b1q = sb("b1q", [P, 1])
        b1k = sb("b1k", [P, 1])
        bvob2 = sb("bvob2", [1, 3, D])
        wf1 = sb("wf1", [P, FF])
        bf1 = sb("bf1", [P, FF // P])
        wf2 = sb("wf2", [P, FF // P, D])
        ring = sb("ring", [P, RING, TOKW])
        EVEN = NT * D
        tail = ring[0:GR, GT % RING, :]
        H = sb("H", [P, NT, D])
        Y = sb("Y", [P, NT, D])
        XNX = sb("XNX", [P, NT, D + 1])
        XN = XNX[:, :, 0:D]
        stats = sb("stats", [P, NT, 6])
        mv = sb("mv", [P, NT, 2])
        var_eps = sb("var_eps", [P, NT])
        neg_half = sb("neg_half", [P, NT])
        rstd = sb("rstd", [P, NT])
        over = ring[:].rearrange("p j n -> p (j n)")
        FT = over[:, 0:4 * ROWS].rearrange("p (f r) -> p f r", r=ROWS)
        eq = over[:, 4 * ROWS:6 * ROWS].rearrange("p (j r) -> p j r", r=ROWS)
        rq = over[:, 6 * ROWS:8 * ROWS].rearrange("p (j r) -> p j r", r=ROWS)
        QT = over[:, 8 * ROWS:9 * ROWS]
        KT = over[:, 9 * ROWS:10 * ROWS]
        HT = over[:, 10 * ROWS:11 * ROWS]
        HN = over[:, 11 * ROWS:12 * ROWS].rearrange("p (t d) -> p t d", d=D)
        X1 = over[:, 12 * ROWS:13 * ROWS].rearrange("p (t d) -> p t d", d=D)
        xs = [sb(f"xs{u}", [P, D]) for u in range(2)]
        hT = [sb(f"hT{u}", [P, P]) for u in range(2)]
        LQ = [[sb(f"LQ{u}{n2}", [P, 2, NC, P]) for n2 in range(2)] for u in range(2)]
        RK = [[sb(f"RK{u}{n2}", [P, NC, P]) for n2 in range(2)] for u in range(2)]
        ksq = [sb(f"ksq{u}", [P, NC, P]) for u in range(2)]
        vt = [sb(f"vt{u}", [P, NHEAD * DH]) for u in range(2)]
        z1 = [sb(f"z1{u}", [P, NHEAD, S]) for u in range(2)]
        sc = [sb(f"sc{u}", [P, NHEAD, S]) for u in range(2)]
        pT = [sb(f"pT{u}", [P, NC, P]) for u in range(2)]
        vecT = [sb(f"vecT{u}", [P, NC, 2, S]) for u in range(2)]
        rmin = [sb(f"rmin{u}", [P, NHEAD]) for u in range(2)]
        rsum = [sb(f"rsum{u}", [P, NHEAD]) for u in range(2)]
        XT = sb("XT", [P, ROWS])
        XTh = sb("XTh", [P, ROWS], F32R)
        XTl = sb("XTl", [P, ROWS], F32R)
        few = [sb(f"few{u}", [P, FEW]) for u in range(SLOTS)]
        fewh13 = [sb(f"fewh13{u}", [P, 2 * P], F32R) for u in range(2)]
        fewl13 = [sb(f"fewl13{u}", [P, 2 * P], F32R) for u in range(2)]
        fewh2 = [sb(f"fewh2{u}", [P, P], F32R) for u in range(2)]
        fewl2 = [sb(f"fewl2{u}", [P, P], F32R) for u in range(2)]
        comb_b = [over[:, u * ROWS:(u + 1) * ROWS] for u in range(SLOTS)]
        act_s = [sb(f"act_s{u}", [P, 512]) for u in range(2)]
        act_g = [sb(f"act_g{u}", [P, 512]) for u in range(2)]
        hid = [sb(f"hid{u}", [P, 512]) for u in range(2)]
        hidh = [sb(f"hidh{u}", [P, 512], F32R) for u in range(4)]
        hidl = [sb(f"hidl{u}", [P, 512], F32R) for u in range(4)]
        ksqh, ksql = hidh[0:2], hidl[0:2]
        headones_r = fewh13[0][:, 0:P]
        lg, lgr = (vt[u][:].rearrange("p (t e) -> p t e", e=E0) for u in range(2))
        comb = ksq[0][:].rearrange("p c r -> p (c r)").rearrange("p (t e) -> p t e", e=E0)
        combT = LQ[1][0][0:E0, :, :, :].rearrange("p a c r -> p (a c r)")
        mx = sb("mx", [P, NT, K0])
        mxi = sb("mxi", [P, NT, K0], U32)
        rs8 = sb("rs8", [P, NT])
        HN2 = HN
        VA = sb("VA", [P, NT, H1, DH1 + 1])
        qbd = [LQ[u][0][:].rearrange("p a c r -> p (a c) r") for u in range(2)]
        am = [LQ[u][1][:].rearrange("p a c r -> p (a c) r") for u in range(2)]
        den = sb("den", [P, NT, H1])
        rden = sb("rden", [P, NT, H1])
        AO = XN
        onehot = sb("onehot", [P, NT, E1])
        rank = sb("rank", [P, NT, E1])
        counts = sb("counts", [P, E1])
        cmp8 = sb("cmp8", [P, E1, NT])
        full = sb("full", [P, E1])
        base = sb("base", [P, E1])
        ends = sb("ends", [P, E1])
        cmp_e = sb("cmp_e", [P, MT, E1])
        tile_e = sb("tile_e", [P, MT])
        place = sb("place", [P, NT])
        place_i = sb("place_i", [P, NT], U32)
        wrow_i = sb("wrow_i", [P, MT], U32)
        e13 = [over[:, u * 2 * I1:(u + 1) * 2 * I1] for u in range(2)]
        e2 = [over[:, 4 * I1 + u * C1 * D:4 * I1 + (u + 1) * C1 * D] for u in range(2)]
        xg = [over[:, 11 * ROWS + u * (D + 1):11 * ROWS + (u + 1) * (D + 1)] for u in range(2)]
        yg = [over[:, 12 * ROWS + u * D:12 * ROWS + (u + 1) * D] for u in range(2)]
        yrow_i = sb("yrow_i", [P, MT], U32)
        e13h = [XTh[:], sb("e13h1", [P, 2 * I1], F32R)[:]]
        e13l = [XTl[:], sb("e13l1", [P, 2 * I1], F32R)[:]]
        e2h = [hidh[2 + u][:] for u in range(2)]
        e2l = [hidl[2 + u][:] for u in range(2)]
        xgh = [fewh2[u][:] for u in range(2)]
        xgl = [fewl2[u][:] for u in range(2)]
        bias0, bias1 = (LQ[u][0][0:1, :, :, :].rearrange("p a c r -> p (a c r)") for u in range(2))

        consts = [
            (onesrow[:], a["onesrow"]),
            (bias0, a["tok_bias_row"][:, 0:B * D // 2]), (bias1, a["tok_bias_row"][:, B * D // 2:]),
            (row_id[:], a["row_id"]), (ident[:], a["ident"]), (headones[:], a["headones"]),
            (wq[:], a["L0_attn_Wq"]), (wkv[:], a["L0_attn_Wkv"]),
            (wo[:], a["L0_attn_Wo"].rearrange("(c p) d -> p c d", p=P)),
            (mu[:].rearrange("p c k -> p (c k)"), a["mu_cols"]),
        ] + [(rowvec[:, n, :], a[name].partition_broadcast(P)) for n, name in enumerate(
            ["L0_attn_gamma", "L0_attn_beta"])]
        N_FIRST = 3
        N_CONSTS = 16 * (len(consts) - N_FIRST)
        late_consts = [
            (gate0[:], a["gate0T"]), (gate1[:], a["gate1T"]),
            (lncols[:], a["lncols"]), (before_p[:], a["before_p"]), (allones[:], a["allones"]),
            (steps128[:], a["steps128"]), (before_e[:].rearrange("p e f -> p (e f)"), a["before_e"]),
            (causal[:], a["causal"]), (headmask[:], a["headmask"]), (iota8[:], a["iota8"]),
            (w1q[:], a["L1_attn_Wq"]), (w1k[:], a["L1_attn_Wk"]), (w1v[:], a["L1_attn_Wv"]),
            (w1o[:], a["L1_attn_Wo"]), (b1q[:], a["L1_attn_bq"]), (b1k[:], a["L1_attn_bk"]),
            (bvob2[:, 0, :], a["L1_attn_bv"]), (bvob2[:, 1, :], a["L1_attn_bo"]),
            (bvob2[:, 2, :], a["L1_attn_b2"]),
            (wf1[:], a["L1_attn_W1"]), (bf1[:], a["b1_cols"]),
            (wf2[:], a["L1_attn_W2"].rearrange("(c p) d -> p c d", p=P)),
        ]
        N_LATE = 16 * len(late_consts)

        names = """first_loaded const_loaded late_loaded tail_loaded last_loaded tok_masked tok_used tok_done h0_ready fill_done
            va_filled ones_filled xn_ready ksqh_ready ksql_ready headones_ready var_ready rstd_ready dve_step
            xs_ready xT_done hT_ready q_done q_read k_done k_read v_done v_read qsq_ready x_done z1_read m_done
            e_ready p_exp p_ready pT_done pT_ready pv_done vec0_ready vec1_ready wo_done y_ready y_stats
            hsum_ready norm_ready tr_done tr_copied xth_ready xtl_ready logits_done logits_copied lmax_sub lexp
            comb_ready combT_done combT_copied comb_stored ht_done ht_copied few_loaded0 few_loaded1 few_loaded2
            few_loaded3 row_loaded0 row_loaded1 row_loaded2 row_loaded3 w13h_ready w13l_ready w2h_ready
            w2l_ready h1_done h_done act_ready gated_ready hid_ready hidh_ready hidl_ready y_done g_ready
            qk1_done erq_ready qk_ready v1_done va_ready qbd_ready at_done am_ready num_done ao_ready wo1_done
            ff1_done ft_ready ff2_done onehot_ready rank_done places_ready cleared rows_scattered e13_loaded0
            e13_loaded1 e2_loaded0 e2_loaded1 xg_loaded0 xg_loaded1 e13h_ready e13l_ready e2h_ready e2l_ready
            xgT_done xgh_ready xgl_ready s1_done s3_done silu_ready hs_ready hsT_done hsh_ready hsl_ready
            yg_done yg_ready yg_stored0 yg_stored1 y_loaded0 y_loaded1 yrow_ready shared_added out_ready out_stored""".split()
        s = {n: sem(n) for n in names}
        tok_loaded = [sem(f"tok_loaded{j}") for j in range(RING)]

        W1 = IS_CHUNKS + E0
        WEND = W1 + C1
        def wait(eng, name, value):
            if not isinstance(value, int) or value > 0:
                eng.wait_ge(s[name], value)

        def steps(eng, step):
            def peeled(t):
                step(t, t % 2, lambda d: 0 <= t + d < NT)
            for t in range(-2, 2):
                peeled(t)
            with eng.Fori(1, NT // 2 - 1) as i:
                for u in range(2):
                    step(2 * i + u, u, lambda d: True)
            for t in range(NT - 2, NT + 1):
                peeled(t)

        def chunks(eng, body, layer):
            if layer == 1:
                for w in range(W1, WEND):
                    body(w, w // SLOTS, w % SLOTS, min(w - W1, 2))
                return
            for w in range(SLOTS):
                body(w, 0, w, min(w, 2))
            with eng.Fori(1, W1 // SLOTS) as i:
                for u in range(SLOTS):
                    body(SLOTS * i + u, i, u, 2)
            for w in range(W1 // SLOTS * SLOTS, W1):
                body(w, w // SLOTS, w % SLOTS, 2)

        def routed(eng, step):
            def peeled(t):
                step(t, t % 2, lambda d: 0 <= t + d < MT)
            for t in range(-1, 6):
                peeled(t)
            with eng.Fori(3, (MT - 1) // 2) as i:
                for u in range(2):
                    step(2 * i + u, u, lambda d: True)
            for t in range((MT - 1) // 2 * 2, MT + 3):
                peeled(t)

        def slot_loads(t, u):
            return 16 * (t // 2 + 1) if isinstance(t, int) else 8 * (t - u) + 16

        def is_last(w):
            return isinstance(w, int) and w + 1 in (W1, WEND)

        def is_gelu(w):
            return isinstance(w, int) and W1 <= w < W1 + C1

        ROOTS = [0, 1] + [0, 0, 1, 1] + [0, 1, 0, 1] + [0, 1] + [0, 1]

        block = ctx.enter_context(nc.Block())

        @block.sync
        def _(sp):
            def load_tile(k, j):
                sp.dma_start(ring[:, j, :], a["tok_main"][bass.ds(k, 1), :, :].rearrange("t p n -> (t p) n")
                             ).then_inc(tok_loaded[j], 16)

            for j in range(RING):
                load_tile(j, j)
            with sp.Fori(1, GT // RING) as r:
                for j in range(RING):
                    sp.wait_ge(s["tok_used"], RING * (r - 1) + j + 1)
                    load_tile(r * RING + j, j)

            def load_straight(k):
                sp.wait_ge(s["tok_used"], k - RING + 1)
                load_tile(k, k % RING)

            for k in range(GT // RING * RING, GT - 1):
                load_straight(k)
            sp.wait_ge(s["tok_used"], GT - RING + 1)
            sp.dma_start(tail, a["tok_tail"]).then_inc(s["tail_loaded"], 16)
            last = ring[:, (GT - 1) % RING, :]
            sp.dma_start(last[:, EVEN:], a["tok_main"][GT - 1, :, EVEN:]).then_inc(tok_loaded[(GT - 1) % RING], 16)
            sp.dma_start(last[:, 0:EVEN], a["tok_main"][GT - 1, :, 0:EVEN]).then_inc(s["last_loaded"], 16)

            sp.wait_ge(s["tok_done"], 1)
            for dst, src in late_consts:
                sp.dma_start(dst, src).then_inc(s["late_loaded"], 16)

            def load_chunk(w, i, u, age, layer):
                few_dram, first = ((a["few0"], 0), (a["few1"], W1))[layer]
                wait(sp, "w2l_ready", w - 3)
                sp.dma_start(few[u][:], few_dram[bass.ds(w - first, 1), :, :].rearrange("e p n -> (e p) n")
                             ).then_inc(s[f"few_loaded{u}"], 16)
                if layer == 1:
                    return
                wait(sp, "gated_ready", 2 * (w - 3))
                if isinstance(w, int) and w == 0:
                    sp.wait_ge(s["tok_done"], 2)
                if isinstance(w, int) and w < IS_CHUNKS:
                    row = a["ones_row"].partition_broadcast(P)
                else:
                    if isinstance(w, int) and w == IS_CHUNKS:
                        sp.wait_ge(s["combT_copied"], 2)
                        sp.dma_start(comb_rows0, combT).then_inc(s["comb_stored"], 16)
                        sp.wait_ge(s["comb_stored"], 16)
                    row = comb_rows0[bass.ds(w - IS_CHUNKS, 1), :].rearrange("a n -> (a n)").partition_broadcast(P)
                sp.dma_start(comb_b[u], row).then_inc(s[f"row_loaded{u}"], 16)

            for layer in range(2):
                chunks(sp, lambda *k: load_chunk(*k, layer), layer)

            def grouped(t, u, has):
                if has(1):
                    wait(sp, "xgT_done", t)
                    wait(sp, "yrow_ready", t)
                    sp.dma_start(xg[1 - u], x_grouped[bass.ds(P * (t + 1), P), :]).then_inc(s[f"xg_loaded{1 - u}"], 16)

            sp.wait_ge(s["rows_scattered"], 16 * NT)
            routed(sp, grouped)

            for t in (MT - 2, MT - 1):
                sp.wait_ge(s[f"yg_stored{t % 2}"], slot_loads(t, t % 2))
            for h in range(2):
                sp.dma_start(Y[:, 4 * h:4 * h + 4, :], y_rows[4 * h * P:(4 * h + 4) * P, :].rearrange(
                    "(t p) d -> p t d", p=P)).then_inc(s[f"y_loaded{h}"], 16)

            o = out.rearrange("(t s) b d -> (s b) t d", s=P // B)
            for h in range(2):
                sp.wait_ge(s["out_ready"], h + 1)
                sp.dma_start(o[:, 4 * h:4 * h + 4, :], H[:, 4 * h:4 * h + 4, :]).then_inc(s["out_stored"], 16)
            sp.wait_ge(s["out_stored"], 32)

        @block.scalar
        def _(act):
            for n, (dst, src) in enumerate(consts):
                act.dma_start(dst, src).then_inc(s["first_loaded" if n < N_FIRST else "const_loaded"], 16)

            for h in range(2):
                act.wait_ge(s["tok_done"], h + 1)
                nc.scalar.copy(H[:, 4 * h:4 * h + 4, :], bank[h][:].rearrange("p (t d) -> p t d", d=D)
                               ).then_inc(s["h0_ready"], 1)

            act.wait_ge(s["const_loaded"], N_CONSTS)
            nc.scalar.copy(headones_r, headones[:]).then_inc(s["headones_ready"], 1)

            def squares(t, v, n2):
                act.wait_ge(s["q_read"], 4 * t + 4)
                rows, other = slice(S * n2, S * n2 + S), slice(S * (1 - n2), S * (1 - n2) + S)
                nc.scalar.activation(LQ[v][n2][other, :, :, :], LQ[v][n2][rows, :, :, :], ACT.Square
                                     ).then_inc(s["qsq_ready"], 1)

            def attention(t, u, has):
                v = 1 - u
                if has(1):
                    act.wait_ge(s["k_done"], t + 2)
                    wait(act, "x_done", 2 * t)
                    wait(act, "ksql_ready", t)
                    for n2 in range(2):
                        rows = slice(S * n2, S * n2 + S)
                        nc.scalar.mul(RK[v][n2][rows, :, :], bank[2][rows, :].rearrange("p (c r) -> p c r", c=NC), -2.0
                                      ).then_inc(s["k_read"], 1)
                    nc.scalar.activation(ksq[v][:], bank[2][:].rearrange("p (c r) -> p c r", c=NC), ACT.Square
                                         ).then_inc(s["k_read"], 1)
                    act.wait_ge(s["k_read"], 3 * t + 6)
                    nc.scalar.copy(ksqh[v][:], ksq[v][:].rearrange("p c r -> p (c r)")).then_inc(s["ksqh_ready"], 1)
                if has(-1):
                    act.wait_ge(s["pT_done"], t)
                    wait(act, "pv_done", t - 2)
                    nc.scalar.copy(pT[v][:], bank[6][:].rearrange("p (c r) -> p c r", c=NC)).then_inc(s["pT_ready"], 1)
                if has(0):
                    act.wait_ge(s["x_done"], 2 * t + 2)
                    wait(act, "m_done", t - 1)
                    nc.scalar.mul(z1[u][:], bank[5][:].rearrange("p (n j) -> p n j", j=S), 1.5 * SCALE
                                  ).then_inc(s["z1_read"], 1)
                if has(1):
                    squares(t + 1, v, 0)
                if has(-1):
                    act.wait_ge(s["pv_done"], t)
                    wait(act, "wo_done", t - 2)
                    nc.scalar.copy(vecT[v][:, :, 0, :], bank[6][:, 0:NC * S].rearrange("p (c i) -> p c i", c=NC)
                                   ).then_inc(s["vec0_ready"], 1)
                if has(1):
                    squares(t + 1, v, 1)
                if has(2):
                    act.wait_ge(s["xT_done"], t + 3)
                    wait(act, "v_done", t + 1)
                    nc.scalar.copy(hT[u][:], bank[0][:, 0:P]).then_inc(s["hT_ready"], 1)
                if has(1):
                    act.wait_ge(s["v_done"], t + 2)
                    wait(act, "pv_done", t)
                    nc.scalar.copy(vt[v][:], bank[3][:]).then_inc(s["v_read"], 1)
                if has(0):
                    act.wait_ge(s["e_ready"], t + 1)
                    nc.scalar.activation(sc[u][:], sc[u][:], ACT.Exp, scale=-1.0).then_inc(s["p_exp"], 1)
            act.dma_start(x_grouped, a["empty_rows"]).then_inc(s["cleared"], 16)
            steps(act, attention)

            def copy_transposed(n, h, b, dst, norm=None):
                act.wait_ge(s["tr_done"], 2 * n + h + 1)
                src = bank[b][:] if len(dst.shape) == 2 else bank[b][:].rearrange("p (t d) -> p t d", d=D)
                if norm is None:
                    nc.scalar.copy(dst, src).then_inc(s["tr_copied"], 1)
                else:
                    nc.scalar.activation(dst, src, ACT.Identity, bias=lncols[:, norm + 1:norm + 2],
                                         scale=lncols[:, norm:norm + 1]).then_inc(s["tr_copied"], 1)

            def warm(func, n):
                nc.scalar.activation(warmed[:, n:n + 1], ident[:, 0:1], func)

            def XT_half(h):
                return XT[:, 512 * h:512 * h + 512]

            def x_high(n, h):
                act.wait_ge(s["tr_copied"], 2 * n + h + 1)
                nc.scalar.copy(XTh[:, 512 * h:512 * h + 512], XT_half(h)).then_inc(s["xth_ready"], 1)

            def logits_copy(layer, e):
                for h in range(2):
                    act.wait_ge(s["logits_done"], 2 * layer + h + 1)
                    nc.scalar.copy(lg[:, 4 * h:4 * h + 4, 0:e], bank[6 + h][:, 0:4 * e].rearrange(
                        "p (t e) -> p t e", e=e)).then_inc(s["logits_copied"], 1)

            def comb_transposed():
                for h in range(2):
                    act.wait_ge(s["combT_done"], h + 1)
                    nc.scalar.copy(combT[:, 512 * h:512 * h + 512], bank[6 + h][0:E0, :]
                                   ).then_inc(s["combT_copied"], 1)

            def w13_high(w, i, u):
                act.wait_ge(s[f"few_loaded{u}"], 16 * (i + 1))
                wait(act, "h_done", 2 * (w - 1))
                wait(act, "w13l_ready", w - 1)
                nc.scalar.copy(fewh13[u % 2][:], few[u][:, 0:2 * P]).then_inc(s["w13h_ready"], 1)

            def w2_high(w, u):
                wait(act, "y_done", 2 * (w - 1))
                wait(act, "w2l_ready", w - 1)
                nc.scalar.copy(fewh2[u % 2][:], few[u][:, 2 * P:]).then_inc(s["w2h_ready"], 1)

            def activate(n, m, gelu):
                act.wait_ge(s["h_done" if gelu else "h1_done"], n + 1)
                wait(act, "hid_ready" if gelu and n >= 2 * W1 + 2 else "gated_ready", n - 1)
                nc.scalar.activation(act_s[m % 2][:], bank[m % 2][:], ACT.Gelu if gelu else ACT.Silu
                                     ).then_inc(s["act_ready"], 1)

            def hidden_high(n, m):
                act.wait_ge(s["hid_ready"], n + 1)
                wait(act, "y_done", n - 3)
                nc.scalar.copy(hidh[m % 4][:], hid[m % 2][:]).then_inc(s["hidh_ready"], 1)

            def chunk(w, i, u, age):
                n = 2 * w
                activate(n, 2 * u, is_gelu(w))
                if age:
                    w2_high(w - 1, (u - 1) % SLOTS)
                if not is_last(w):
                    w13_high(w + 1, i + (u + 1) // SLOTS, (u + 1) % SLOTS)
                if age:
                    hidden_high(n - 1, 2 * u - 1)
                activate(n + 1, 2 * u + 1, is_gelu(w))
                hidden_high(n, 2 * u)
                if is_last(w):
                    w2_high(w, u)
                if isinstance(w, int) and w == 1:
                    comb_transposed()
                if is_last(w):
                    hidden_high(n + 1, 2 * u + 1)

            act.wait_ge(s["late_loaded"], N_LATE)
            copy_transposed(0, 0, 0, XT_half(0))
            x_high(0, 0)
            for h in range(2):
                act.wait_ge(s["ht_done"], h + 1)
                nc.scalar.copy(HT[:, 512 * h:512 * h + 512], bank[2 + h][:]).then_inc(s["ht_copied"], 1)
            w13_high(0, 0, 0)
            copy_transposed(0, 1, 1, XT_half(1))
            x_high(0, 1)
            logits_copy(0, E0)
            act.wait_ge(s["lmax_sub"], 1)
            nc.scalar.activation(comb, comb, ACT.Exp).then_inc(s["lexp"], 1)
            chunks(act, chunk, 0)

            for h in range(2):
                copy_transposed(1, h, h, H[:, 4 * h:4 * h + 4, :])
            warm(ACT.Exp, 0)
            for h in range(2):
                copy_transposed(2, h, h, XT_half(h), norm=0)
                cols = slice(512 * h, 512 * h + 512)
                for j in range(2):
                    act.wait_ge(s["qk1_done"], 2 * h + j + 1)
                    bias = (b1q, b1k)[j][:, 0:1]
                    nc.scalar.activation(eq[:, j, cols], bank[2 + 2 * j + h][:], ACT.Exp, bias=bias
                                         ).then_inc(s["erq_ready"], 1)
                    nc.scalar.activation(rq[:, j, cols], bank[2 + 2 * j + h][:], ACT.Relu, bias=bias
                                         ).then_inc(s["erq_ready"], 1)
                act.wait_ge(s["v1_done"], h + 1)
                act.wait_ge(s["va_filled"], 1)
                nc.scalar.copy(VA[:, 4 * h:4 * h + 4, :, 0:DH1].rearrange("p t h d -> p (t h) d"),
                               bank[6 + h][:].rearrange("p (t d) -> p t d", d=DH1)).then_inc(s["va_ready"], 1)
            copy_transposed(3, 0, 6, XT_half(0))
            copy_transposed(3, 1, 0, XT_half(1))
            for h in range(2):
                copy_transposed(4, h, (6, 0)[h], XT_half(h), norm=2)
                for f in range(FF // P):
                    act.wait_ge(s["ff1_done"], FF // P * h + f + 1)
                    nc.scalar.activation(FT[:, f, 512 * h:512 * h + 512], bank[2 + f][:], ACT.Relu,
                                         bias=bf1[:, f:f + 1]).then_inc(s["ft_ready"], 1)

            warm(ACT.Gelu, 1)
            w13_high(W1, W1 // SLOTS, W1 % SLOTS)
            for h in range(2):
                copy_transposed(5, h, h, XT_half(h))
                x_high(5, h)
            logits_copy(1, E1)
            chunks(act, chunk, 1)
            warm(ACT.Silu, 2)

            def grouped(t, u, has):
                v = 1 - u
                if has(-2):
                    act.wait_ge(s["hsT_done"], t - 1)
                    wait(act, "yg_done", t - 3)
                    nc.scalar.copy(hidh[u][:], bank[(4, 7)[u]][:]).then_inc(s["hsh_ready"], 1)
                if has(1):
                    act.wait_ge(s[f"e13_loaded{v}"], slot_loads(t + 1, v))
                    wait(act, "s3_done", t)
                    wait(act, "e13l_ready", t)
                    nc.scalar.copy(e13h[v], e13[v]).then_inc(s["e13h_ready"], 1)
                if has(-3):
                    act.wait_ge(s["yg_done"], t - 2)
                    if has(-5):
                        act.wait_ge(s[f"yg_stored{v}"], slot_loads(t - 5, v))
                    nc.scalar.copy(yg[v], bank[5][:, 0:D]).then_inc(s["yg_ready"], 1)
                if has(0):
                    act.wait_ge(s["s1_done"], t + 1)
                    wait(act, "hs_ready", t - 1)
                    nc.scalar.activation(act_s[u][:], bank[2 * u][:], ACT.Silu).then_inc(s["silu_ready"], 1)
                if has(1):
                    act.wait_ge(s["xgT_done"], t + 2)
                    nc.scalar.copy(xgh[v], bank[6][:, 0:P]).then_inc(s["xgh_ready"], 1)
                if has(-1):
                    act.wait_ge(s[f"e2_loaded{v}"], slot_loads(t - 1, v))
                    wait(act, "yg_done", t - 2)
                    wait(act, "e2l_ready", t - 2)
                    nc.scalar.copy(e2h[v], e2[v]).then_inc(s["e2h_ready"], 1)
            routed(act, grouped)

        @block.gpsimd
        def _(pool):
            pool.memset(neg_half[:], -0.5).then_inc(s["fill_done"], 1)

            def roots(n, count):
                for n in range(n, n + count):
                    pool.wait_ge(s["var_ready"], n + 1)
                    pool.wait_ge(s["fill_done"], 1)
                    tiles = slice(4 * ROOTS[n], 4 * ROOTS[n] + 4)
                    pool.tensor_tensor(rstd[:, tiles], var_eps[:, tiles], neg_half[:, tiles], ALU.pow
                                       ).then_inc(s["rstd_ready"], 1)

            def attention(t, u, has):
                if has(2):
                    if isinstance(t, int):
                        pool.wait_ge(s["xn_ready"], 1 + (t + 2) // 4)
                    elif u == 0:
                        pool.wait_ge(s["xn_ready"], 2)
                    wait(pool, "xT_done", t + 1)
                    pool.tensor_copy(xs[u][:], XN[:, bass.ds(t + 2, 1), :].rearrange("p a d -> p (a d)")
                                     ).then_inc(s["xs_ready"], 1)

            def chunk(w, i, u, age):
                pool.wait_ge(s[f"row_loaded{u}"], 16 * (i + 1))
                for h in range(2):
                    n = 2 * w + h
                    pool.wait_ge(s["act_ready"], n + 1)
                    wait(pool, "hid_ready", n - 1)
                    pool.tensor_tensor(act_g[h][:], act_s[h][:], comb_b[u][:, 512 * h:512 * h + 512], ALU.mult
                                       ).then_inc(s["gated_ready"], 1)

            roots(0, 2)
            steps(pool, attention)
            roots(2, 4)
            chunks(pool, chunk, 0)
            roots(6, 4)
            pool.wait_ge(s["late_loaded"], N_LATE)
            for T in range(NT):
                pool.wait_ge(s["qk_ready"], 2 * (T // 4) + 1)
                wait(pool, "at_done", 2 * (T - 1))
                pool.tensor_tensor(qbd[T % 2], QT[:, P * T:P * T + P].unsqueeze(1).broadcast_to([P, H1, P]),
                                   headmask[:].unsqueeze(2).broadcast_to([P, H1, P]), ALU.mult
                                   ).then_inc(s["qbd_ready"], 1)
            roots(10, 4)

            pool.wait_ge(s["places_ready"], 1)
            pool.wait_ge(s["cleared"], 16)
            pool.wait_ge(s["norm_ready"], 8)
            for T in range(NT):
                pool.indirect_dma_start(x_grouped, bass.IndirectOffsetOnAxis(ap=place_i[:, T:T + 1], axis=0),
                                        XNX[:, T, :], None).then_inc(s["rows_scattered"], 16)

            def expert_rows(t, dst, src, signal):
                pool.indirect_dma_start(dst, None, src, bass.IndirectOffsetOnAxis(ap=wrow_i[:, t:t + 1], axis=0)
                                        ).then_inc(s[signal], 16)

            pool.wait_ge(s["places_ready"], 2)
            def results(t):
                pool.wait_ge(s["yg_ready"], t + 1)
                pool.indirect_dma_start(y_rows, bass.IndirectOffsetOnAxis(ap=yrow_i[:, t:t + 1], axis=0), yg[t % 2],
                                        None, bounds_check=ROWS - 1, oob_is_err=False
                                        ).then_inc(s[f"yg_stored{t % 2}"], 16)

            def first_weights(t):
                wait(pool, "e13l_ready", t - 1)
                expert_rows(t, e13[t % 2], a["expert13"], f"e13_loaded{t % 2}")

            def second_weights(t):
                wait(pool, "e2l_ready", t - 1)
                expert_rows(t, e2[t % 2], a["expert2"], f"e2_loaded{t % 2}")

            for t in range(2):
                first_weights(t)
            for t in range(2):
                second_weights(t)
            for t in range(MT):
                if t + 2 < MT:
                    first_weights(t + 2)
                if t >= 2:
                    second_weights(t)
                if t >= 4:
                    results(t - 4)
            for t in range(MT - 4, MT):
                results(t)

        @block.vector
        def _(dve):
            class Chain:
                base, n = 0, 0

                def __call__(self, ins):
                    self.n += 1
                    ins.then_inc(s["dve_step"], 1)

                def sync(self):
                    dve.wait_ge(s["dve_step"], self.base + self.n)

                def link(self, ins):
                    self(ins)
                    self.sync()
            chain = Chain()

            norm_count = [0]

            def variance(h):
                dve.tensor_scalar(var_eps[:, 4 * h:4 * h + 4], mv[:, 4 * h:4 * h + 4, 1], EPS, None, ALU.add
                                  ).then_inc(s["var_ready"], 1)
                norm_count[0] += 1
                return norm_count[0]

            def stats_of(src, h):
                for T in range(4 * h, 4 * h + 4):
                    chain(dve.bn_stats(stats[:, T, :], src[:, T, :]))
                chain.sync()
                return aggregated(h)

            def aggregated(h):
                for T in range(4 * h, 4 * h + 4):
                    chain(dve.bn_aggr(mv[:, T, :], stats[:, T, :]))
                chain.sync()
                return variance(h)

            def normalised(dst, src, h, n, signal=None, count=0):
                dve.wait_ge(s["rstd_ready"], n)
                for T in range(4 * h, 4 * h + 4):
                    ins = dve.tensor_scalar(dst[:, T, :], src[:, T, :], mv[:, T, 0:1], rstd[:, T:T + 1],
                                            ALU.subtract, ALU.mult)
                    if signal and T == 4 * h + 3:
                        ins.then_inc(s[signal], 1)
                    else:
                        chain(ins)
                chain.sync()
                if signal:
                    dve.wait_ge(s[signal], count)

            def half(buf, h):
                return buf[:, 4 * h:4 * h + 4, :]

            def mask(rows, slot_ap, cols=slice(0, 2 * EVEN)):
                w = slot_ap[:, cols].rearrange("p (b d) -> p b d", d=D)
                m = slot_ap[:, B * D + S:].unsqueeze(1).broadcast_to([rows, w.shape[1], D])
                dve.tensor_tensor(w, w, m, ALU.mult).then_inc(s["tok_masked"], 1)

            dve.memset(VA[:].rearrange("p t h d -> p (t h d)"), 1.0).then_inc(s["va_filled"], 1)
            for u in range(2):
                for n2 in range(2):
                    other = slice(S * (1 - n2), S * (1 - n2) + S)
                    dve.memset(RK[u][n2][other, :, :], 1.0).then_inc(s["ones_filled"], 1)
            with dve.Fori(0, GT // RING) as r:
                for j in range(RING):
                    dve.wait_ge(tok_loaded[j], 16 * (r + 1))
                    mask(P, ring[:, j, :])
            for k in range(GT // RING * RING, GT - 1):
                dve.wait_ge(tok_loaded[k % RING], 16 * (k // RING + 1))
                mask(P, ring[:, k % RING, :])
            dve.wait_ge(s["tail_loaded"], 16)
            mask(GR, tail)
            dve.wait_ge(tok_loaded[(GT - 1) % RING], 16 * (GT // RING + 1))
            mask(P, ring[:, (GT - 1) % RING, :], slice(EVEN, 2 * EVEN))
            dve.wait_ge(s["last_loaded"], 16)
            mask(P, ring[:, (GT - 1) % RING, :], slice(0, EVEN))

            for h in range(2):
                dve.wait_ge(s["h0_ready"], h + 1)
                n = stats_of(H, h)
            for h in range(2):
                normalised(XN, H, h, n - 1 + h, "xn_ready", h + 1)
            dve.wait_ge(s["const_loaded"], N_CONSTS)
            chain.link(dve.tensor_copy(XNX[:, :, D:D + 1], row_id[:].unsqueeze(2)))
            for h in range(2):
                chain.link(dve.tensor_tensor(half(H, h), half(H, h),
                                             rowvec[:, 1, :].unsqueeze(1).broadcast_to([P, 4, D]), ALU.add))

            before = chain.n
            roots0 = []

            def output_added(h, n):
                dve.wait_ge(s["xs_ready"], NT)
                for T in range(4 * h, 4 * h + 4):
                    chain(dve.scalar_tensor_tensor(out=XN[:, T, :], in0=Y[:, T, :], scalar=mv[:, T, 0:1],
                                                   in1=rowvec[:, 0, :], op0=ALU.subtract, op1=ALU.mult))
                chain.sync()
                dve.wait_ge(s["rstd_ready"], n)
                for T in range(4 * h, 4 * h + 4):
                    ins = dve.scalar_tensor_tensor(out=H[:, T, :], in0=XN[:, T, :], scalar=rstd[:, T:T + 1],
                                                   in1=H[:, T, :], op0=ALU.mult, op1=ALU.add)
                    if T % 4 == 3:
                        ins.then_inc(s["hsum_ready"], 1)
                    else:
                        chain(ins)
                chain.sync()
                dve.wait_ge(s["hsum_ready"], h + 1)
                return stats_of(H, h)

            def attention(t, u, has):
                v = 1 - u
                if not isinstance(t, int):
                    chain.base, chain.n = before + 4 * t, 0
                elif t == NT - 2:
                    chain.base, chain.n = 0, before + 4 * t
                if isinstance(t, int) and t == NT - 1:
                    roots0.append(output_added(0, roots0[0]))
                if has(1):
                    dve.wait_ge(s["q_done"], t + 2)
                    wait(dve, "x_done", 2 * t)
                    for n2 in range(2):
                        rows = slice(S * n2, S * n2 + S)
                        for c in range(2):
                            dve.tensor_tensor(LQ[v][n2][rows, c, :, :],
                                              bank[1][rows, :].rearrange("p (c r) -> p c r", c=NC),
                                              mu[rows, c, :].unsqueeze(2).broadcast_to([S, NC, P]), ALU.add
                                              ).then_inc(s["q_read"], 1)
                    dve.wait_ge(s["ksqh_ready"], t + 2)
                    dve.tensor_tensor(ksql[v][:], ksq[v][:].rearrange("p c r -> p (c r)"), ksqh[v][:].bitcast(F32),
                                      ALU.subtract).then_inc(s["ksql_ready"], 1)
                if has(-1):
                    dve.wait_ge(s["pv_done"], t)
                    wait(dve, "wo_done", t - 2)
                    dve.tensor_copy(vecT[v][:, :, 1, :], bank[7][:, 0:NC * S].rearrange("p (c i) -> p c i", c=NC)
                                    ).then_inc(s["vec1_ready"], 1)
                if has(0):
                    dve.wait_ge(s["z1_read"], t + 1)
                    wait(dve, "pT_done", t - 1)
                    dve.scalar_tensor_tensor(out=sc[u][:], in0=bank[4][:].rearrange("p (n j) -> p n j", j=S),
                                             scalar=0.5 * SCALE, in1=z1[u][:], op0=ALU.mult, op1=ALU.min
                                             ).then_inc(s["m_done"], 1)
                    dve.wait_ge(s["m_done"], t + 1)
                    chain.link(dve.tensor_reduce(rmin[u][:], sc[u][:], AX.X, ALU.min))
                    chain.link(dve.tensor_scalar(rmin[u][:], rmin[u][:], 0.0, None, ALU.max))
                    dve.scalar_tensor_tensor(out=sc[u][:], in0=sc[u][:], scalar=0.0,
                                             in1=rmin[u][:].unsqueeze(2).broadcast_to([P, 2 * NC, S]),
                                             op0=ALU.max, op1=ALU.subtract).then_inc(s["e_ready"], 1)
                if has(-1):
                    dve.wait_ge(s["wo_done"], t)
                    dve.tensor_tensor(Y[:, bass.ds(t - 1, 1), :].rearrange("p a d -> p (a d)"), bank[7][:, 2 * P:3 * P],
                                      XN[:, bass.ds(t - 1, 1), :].rearrange("p a d -> p (a d)"), ALU.add
                                      ).then_inc(s["y_ready"], 1)
                    dve.wait_ge(s["y_ready"], t)
                    dve.bn_stats(stats[:, bass.ds(t - 1, 1), :].rearrange("p a n -> p (a n)"),
                                 Y[:, bass.ds(t - 1, 1), :].rearrange("p a d -> p (a d)")).then_inc(s["y_stats"], 1)
                if has(0):
                    dve.wait_ge(s["p_exp"], t + 1)
                    chain.link(dve.tensor_reduce(rsum[u][:], sc[u][:], AX.X, ALU.add))
                    chain.link(dve.reciprocal(rsum[u][:], rsum[u][:]))
                    dve.tensor_tensor(sc[u][:], sc[u][:], rsum[u][:].unsqueeze(2).broadcast_to([P, 2 * NC, S]),
                                      ALU.mult).then_inc(s["p_ready"], 1)
                if isinstance(t, int) and t == NT - 2:
                    dve.wait_ge(s["y_stats"], NT // 2)
                    roots0.append(aggregated(0))
                if isinstance(t, int) and t == NT - 1:
                    normalised(XN, H, 0, roots0[1], "norm_ready", 1)
            steps(dve, attention)
            dve.wait_ge(s["y_stats"], NT)
            n = output_added(1, aggregated(1))

            dve.wait_ge(s["late_loaded"], N_LATE)

            def x_low(layer, h):
                cols = slice(512 * h, 512 * h + 512)
                dve.wait_ge(s["xth_ready"], 2 * layer + h + 1)
                dve.tensor_tensor(XTl[:, cols], XT[:, cols], XTh[:, cols].bitcast(F32), ALU.subtract
                                  ).then_inc(s["xtl_ready"], 1)

            x_low(0, 0)
            normalised(XN, H, 1, n, "norm_ready", 2)

            TAKEN = -3.0e38

            def router0_select():
                dve.wait_ge(s["logits_copied"], 2)
                for T in range(NT):
                    chain(dve.max(mx[:, T, :], lg[:, T, :]))
                chain.sync()
                dve.tensor_tensor(comb, lg, mx[:, :, 0:1].broadcast_to([P, NT, E0]), ALU.subtract
                                  ).then_inc(s["lmax_sub"], 1)
                for T in range(NT):
                    chain(dve.match_replace(lgr[:, T, :], mx[:, T, :], lg[:, T, :], TAKEN))
                chain.sync()
                chain.link(dve.tensor_scalar(lgr, lgr, TAKEN, None, ALU.is_equal))

            def router0_weights():
                dve.wait_ge(s["lexp"], 1)
                chain.link(dve.tensor_tensor(comb, comb, lgr, ALU.mult))
                chain.link(dve.tensor_reduce(rs8[:], comb, AX.X, ALU.add))
                chain.link(dve.reciprocal(rs8[:], rs8[:]))
                dve.tensor_tensor(comb, comb, rs8[:].unsqueeze(2).broadcast_to([P, NT, E0]), ALU.mult
                                  ).then_inc(s["comb_ready"], 1)

            def router1_select():
                dve.wait_ge(s["logits_copied"], 4)
                for T in range(NT):
                    chain(dve.max(mx[:, T, :], lg[:, T, 0:E1]))
                chain.sync()
                for T in range(NT):
                    chain(dve.max_index(mxi[:, T, :], mx[:, T, :], lg[:, T, 0:E1]))
                chain.sync()
                chain.link(dve.tensor_copy(rs8[:], mxi[:, :, 0]))
                dve.tensor_tensor(onehot[:], iota8[:].unsqueeze(1).broadcast_to([P, NT, E1]),
                                  rs8[:].unsqueeze(2).broadcast_to([P, NT, E1]), ALU.is_equal
                                  ).then_inc(s["onehot_ready"], 1)

            def router1_places():
                dve.wait_ge(s["rank_done"], 2)
                chain.link(dve.tensor_reduce(counts[:], bank[7][:, 0:NT * E1].rearrange("p (t e) -> p e t", e=E1),
                                             AX.X, ALU.add))
                chain.link(dve.tensor_tensor(cmp8[:], counts[:].unsqueeze(2).broadcast_to([P, E1, NT]),
                                             steps128[:, 0:NT].unsqueeze(1).broadcast_to([P, E1, NT]), ALU.is_gt))
                chain.link(dve.tensor_reduce(full[:], cmp8[:], AX.X, ALU.add))
                chain.link(dve.tensor_tensor(cmp8[:, :, 0:E1], before_e[:],
                                             full[:].unsqueeze(1).broadcast_to([P, E1, E1]), ALU.mult))
                chain.link(dve.tensor_reduce(base[:], cmp8[:, :, 0:E1], AX.X, ALU.add))
                chain.link(dve.tensor_tensor(rank[:], bank[6][:, 0:NT * E1].rearrange("p (t e) -> p t e", e=E1),
                                             base[:].unsqueeze(1).broadcast_to([P, NT, E1]), ALU.add))
                chain.link(dve.tensor_tensor(rank[:], rank[:], onehot[:], ALU.mult))
                chain.link(dve.tensor_reduce(place[:], rank[:], AX.X, ALU.add))
                dve.tensor_copy(place_i[:], place[:]).then_inc(s["places_ready"], 1)
                chain.link(dve.scalar_tensor_tensor(out=ends[:], in0=full[:], scalar=float(P), in1=base[:],
                                                    op0=ALU.mult, op1=ALU.add))
                chain.link(dve.tensor_tensor(cmp_e[:], steps128[:].unsqueeze(2).broadcast_to([P, MT, E1]),
                                             ends[:].unsqueeze(1).broadcast_to([P, MT, E1]), ALU.is_ge))
                chain.link(dve.tensor_reduce(tile_e[:], cmp_e[:], AX.X, ALU.add))
                chain.link(dve.tensor_scalar(tile_e[:], tile_e[:], float(E1 - 1), float(P), ALU.min, ALU.mult))
                dve.tensor_scalar(wrow_i[:], tile_e[:], row_id[:, 0:1], None, ALU.add
                                  ).then_inc(s["places_ready"], 1)

            def w13_low(w, u):
                dve.wait_ge(s["w13h_ready"], w + 1)
                dve.tensor_tensor(fewl13[u % 2][:], few[u][:, 0:2 * P], fewh13[u % 2][:].bitcast(F32), ALU.subtract
                                  ).then_inc(s["w13l_ready"], 1)

            def w2_low(w, u):
                dve.wait_ge(s["w2h_ready"], w + 1)
                dve.tensor_tensor(fewl2[u % 2][:], few[u][:, 2 * P:], fewh2[u % 2][:].bitcast(F32), ALU.subtract
                                  ).then_inc(s["w2l_ready"], 1)

            def hidden(n, m, gelu):
                dve.wait_ge(s["act_ready" if gelu else "gated_ready"], n + 1)
                dve.wait_ge(s["h_done"], n + 1)
                wait(dve, "hidh_ready", n - 1)
                wait(dve, "hidl_ready", n - 1)
                if gelu:
                    dve.tensor_copy(hid[m % 2][:], act_s[m % 2][:]).then_inc(s["hid_ready"], 1)
                else:
                    dve.tensor_tensor(hid[m % 2][:], bank[2 + m % 2][:], act_g[m % 2][:], ALU.mult
                                      ).then_inc(s["hid_ready"], 1)

            def hidden_low(n, m):
                dve.wait_ge(s["hidh_ready"], n + 1)
                dve.tensor_tensor(hidl[m % 4][:], hid[m % 2][:], hidh[m % 4][:].bitcast(F32), ALU.subtract
                                  ).then_inc(s["hidl_ready"], 1)

            def chunk(w, i, u, age):
                n = 2 * w
                if not is_last(w):
                    w13_low(w + 1, (u + 1) % SLOTS)
                if isinstance(w, int) and w == W1:
                    router1_select()
                hidden(n, 2 * u, is_gelu(w))
                if age:
                    hidden_low(n - 1, 2 * u - 1)
                hidden(n + 1, 2 * u + 1, is_gelu(w))
                hidden_low(n, 2 * u)
                w2_low(w, u)
                if isinstance(w, int) and w == 0:
                    router0_weights()
                if isinstance(w, int) and w == W1:
                    router1_places()
                if is_last(w):
                    hidden_low(n + 1, 2 * u + 1)

            w13_low(0, 0)
            x_low(0, 1)
            router0_select()
            chunks(dve, chunk, 0)

            for h in range(2):
                dve.wait_ge(s["ht_copied"], h + 1)
                dve.wait_ge(s["y_done"], 2 * W1 - 1 + h)
                dve.tensor_tensor(XT[:].rearrange("p (s b) -> p b s", b=B)[:, 8 * h:8 * h + 8, :],
                                  HT[:, 512 * h:512 * h + 512].rearrange("p (b s) -> p b s", s=S),
                                  bank[4 + h][:].rearrange("p (b s) -> p b s", s=S), ALU.add
                                  ).then_inc(s["g_ready"], 1)
            n = []
            for h in range(2):
                dve.wait_ge(s["tr_copied"], 3 + h)
                n.append(stats_of(H, h))
            normalised(X1, H, 0, n[0])
            n[0] = stats_of(X1, 0)
            normalised(X1, H, 1, n[1])
            normalised(HN, X1, 0, n[0], "norm_ready", 3)
            n[1] = stats_of(X1, 1)
            normalised(HN, X1, 1, n[1], "norm_ready", 4)
            for h in range(2):
                for j in range(2):
                    cols = slice(512 * h, 512 * h + 512)
                    dve.wait_ge(s["erq_ready"], 2 * (2 * h + j) + 2)
                    dve.scalar_tensor_tensor(out=(QT, KT)[j][:, cols], in0=eq[:, j, cols], scalar=1.0,
                                             in1=rq[:, j, cols], op0=ALU.min, op1=ALU.add).then_inc(s["qk_ready"], 1)

            def causal_scores(T):
                wait(dve, "num_done", T - 1)
                for q in range(2):
                    dve.wait_ge(s["at_done"], 2 * T + q + 1)
                    dve.tensor_tensor(am[T % 2][:, 4 * q:4 * q + 4, :],
                                      bank[2 * (T % 2) + q][:].rearrange("p (h r) -> p h r", h=4),
                                      causal[:].unsqueeze(1).broadcast_to([P, 4, P]), ALU.mult
                                      ).then_inc(s["am_ready"], 1)

            def divided(T):
                dve.wait_ge(s["num_done"], T + 1)
                o = bank[4 + T % 2][:, 0:H1 * (DH1 + 1)].rearrange("p (h d) -> p h d", h=H1)
                chain.link(dve.tensor_scalar(den[:, T, :], o[:, :, DH1], DEN_MIN, None, ALU.max))
                chain.link(dve.reciprocal(rden[:, T, :], den[:, T, :]))
                dve.tensor_tensor(AO[:, T, :].rearrange("p (h d) -> p h d", h=H1), o[:, :, 0:DH1],
                                  rden[:, T, :].unsqueeze(2).broadcast_to([P, H1, DH1]), ALU.mult
                                  ).then_inc(s["ao_ready"], 1)

            def attended(h, b):
                dve.wait_ge(s["wo1_done"], h + 1)
                chain.link(dve.tensor_tensor(half(Y, h), half(X1, h), bank[b][:].rearrange("p (t d) -> p t d", d=D),
                                             ALU.add))
                return stats_of(Y, h)

            def inner_norm(h, n):
                dve.wait_ge(s["tr_done"], 2 * 2 + h + 1)
                normalised(HN2, Y, h, n, "norm_ready", 5 + h)

            def fed(h, b):
                chain.link(dve.tensor_tensor(half(H, h), half(H, h), half(Y, h), ALU.add))
                dve.wait_ge(s["ff2_done"], h + 1)
                chain.link(dve.tensor_tensor(half(H, h), half(H, h), bank[b][:].rearrange("p (t d) -> p t d", d=D),
                                             ALU.add))
                return stats_of(H, h)

            causal_scores(0)
            for T in range(NT):
                if T + 1 < NT:
                    causal_scores(T + 1)
                divided(T)
                if T == NT - 2:
                    n[0] = attended(0, 7)
            inner_norm(0, n[0])
            n[1] = attended(1, 1)
            inner_norm(1, n[1])
            n = [fed(0, 7)]
            normalised(XN, H, 0, n[0], "norm_ready", 7)
            w13_low(W1, W1 % SLOTS)
            n.append(fed(1, 1))
            normalised(XN, H, 1, n[1], "norm_ready", 8)
            x_low(1, 0)
            x_low(1, 1)

            chunks(dve, chunk, 1)
            for h in range(2):
                dve.wait_ge(s["y_done"], 2 * WEND - 1 + h)
                dve.tensor_copy(HT[:, 512 * h:512 * h + 512], bank[4 + h][:]).then_inc(s["g_ready"], 1)
            def shared_added():
                for h in range(2):
                    dve.wait_ge(s["tr_done"], 2 * 6 + h + 1)
                    dve.tensor_tensor(half(H, h), half(H, h), bank[2 + h][:].rearrange("p (t d) -> p t d", d=D),
                                      ALU.add).then_inc(s["shared_added"], 1)

            def grouped(t, u, has):
                v = 1 - u
                if has(-2):
                    dve.wait_ge(s["hsh_ready"], t - 1)
                    dve.tensor_tensor(hidl[u][:], bank[(4, 7)[u]][:], hidh[u][:].bitcast(F32), ALU.subtract
                                      ).then_inc(s["hsl_ready"], 1)
                if has(1):
                    dve.wait_ge(s["e13h_ready"], t + 2)
                    dve.tensor_tensor(e13l[v], e13[v], e13h[v].bitcast(F32), ALU.subtract
                                      ).then_inc(s["e13l_ready"], 1)
                    dve.wait_ge(s["xgh_ready"], t + 2)
                    dve.tensor_tensor(xgl[v], bank[6][:, 0:P], xgh[v].bitcast(F32), ALU.subtract
                                      ).then_inc(s["xgl_ready"], 1)
                    dve.tensor_copy(yrow_i[:, bass.ds(t + 1, 1)], xg[v][:, D:D + 1]).then_inc(s["yrow_ready"], 1)
                if isinstance(t, int) and t == -1:
                    shared_added()
                if has(0):
                    dve.wait_ge(s["silu_ready"], t + 1)
                    dve.wait_ge(s["s3_done"], t + 1)
                    wait(dve, "hsT_done", t - 1)
                    dve.tensor_tensor(hid[u][:], bank[2 * u + 1][:], act_s[u][:], ALU.mult).then_inc(s["hs_ready"], 1)
                if has(-1):
                    dve.wait_ge(s["e2h_ready"], t)
                    dve.tensor_tensor(e2l[v], e2[v], e2h[v].bitcast(F32), ALU.subtract).then_inc(s["e2l_ready"], 1)
            routed(dve, grouped)

            for h in range(2):
                dve.wait_ge(s[f"y_loaded{h}"], 16)
                dve.wait_ge(s["shared_added"], 2)
                dve.tensor_tensor(half(H, h), half(H, h), half(Y, h), ALU.add).then_inc(s["out_ready"], 1)

        @block.tensor
        def _(pe):
            def keep_clock(b, n):
                for _ in range(n):
                    pe.matmul(bank[b][:], ident[:], wkv[:, 0:512], start=True, stop=True)

            def tok_product(src, h, b2, **flags):
                return pe.matmul(bank[h][S * b2:S * b2 + S, :], src[:, B * D:B * D + S],
                                 src[:, 1024 * b2 + 512 * h:1024 * b2 + 512 * h + 512], **flags)

            def tile_products(src):
                for h in range(2):
                    for b2 in range(2):
                        mm = tok_product(src, h, b2, start=False, stop=False)
                mm.then_inc(s["tok_used"], 1)

            pe.wait_ge(s["first_loaded"], 16 * N_FIRST)
            for h in range(2):
                for b2 in range(2):
                    pe.matmul(bank[h][S * b2:S * b2 + S, :], onesrow[:, 0:S],
                              (bias0, bias1)[b2][:, 512 * h:512 * h + 512], start=True, stop=False)
            with pe.Fori(0, GT // RING) as r:
                for j in range(RING):
                    pe.wait_ge(s["tok_masked"], RING * r + j + 1)
                    tile_products(ring[:, j, :])
            for k in range(GT // RING * RING, GT - 1):
                pe.wait_ge(s["tok_masked"], k + 1)
                tile_products(ring[:, k % RING, :])
            pe.wait_ge(s["tok_masked"], GT)
            tile_products(tail)
            for n, b2 in enumerate((1, 0)):
                pe.wait_ge(s["tok_masked"], GT + n + 1)
                for h in range(2):
                    mm = tok_product(ring[:, (GT - 1) % RING, :], h, b2, start=False, stop=True)
                    if b2 == 0:
                        mm.then_inc(s["tok_done"], 1)

            def wait_apart():
                pe.wait_ge(s["const_loaded"], N_CONSTS)

            def distances(u, m):
                for c in range(NC):
                    for b2 in range(2):
                        for n2 in range(2):
                            mm = pe.matmul(bank[4 + m][S * n2:S * n2 + S, S * (2 * c + b2):S * (2 * c + b2) + S],
                                           LQ[u][n2][:, m, c, S * b2:S * b2 + S], RK[u][n2][:, c, S * b2:S * b2 + S],
                                           start=False, stop=True, skip_group_check=True)
                mm.then_inc(s["x_done"], 1)

            def attention(t, u, has):
                v = 1 - u
                if has(0):
                    pe.wait_ge(s["ksql_ready"], t + 1)
                    wait(pe, "m_done", t)
                    wait(pe, "z1_read", t)
                    for m in range(2):
                        pe.matmul(bank[4 + m][:], headones_r, ksqh[u][:], start=True, stop=False)
                        pe.matmul(bank[4 + m][:], headones_r, ksql[u][:], start=False, stop=True)
                if has(1):
                    pe.wait_ge(s["hT_ready"], t + 2)
                    wait(pe, "q_read", 4 * t + 4)
                    for c in range(NC):
                        mm = pe.matmul(bank[1][:, P * c:P * c + P], wq[:, P * c:P * c + P], hT[v][:],
                                       start=True, stop=True)
                    mm.then_inc(s["q_done"], 1)
                    wait(pe, "k_read", 3 * t + 3)
                    for c in range(NC):
                        mm = pe.matmul(bank[2][:, P * c:P * c + P], wkv[:, P * c:P * c + P], hT[v][:],
                                       start=True, stop=True)
                    mm.then_inc(s["k_done"], 1)
                if has(0):
                    pe.wait_ge(s["qsq_ready"], 2 * t + 2)
                    distances(u, 0)
                if has(-1):
                    if isinstance(t, int) and t == NT:
                        keep_clock(2, 3)
                    pe.wait_ge(s["p_ready"], t)
                    wait(pe, "vec0_ready", t - 1)
                    for c in range(NC):
                        mm = pe.transpose(bank[6][:, P * c:P * c + P], sc[v][:, 2 * c:2 * c + 2, :].rearrange(
                            "p n j -> p (n j)"), ident[:])
                    mm.then_inc(s["pT_done"], 1)
                if has(0):
                    distances(u, 1)
                if has(-1):
                    wait_apart()
                    pe.wait_ge(s["pT_ready"], t)
                    pe.wait_ge(s["v_read"], t)
                    wait(pe, "y_ready", t - 1)
                    for c in range(NC):
                        for n2 in range(2):
                            for b2 in range(2):
                                rows = slice(S * b2, S * b2 + S)
                                mm = pe.matmul(bank[6 + b2][S * n2:S * n2 + S, S * c:S * c + S],
                                               vt[v][rows, DH * (2 * c + n2):DH * (2 * c + n2) + DH],
                                               pT[v][rows, c, S * n2:S * n2 + S], start=True, stop=True)
                    mm.then_inc(s["pv_done"], 1)
                if has(1):
                    wait(pe, "v_read", t + 1)
                    pe.matmul(bank[3][:], hT[v][:], wkv[:, NHEAD * DH:], start=True, stop=True
                              ).then_inc(s["v_done"], 1)
                if has(2):
                    pe.wait_ge(s["xs_ready"], t + 3)
                    wait(pe, "hT_ready", t + 2)
                    pe.transpose(bank[0][:, 0:P], xs[u][:], ident[:]).then_inc(s["xT_done"], 1)
                if has(-1):
                    pe.wait_ge(s["vec0_ready"], t)
                    pe.wait_ge(s["vec1_ready"], t)
                    for c in range(NC):
                        mm = pe.matmul(bank[7][:, 2 * P:3 * P], vecT[v][:, c, :, :].rearrange("p b i -> p (b i)"),
                                       wo[:, c, :], start=(c == 0), stop=(c == NC - 1))
                    mm.then_inc(s["wo_done"], 1)
            pe.wait_ge(s["const_loaded"], N_CONSTS)
            pe.wait_ge(s["ones_filled"], 4)
            pe.wait_ge(s["headones_ready"], 1)
            keep_clock(2, 4)
            steps(pe, attention)

            def transposed(src_tile, h, b, signal="tr_done"):
                for k in range(4):
                    tr = pe.transpose(bank[b][:, P * k:P * k + P], src_tile(4 * h + k), ident[:])
                tr.then_inc(s[signal], 1)

            def XT_tile(T):
                return XT[:, P * T:P * T + P]

            def logits(gate, e, h):
                for T in range(4 * h, 4 * h + 4):
                    k = e * (T % 4)
                    mm = pe.matmul(bank[6 + h][:, k:k + e], XT_tile(T), gate[:], start=True, stop=True)
                mm.then_inc(s["logits_done"], 1)

            def comb_transposed():
                pe.wait_ge(s["comb_ready"], 1)
                for T in range(NT):
                    mm = pe.matmul(bank[6 + T // 4][0:E0, P * (T % 4):P * (T % 4) + P], comb[:, T, :], ident[:],
                                   start=True, stop=True)
                    if T % 4 == 3:
                        mm.then_inc(s["combT_done"], 1)

            pe.wait_ge(s["late_loaded"], N_LATE)
            pe.wait_ge(s["norm_ready"], 1)
            transposed(lambda T: XN[:, T, :], 0, 0)
            for h in range(2):
                pe.wait_ge(s["hsum_ready"], h + 1)
                transposed(lambda T: H[:, T, :], h, 2 + h, "ht_done")
                keep_clock(4, (1, 3)[h])
            pe.wait_ge(s["norm_ready"], 2)
            transposed(lambda T: XN[:, T, :], 1, 1)
            for h in range(2):
                pe.wait_ge(s["tr_copied"], h + 1)
                logits(gate0, E0, h)

            def ranks():
                keep_clock(2, 2)
                pe.wait_ge(s["onehot_ready"], 1)
                chosen = onehot[:].rearrange("p t e -> p (t e)")
                n = NT * E1
                pe.matmul(bank[6][:, 0:n], before_p[:], chosen, start=True, stop=True)
                for k in range(1, NT):
                    mm = pe.matmul(bank[6][:, E1 * k:n], allones[:], chosen[:, 0:n - E1 * k], start=False, stop=True,
                                   skip_group_check=True)
                mm.then_inc(s["rank_done"], 1)
                pe.matmul(bank[7][:, 0:n], allones[:], chosen, start=True, stop=True).then_inc(s["rank_done"], 1)

            def three(dst, high, low, x_high, x_low, start, stop):
                pe.matmul(dst, high, x_high, start=start, stop=False)
                pe.matmul(dst, high, x_low, start=False, stop=False)
                return pe.matmul(dst, low, x_high, start=False, stop=stop)

            def units_in(w, n, m, u, h):
                cols = slice(512 * h, 512 * h + 512)
                wait(pe, "act_ready", n - 1)
                for j in range(1 if is_gelu(w) else 2):
                    if j == 1:
                        wait(pe, "hid_ready", n - 1)
                    c = slice(P * j, P * j + P)
                    mm = three(bank[2 * j + m % 2][:], fewh13[u % 2][:, c], fewl13[u % 2][:, c], XTh[:, cols],
                               XTl[:, cols], True, True)
                    if is_gelu(w) or j == 1:
                        mm.then_inc(s["h_done"], 1)
                    else:
                        mm.then_inc(s["h1_done"], 1)

            def unit_out(w, n, m, first, last):
                pe.wait_ge(s["hidl_ready"], n + 1)
                pe.wait_ge(s["w2l_ready"], w + 1)
                u = m // 2
                three(bank[4 + m % 2][:], fewh2[u % 2][:], fewl2[u % 2][:], hidh[m % 4][:], hidl[m % 4][:], first, last
                      ).then_inc(s["y_done"], 1)

            def chunk(w, i, u, age):
                n, m = 2 * w, 2 * u
                pe.wait_ge(s["w13l_ready"], w + 1)
                if age == 0:
                    pe.wait_ge(s["xtl_ready"], 2 if w == 0 else 4)
                units_in(w, n, m, u, 0)
                if age == 2:
                    unit_out(w - 2, n - 3, m - 3, isinstance(w, int) and w in (2, W1 + 2), False)
                units_in(w, n + 1, m + 1, u, 1)
                if age:
                    unit_out(w - 1, n - 2, m - 2, age == 1, False)
                if is_last(w):
                    unit_out(w - 1, n - 1, m - 1, False, False)
                    unit_out(w, n, m, False, True)
                    unit_out(w, n + 1, m + 1, False, True)

                if isinstance(w, int) and w == 1:
                    comb_transposed()
                if isinstance(w, int) and w == W1:
                    ranks()

            pe.wait_ge(s["ht_copied"], 2)
            chunks(pe, chunk, 0)

            pe.wait_ge(s["g_ready"], 2)
            for h in range(2):
                transposed(XT_tile, h, h)
            keep_clock(2, 9)

            def rows_product(h, b, bias, terms, signal):
                pe.matmul(bank[b][:], onesrow[:, 0:P], bvob2[:, bias, :].unsqueeze(1).broadcast_to([1, 4, D]),
                          start=True, stop=True)
                for T in range(4 * h, 4 * h + 4):
                    for left, right in terms(T):
                        mm = pe.matmul(bank[b][:, D * (T % 4):D * (T % 4) + D], left, right, start=False,
                                       stop=True, skip_group_check=True)
                mm.then_inc(s[signal], 1)

            for h in range(2):
                pe.wait_ge(s["norm_ready"], 3 + h)
                transposed(lambda T: HN[:, T, :], h, h)
                pe.wait_ge(s["tr_copied"], 5 + h)
                for j in range(2):
                    pe.matmul(bank[2 + 2 * j + h][:], (w1q, w1k)[j][:], XT[:, 512 * h:512 * h + 512],
                              start=True, stop=True).then_inc(s["qk1_done"], 1)
                rows_product(h, 6 + h, 0, lambda T: [(XT_tile(T), w1v[:])], "v1_done")

            def scores1(T):
                pe.wait_ge(s["qbd_ready"], T + 1)
                wait(pe, "am_ready", 2 * (T - 1))
                for q in range(2):
                    pe.matmul(bank[2 * (T % 2) + q][:], KT[:, P * T:P * T + P],
                              qbd[T % 2][:, 4 * q:4 * q + 4, :].rearrange("p h r -> p (h r)"), start=True, stop=True
                              ).then_inc(s["at_done"], 1)

            def sums1(T):
                pe.wait_ge(s["am_ready"], 2 * T + 2)
                wait(pe, "ao_ready", T - 1)
                for h in range(H1):
                    mm = pe.matmul(bank[4 + T % 2][:, (DH1 + 1) * h:(DH1 + 1) * (h + 1)], am[T % 2][:, h, :],
                                   VA[:, T, h, :], start=True, stop=True)
                mm.then_inc(s["num_done"], 1)

            def attention_transposed(h, b):
                pe.wait_ge(s["ao_ready"], 4 * h + 4)
                transposed(lambda T: AO[:, T, :], h, b)

            def back_projected(h, b):
                pe.wait_ge(s["tr_copied"], 2 * 3 + h + 1)
                rows_product(h, b, 1, lambda T: [(XT_tile(T), w1o[:])], "wo1_done")

            pe.wait_ge(s["erq_ready"], 8)
            pe.wait_ge(s["qk_ready"], 2)
            pe.wait_ge(s["va_ready"], 2)
            scores1(0)
            for T in range(NT):
                if T + 1 < NT:
                    if T + 1 == NT // 2:
                        pe.wait_ge(s["qk_ready"], 4)
                    scores1(T + 1)
                sums1(T)
                if T == NT // 2:
                    attention_transposed(0, 6)
                if T == NT // 2 + 1:
                    back_projected(0, 7)
            keep_clock(2, 2)
            attention_transposed(1, 0)
            back_projected(1, 1)

            def hidden1(h, b):
                pe.wait_ge(s["norm_ready"], 5 + h)
                transposed(lambda T: HN2[:, T, :], h, b)
                pe.wait_ge(s["tr_copied"], 2 * 4 + h + 1)
                for f in range(FF // P):
                    wait(pe, "ft_ready", (FF // P * h + f) - 3)
                    pe.matmul(bank[2 + f][:], wf1[:, P * f:P * f + P], XT[:, 512 * h:512 * h + 512],
                              start=True, stop=True).then_inc(s["ff1_done"], 1)

            def output1(h, b):
                pe.wait_ge(s["ft_ready"], FF // P * (h + 1))
                rows_product(h, b, 2, lambda T: [(FT[:, f, P * T:P * T + P], wf2[:, f, :]) for f in range(FF // P)],
                             "ff2_done")

            hidden1(0, 6)
            output1(0, 7)
            hidden1(1, 0)
            pe.wait_ge(s["norm_ready"], 7)
            transposed(lambda T: XN[:, T, :], 0, 0)
            output1(1, 1)

            keep_clock(2, 5)
            pe.wait_ge(s["norm_ready"], 8)
            transposed(lambda T: XN[:, T, :], 1, 1)
            for h in range(2):
                pe.wait_ge(s["tr_copied"], 2 * 5 + h + 1)
                logits(gate1, E1, h)
            chunks(pe, chunk, 1)
            for h in range(2):
                pe.wait_ge(s["g_ready"], 3 + h)
                transposed(lambda T: HT[:, P * T:P * T + P], h, 2 + h)

            def grouped(t, u, has):
                v = 1 - u
                if isinstance(t, int) and t == 1:
                    pe.wait_ge(s["shared_added"], 2)
                if has(0):
                    pe.wait_ge(s["xgl_ready"], t + 1)
                    pe.wait_ge(s["e13l_ready"], t + 1)
                    wait(pe, "silu_ready", t - 1)
                    for j in range(2):
                        if j == 1:
                            wait(pe, "hs_ready", t - 1)
                        c = slice(I1 * j, I1 * j + I1)
                        pe.matmul(bank[2 * u + j][:], xgh[u], e13h[u][:, c], start=True, stop=False)
                        pe.matmul(bank[2 * u + j][:], xgh[u], e13l[u][:, c], start=False, stop=False)
                        pe.matmul(bank[2 * u + j][:], xgl[u], e13h[u][:, c], start=False, stop=True
                                  ).then_inc(s[("s1_done", "s3_done")[j]], 1)
                if has(1):
                    pe.wait_ge(s[f"xg_loaded{v}"], slot_loads(t + 1, v))
                    wait(pe, "xgl_ready", t + 1)
                    pe.transpose(bank[6][:, 0:P], xg[v][:, 0:D], ident[:]).then_inc(s["xgT_done"], 1)
                if has(-1):
                    pe.wait_ge(s["hs_ready"], t)
                    wait(pe, "hsl_ready", t - 2)
                    for c in range(C1):
                        mm = pe.transpose(bank[(4, 7)[v]][:, P * c:P * c + P], hid[v][:, P * c:P * c + P], ident[:])
                    mm.then_inc(s["hsT_done"], 1)
                if has(-2):
                    pe.wait_ge(s["hsl_ready"], t - 1)
                    pe.wait_ge(s["e2l_ready"], t - 1)
                    wait(pe, "yg_ready", t - 2)
                    for c in range(C1):
                        k = slice(P * c, P * c + P)
                        pe.matmul(bank[5][:, 0:D], hidh[u][:, k], e2h[u][:, k], start=(c == 0), stop=False)
                        pe.matmul(bank[5][:, 0:D], hidh[u][:, k], e2l[u][:, k], start=False, stop=False)
                        mm = pe.matmul(bank[5][:, 0:D], hidl[u][:, k], e2h[u][:, k], start=False, stop=(c == C1 - 1))
                    mm.then_inc(s["yg_done"], 1)

            routed(pe, grouped)


def kernel(**inputs):
    import numpy as np
    import concourse.bacc as bacc
    from concourse.bass_utils import run_bass_kernel_spmd as run

    x = {n: np.asarray(v) for n, v in inputs.items()}

    w = x["L0_tok_weight"].reshape(NT, 2, G, D).transpose(2, 1, 0, 3).reshape(G, B * D)
    tok = np.concatenate([w, x["x"].T, x["L0_tok_mask"]], axis=1)
    arrays = {"tok_main": tok[:GT * P].reshape(GT, P, TOKW), "tok_tail": tok[GT * P:]}
    arrays["tok_bias_row"] = x["L0_tok_bias"].reshape(NT, 2, D).transpose(1, 0, 2).reshape(1, B * D)

    p = np.arange(P)
    arrays["ident"] = np.eye(P, dtype=np.float32)
    arrays["headones"] = (p[:, None] // S == p[None, :] // S).astype(np.float32)
    arrays["causal"] = ((p[:, None] // B == p[None, :] // B) & (p[:, None] <= p[None, :])).astype(np.float32)
    arrays["headmask"] = (p[:, None] // DH1 == np.arange(H1)[None, :]).astype(np.float32)
    arrays["iota8"] = np.tile(np.arange(E1, dtype=np.float32), (P, 1))
    arrays["before_p"] = (p[:, None] < p[None, :]).astype(np.float32)
    arrays["allones"] = np.ones((P, P), np.float32)
    e = np.arange(E1)
    arrays["before_e"] = np.tile((P * (e[None, :] < e[:, None])).astype(np.float32).reshape(1, -1), (P, 1))
    arrays["steps128"] = np.tile(P * np.arange(MT, dtype=np.float32), (P, 1))
    arrays["empty_rows"] = np.zeros((MT * P, D + 1), np.float32)
    arrays["empty_rows"][:, D] = ROWS
    arrays["lncols"] = np.stack([x[f"L1_attn_{n}"] for n in ("ln1_g", "ln1_b", "ln2_g", "ln2_b")], axis=1)
    arrays["row_id"] = (p[:, None] + P * np.arange(NT)).astype(np.float32)
    arrays["onesrow"] = np.ones((1, 512), np.float32)
    arrays["ones_row"] = np.ones(ROWS, np.float32)

    for n in ("L0_attn_Wq", "L0_attn_Wkv", "L0_attn_Wo", "L0_attn_gamma", "L0_attn_beta", "L1_attn_Wq",
              "L1_attn_Wk", "L1_attn_Wv",
              "L1_attn_Wo", "L1_attn_W1", "L1_attn_W2"):
        arrays[n] = x[n]
    for n in ("L1_attn_bq", "L1_attn_bk"):
        arrays[n] = x[n].reshape(D, 1)
    for n in ("L1_attn_bv", "L1_attn_bo", "L1_attn_b2"):
        arrays[n] = x[n].reshape(1, D)
    arrays["b1_cols"] = x["L1_attn_b1"].reshape(FF // P, P).T
    arrays["mu_cols"] = x["L0_attn_mu"].reshape(2, NC, P).transpose(2, 0, 1).reshape(P, 2 * NC)
    arrays["gate0T"] = x["L0_ffn_gate_w"].T
    arrays["gate1T"] = x["L1_ffn_gate_w"].T

    IS = x["L0_ffn_sw1"].shape[1]
    few0 = np.zeros((IS_CHUNKS + E0, P, 3, P), np.float32)
    for c in range(IS_CHUNKS):
        cols = slice(P * c, min(P * c + P, IS))
        k = cols.stop - cols.start
        few0[c, :, 0, :k] = x["L0_ffn_sw1"][:, cols]
        few0[c, :, 1, :k] = x["L0_ffn_sw3"][:, cols]
        few0[c, :k, 2, :] = x["L0_ffn_sw2"][cols]
    few0[IS_CHUNKS:, :, 0] = x["L0_ffn_w1"]
    few0[IS_CHUNKS:, :, 1] = x["L0_ffn_w3"]
    few0[IS_CHUNKS:, :, 2] = x["L0_ffn_w2"]
    arrays["few0"] = few0.reshape(-1, P, FEW)
    few1 = np.zeros((C1, P, 3, P), np.float32)
    few1[:, :, 0] = x["L1_ffn_sw1"].reshape(C1, P, D).transpose(0, 2, 1)
    few1[:, :, 2] = x["L1_ffn_sw2"].reshape(D, C1, P).transpose(1, 2, 0)
    arrays["expert13"] = np.concatenate([x["L1_ffn_w1"].transpose(0, 2, 1), x["L1_ffn_w3"].transpose(0, 2, 1)],
                                        axis=2).reshape(E1 * D, 2 * I1)
    arrays["expert2"] = x["L1_ffn_w2"].reshape(E1, D, C1, P).transpose(0, 3, 2, 1).reshape(E1 * P, C1 * D)
    arrays["few1"] = few1.reshape(-1, P, FEW)
    arrays = {n: np.ascontiguousarray(v) for n, v in arrays.items()}

    nc = bacc.Bacc("TRN2", target_bir_lowering=False, num_devices=1)
    a = {n: nc.dram_tensor(f"in_{n}", v.shape, F32, kind="ExternalInput").ap() for n, v in arrays.items()}
    out = nc.dram_tensor("out_0", (S, B, D), F32, kind="ExternalOutput").ap()
    audio_tower(nc, a, out)
    r = run(nc, [{f"in_{n}": v for n, v in arrays.items()}], core_ids=[0])
    return r.results[0]["out_0"]
```
